# Optimizing a Trainium2 kernel written in Bass

```python
import numpy as np
import jax
import jax.numpy as jnp

def _softmax(x, axis=-1):
    return jax.nn.softmax(x, axis=axis)

def _gelu(x):
    return jax.nn.gelu(x, approximate=True)

def _silu(x):
    return jax.nn.silu(x)

def _sigmoid(x):
    return jax.nn.sigmoid(x)

def _layernorm(x, axis=-1, eps=1e-05):
    m = jnp.mean(x, axis=axis, keepdims=True)
    v = jnp.var(x, axis=axis, keepdims=True)
    return (x - m) / jnp.sqrt(v + eps)

def _scatter_add(tgt, idx, src, axis=0):
    return tgt.at[idx].add(src)

def _segment_sum(src, seg, n):
    return jax.ops.segment_sum(src, seg, n)
kernel_name = 'mk_gnn_resnorm_d4_gnn_r32_c45981'

def setup_inputs(seed: int=0):
    np.random.seed(seed)
    _w = jnp.asarray

    def _rec_inputs():
        import jax
        import jax.numpy as jnp
        _gk = jax.random.key(seed)
        x = -0.0003713 + 1 * jax.random.normal(jax.random.fold_in(_gk, 1), (3125, 256), jnp.float32)
        src = jax.random.randint(jax.random.fold_in(_gk, 2), (50000,), 0, 3125, jnp.int32)
        dst = jax.random.randint(jax.random.fold_in(_gk, 3), (50000,), 0, 3125, jnp.int32)
        _o = jnp.argsort(dst, stable=True)
        src = src[_o]
        dst = dst[_o]
        edge_weight = jax.random.uniform(jax.random.fold_in(_gk, 13), (50000,), jnp.float32, 0.0, 0.999996)
        return (x, src, dst, edge_weight)
    x, src, dst, edge_weight = _rec_inputs()

    def _L0_gnn_setup():
        import jax, jax.numpy as jnp
        import numpy as np
        N, E, L, C, D = (50000, 12500, 3, 4, 64)
        IN_DIM = C * D
        key = jax.random.key(seed)
        ks = jax.random.split(key, 10)
        return {'features': jax.random.normal(ks[0], (N, IN_DIM), dtype=jnp.float32), 'src': jax.random.randint(ks[1], (E,), 0, N, dtype=jnp.int32), 'dst': jax.random.randint(ks[2], (E,), 0, N, dtype=jnp.int32), 'edge_w': jax.random.uniform(ks[3], (E,), dtype=jnp.float32), 'fc_w': jax.random.normal(ks[4], (L, IN_DIM, IN_DIM), dtype=jnp.float32) * 0.05, 'fc_b': jax.random.normal(ks[5], (L, IN_DIM), dtype=jnp.float32) * 0.05, 'ch_w': jax.random.normal(ks[6], (L, C, D, D), dtype=jnp.float32) * 0.1, 'ch_b': jax.random.normal(ks[7], (L, C, D), dtype=jnp.float32) * 0.1, 'mlp_w': jax.random.normal(ks[8], (IN_DIM, L * IN_DIM), dtype=jnp.float32) * 0.05, 'mlp_b': jax.random.normal(ks[9], (IN_DIM,), dtype=jnp.float32) * 0.05}
    _L0_gnn_all = _L0_gnn_setup()
    _L0_gnn_in = {k: v for k, v in _L0_gnn_all.items() if k in ('fc_w', 'fc_b', 'ch_w', 'ch_b', 'mlp_w', 'mlp_b')}
    del _L0_gnn_all

    def _L1_gnn_setup():
        import jax, jax.numpy as jnp
        import numpy as np
        N_NODES = 10000
        N_EDGES = 10000
        D = 256
        key = jax.random.key(seed)
        k1, k2, k3, k4, k5 = jax.random.split(key, 5)
        x = jax.random.normal(k1, (N_NODES, D), dtype=jnp.float32)
        src = jax.random.randint(k2, (N_EDGES,), 0, N_NODES, dtype=jnp.int32)
        dst = jax.random.randint(k3, (N_EDGES,), 0, N_NODES, dtype=jnp.int32)
        s = 1.0 / np.sqrt(D)
        theta_w = jax.random.uniform(k4, (D, D), jnp.float32, -s, s)
        theta_b = jnp.zeros((D,), jnp.float32)
        phi_w = jax.random.uniform(k5, (D, D), jnp.float32, -s, s)
        phi_b = jnp.zeros((D,), jnp.float32)
        return {'x': x, 'src': src, 'dst': dst, 'theta_w': theta_w, 'theta_b': theta_b, 'phi_w': phi_w, 'phi_b': phi_b}
    _L1_gnn_all = _L1_gnn_setup()
    _L1_gnn_in = {k: v for k, v in _L1_gnn_all.items() if k in ('theta_w', 'theta_b', 'phi_w', 'phi_b')}
    del _L1_gnn_all

    def _L2_gnn_setup():
        import jax, jax.numpy as jnp
        import numpy as np
        from jax.ops import segment_max, segment_sum
        N_NODES = 50000
        N_EDGES = 25000
        IN_CH = 256
        HEADS = 8
        OUT_CH = 32
        NEG_SLOPE = 0.2
        EPS = 1e-16
        key = jax.random.key(seed)
        k1, k2, k3, k4, k5 = jax.random.split(key, 5)
        x = jax.random.normal(k1, (N_NODES, IN_CH), dtype=jnp.float32)
        edge_index = jax.random.randint(k2, (2, N_EDGES), 0, N_NODES, dtype=jnp.int64)
        W = jax.random.normal(k3, (HEADS * OUT_CH, IN_CH), dtype=jnp.float32) * (1.0 / np.sqrt(IN_CH))
        a_left = jax.random.normal(k4, (HEADS, OUT_CH), dtype=jnp.float32) * (1.0 / np.sqrt(OUT_CH))
        a_right = jax.random.normal(k5, (HEADS, OUT_CH), dtype=jnp.float32) * (1.0 / np.sqrt(OUT_CH))
        return {'x': x, 'edge_index': edge_index, 'W': W, 'a_left': a_left, 'a_right': a_right}
    _L2_gnn_all = _L2_gnn_setup()
    _L2_gnn_in = {k: v for k, v in _L2_gnn_all.items() if k in ('W', 'a_left', 'a_right')}
    del _L2_gnn_all

    def _L3_gnn_setup():
        import jax, jax.numpy as jnp
        import numpy as np
        N_NODES = 625
        N_EDGES = 10000
        D = 256
        N_LAYERS = 3
        BN_EPS = 1e-05
        key = jax.random.key(seed)
        ks = jax.random.split(key, 5)
        x = jax.random.normal(ks[0], (N_NODES, D), dtype=jnp.float32)
        src = jax.random.randint(ks[1], (N_EDGES,), 0, N_NODES)
        dst = jax.random.randint(ks[2], (N_EDGES,), 0, N_NODES)
        scale = 1.0 / np.sqrt(D)
        thetas = jax.random.normal(ks[3], (N_LAYERS, D, D), dtype=jnp.float32) * scale
        phis = jax.random.normal(ks[4], (N_LAYERS, D, D), dtype=jnp.float32) * scale
        gammas = jnp.ones((N_LAYERS, D), dtype=jnp.float32)
        betas = jnp.zeros((N_LAYERS, D), dtype=jnp.float32)
        return {'x': x, 'src': src, 'dst': dst, 'thetas': thetas, 'phis': phis, 'gammas': gammas, 'betas': betas}
    _L3_gnn_all = _L3_gnn_setup()
    _L3_gnn_in = {k: v for k, v in _L3_gnn_all.items() if k in ('thetas', 'phis', 'gammas', 'betas')}
    del _L3_gnn_all
    return {'x': x, 'src': src, 'dst': dst, 'edge_weight': edge_weight, 'L0_gnn_fc_w': _L0_gnn_in['fc_w'], 'L0_gnn_fc_b': _L0_gnn_in['fc_b'], 'L0_gnn_ch_w': _L0_gnn_in['ch_w'], 'L0_gnn_ch_b': _L0_gnn_in['ch_b'], 'L0_gnn_mlp_w': _L0_gnn_in['mlp_w'], 'L0_gnn_mlp_b': _L0_gnn_in['mlp_b'], 'L1_gnn_theta_w': _L1_gnn_in['theta_w'], 'L1_gnn_theta_b': _L1_gnn_in['theta_b'], 'L1_gnn_phi_w': _L1_gnn_in['phi_w'], 'L1_gnn_phi_b': _L1_gnn_in['phi_b'], 'L2_gnn_W': _L2_gnn_in['W'], 'L2_gnn_a_left': _L2_gnn_in['a_left'], 'L2_gnn_a_right': _L2_gnn_in['a_right'], 'L3_gnn_thetas': _L3_gnn_in['thetas'], 'L3_gnn_phis': _L3_gnn_in['phis'], 'L3_gnn_gammas': _L3_gnn_in['gammas'], 'L3_gnn_betas': _L3_gnn_in['betas']}

def reference(x, src, dst, edge_weight, L0_gnn_fc_w, L0_gnn_fc_b, L0_gnn_ch_w, L0_gnn_ch_b, L0_gnn_mlp_w, L0_gnn_mlp_b, L1_gnn_theta_w, L1_gnn_theta_b, L1_gnn_phi_w, L1_gnn_phi_b, L2_gnn_W, L2_gnn_a_left, L2_gnn_a_right, L3_gnn_thetas, L3_gnn_phis, L3_gnn_gammas, L3_gnn_betas):
    import jax
    import jax.numpy as jnp

    def _L0_gnn_ref(features, src, dst, edge_w, fc_w, fc_b, ch_w, ch_b, mlp_w, mlp_b):
        import jax, jax.numpy as jnp
        import numpy as np
        N, E, L, C, D = (50000, 12500, 3, 4, 64)
        IN_DIM = C * D
        n = features.shape[0]
        ones = jnp.ones_like(edge_w)
        deg_out = jnp.maximum(jax.ops.segment_sum(ones, src, num_segments=n), 1.0)
        deg_in = jnp.maximum(jax.ops.segment_sum(ones, dst, num_segments=n), 1.0)
        norm_out = (deg_out ** (-0.5))[:, None, None]
        norm_in = (deg_in ** (-0.5))[:, None, None]
        x = features
        outs = []
        for l in range(L):
            h = x @ fc_w[l].T + fc_b[l]
            f = h.reshape(n, C, D) * norm_out
            f = jnp.einsum('ncd,cde->nce', f, ch_w[l])
            m = f[src] * edge_w[:, None, None]
            agg = jax.ops.segment_sum(m, dst, num_segments=n)
            r = agg * norm_in + ch_b[l]
            r = jax.nn.relu(r)
            x = r.reshape(n, C * D)
            outs.append(x)
        hcat = jnp.concatenate(outs, axis=-1)
        return hcat @ mlp_w.T + mlp_b

    def _L1_gnn_ref(x, src, dst, theta_w, theta_b, phi_w, phi_b):
        import jax, jax.numpy as jnp
        import numpy as np
        N_NODES = 10000
        N_EDGES = 10000
        D = 256
        x_src = x[src]
        x_dst = x[dst]
        theta_x = (x_dst - x_src) @ theta_w.T + theta_b
        phi_x = x_src @ phi_w.T + phi_b
        e = jax.nn.relu(theta_x + phi_x)
        out = jax.ops.segment_max(e, dst, num_segments=x.shape[0])
        return jnp.where(jnp.isfinite(out), out, 0.0)

    def _L2_gnn_ref(x, edge_index, W, a_left, a_right):
        import jax, jax.numpy as jnp
        import numpy as np
        from jax.ops import segment_max, segment_sum
        N_NODES = 50000
        N_EDGES = 25000
        IN_CH = 256
        HEADS = 8
        OUT_CH = 32
        NEG_SLOPE = 0.2
        EPS = 1e-16
        N = x.shape[0]
        H, C = (HEADS, OUT_CH)
        loops = jnp.arange(N, dtype=edge_index.dtype)
        src = jnp.concatenate([edge_index[0], loops])
        dst = jnp.concatenate([edge_index[1], loops])
        Wh = (x @ W.T).reshape(N, H, C)
        e_left = jnp.einsum('nhc,hc->nh', Wh, a_left)
        e_right = jnp.einsum('nhc,hc->nh', Wh, a_right)
        e = e_left[src] + e_right[dst]
        e = jnp.where(e >= 0, e, NEG_SLOPE * e)
        e_max = segment_max(e, dst, num_segments=N)
        e_max = jnp.where(jnp.isfinite(e_max), e_max, 0.0)
        e_exp = jnp.exp(e - e_max[dst])
        denom = segment_sum(e_exp, dst, num_segments=N)
        alpha = e_exp / (denom[dst] + EPS)
        out = segment_sum(Wh[src] * alpha[:, :, None], dst, num_segments=N)
        return out.reshape(N, H * C)

    def _L3_gnn_ref(x, src, dst, thetas, phis, gammas, betas):
        import jax, jax.numpy as jnp
        import numpy as np
        N_NODES = 625
        N_EDGES = 10000
        D = 256
        N_LAYERS = 3
        BN_EPS = 1e-05
        N = x.shape[0]
        for l in range(thetas.shape[0]):
            xi = x[src]
            xj = x[dst]
            e = jax.nn.relu((xj - xi) @ thetas[l].T + xi @ phis[l].T)
            agg = jax.ops.segment_max(e, src, num_segments=N)
            agg = jnp.where(agg < -1e+30, 0.0, agg)
            mu = agg.mean(axis=0)
            var = agg.var(axis=0)
            x = jax.nn.relu((agg - mu) * jax.lax.rsqrt(var + BN_EPS) * gammas[l] + betas[l])
        return x
    edge_index = jnp.stack([src, dst])
    x = _layernorm(x + _L0_gnn_ref(x, src, dst, edge_weight, L0_gnn_fc_w, L0_gnn_fc_b, L0_gnn_ch_w, L0_gnn_ch_b, L0_gnn_mlp_w, L0_gnn_mlp_b), axis=-1)
    x = _layernorm(x + _L1_gnn_ref(x, src, dst, L1_gnn_theta_w, L1_gnn_theta_b, L1_gnn_phi_w, L1_gnn_phi_b), axis=-1)
    x = _layernorm(x + _L2_gnn_ref(x, edge_index, L2_gnn_W, L2_gnn_a_left, L2_gnn_a_right), axis=-1)
    x = _layernorm(x + _L3_gnn_ref(x, src, dst, L3_gnn_thetas, L3_gnn_phis, L3_gnn_gammas, L3_gnn_betas), axis=-1)
    return x

_drawn_inputs = setup_inputs


def setup_inputs(seed=0):
    import zlib

    import numpy as np

    out = dict(_drawn_inputs(seed))
    spreads = {'L1_gnn_theta_b': (0.0, 0.1),
     'L1_gnn_phi_b': (0.0, 0.1),
     'L3_gnn_gammas': (1.0, 0.2),
     'L3_gnn_betas': (0.0, 0.1)}
    factors = {}
    for name, (base, spread) in spreads.items():
        noise = np.random.default_rng([zlib.crc32(name.encode()), seed]).standard_normal(out[name].shape)
        drawn = base * np.exp(spread * noise) if base else spread * noise
        out[name] = jnp.asarray(drawn.astype(out[name].dtype))
    for name, factor in factors.items():
        out[name] = (out[name] * factor).astype(out[name].dtype)
    return out
```

```python
import concourse.bass as bass
from concourse import mybir
from contextlib import ExitStack, contextmanager

F32 = mybir.dt.float32
BF16 = mybir.dt.bfloat16
F16 = mybir.dt.float16
I32 = mybir.dt.int32
ALU = mybir.AluOpType
ACT = mybir.ActivationFunctionType
AX = mybir.AxisListType
ds = bass.ds

P = 128
N = 3125
E = 50000
D = 256
NT = (N + P - 1) // P
NP = NT * P
LAST = N - (NT - 1) * P
GT = 4
NG = -(-E // (P * GT))
ET = NG * GT
EP = ET * P
ROW_ZERO = EP
ROW_LOW = EP + 1
LOW = -1e38
HEADS = 8
TW = D + HEADS
RW = D + 2 * HEADS
LO = 32
HI = -(-(N + 1) // LO)
LAYERS = 3
NODE_UNROLL = 5
EPS = 1e-5
OOB = 60000.0


class Count:

    def __init__(self, eng, sem):
        self.eng, self.sem, self.n, self.turn, self.per, self.at = eng, sem, 0, 0, 0, 0

    def inc(self, ins):
        self.n += 1
        ins.then_inc(self.sem, 1)
        return ins

    def value(self):
        return self.turn * self.per + self.n if self.per else self.n

    def wait(self):
        self.eng.wait_ge(self.sem, self.value())

    def link(self, ins):
        self.inc(ins)
        self.wait()

    @contextmanager
    def loop(self, turns, per):
        start = self.n
        with self.eng.Fori(0, turns) as i:
            self.turn, self.per = i, per
            yield i
            assert self.n - start == per, (self.n, start, per)
        self.turn, self.per, self.n = 0, 0, start + turns * per


def pipelined(total, unroll, eng, *steps):
    most = max(lead for _, lead in steps)
    turns = (total - most) // unroll

    def straight(s):
        for fn, lead in steps:
            if 0 <= s + lead < total:
                fn(s + lead, (s + lead) % unroll, (s + lead) // unroll)

    for s in range(-most, 0):
        straight(s)
    with eng.Fori(0, turns) as i:
        for j in range(unroll):
            for fn, lead in steps:
                fn(i * unroll + (j + lead), (j + lead) % unroll, i + (j + lead) // unroll)
    for s in range(turns * unroll, total):
        straight(s)


class Gathered:

    def __init__(self, sem):
        self.sem, self.before = sem, 0

    def arrived(self, eng, dmas):
        eng.wait_ge(self.sem, dmas * 16 + self.before)

    def close(self, dmas):
        self.before += 16 * dmas


class Stage:

    used = []
    def __init__(self, nc, name):
        self.nc, self.name, self.stack, self.sems = nc, name, ExitStack(), []

    def sem(self, name):
        self.sems.append(self.stack.enter_context(self.nc.semaphore(f"{self.name}_{name}")))
        return self.sems[-1]

    def __enter__(self):
        return self

    def block(self):
        block = self.stack.enter_context(self.nc.Block())
        before, Stage.used = Stage.used, sorted(s.num for s in self.sems)
        assert not set(before) & set(Stage.used)

        @block.gpsimd
        def _(eng):
            while before:
                n = 1
                while n < len(before) and before[n] == before[0] + n:
                    n += 1
                eng.sem_clear(range(before[0], before[0] + n))
                del before[:n]

        return block

    def __exit__(self, *a):
        return self.stack.__exit__(*a)


def build(nc, a, out):
    top = ExitStack()
    Stage.used = []
    with top:
        gathered = [Gathered(top.enter_context(nc.semaphore(f"gathered_{k}"))) for k in range(5)]
        def sb(name, shape, dt=F32):
            return top.enter_context(nc.sbuf_tensor(name, shape, dt))

        def dram(name, shape, dt=F32):
            return nc.dram_tensor(name, shape, dt).ap()

        def carve(base, *wanted):
            at, made = 0, []
            for shape, dt in wanted:
                n = 1
                for k in shape:
                    n *= k
                words = n if dt in (F32, I32) else -(-n // 2)
                v = base[:, at:at + words]
                if dt != F32:
                    v = v.bitcast(dt)
                names = "abcd"[:len(shape)]
                if len(shape) > 1:
                    v = v.rearrange(f"p ({' '.join(names)}) -> p {' '.join(names)}", **dict(zip(names, shape)))
                made.append(v)
                at += words
            assert at <= base.shape[1], (at, base.shape)
            return made

        X = sb("X", [P, NT, D])
        ARENA = sb("ARENA", [P, NT * 2 * RW])
        AGW = ARENA[:, 0:NT * RW].rearrange("p (t d) -> p t d", d=RW)
        AGG = AGW[:, :, 0:D]
        C = ARENA[:, NT * RW:NT * 2 * RW].rearrange("p (t d) -> p t d", d=RW)
        HIST = ARENA[:, 0:ET * LO].rearrange("p (t l) -> p t l", l=LO)
        YBASE = sb("YBASE", [P, NT * RW])
        YW = YBASE[:, :].rearrange("p (t d) -> p t d", d=RW)
        Y = YW[:, :, 0:D]
        WORK = sb("WORK", [P, 4 * GT * TW + 4 * GT * P + 2 * GT * RW])
        G, S, O = carve(WORK, ((4 * GT, TW), F32), ((2, 2, GT * P), F32), ((2, GT, RW), F32))
        R, XT, TMP, TMP2 = carve(WORK, *[((NODE_UNROLL, D), F32)] * 4)
        HB = 14
        RB = GT
        oh_hi, oh_lo, oh_t, oh_tf, rank_tmp, sel, ohp, val = carve(
            YBASE, ((2, HB, HI), BF16), ((2, HB, LO), BF16), ((2, 2, RB * P), BF16), ((2, RB * P), F32),
            ((2, RB, P), BF16), ((2, RB, LO), F32), ((4, P), BF16), ((4, 2, ET), BF16))
        key_tmp, key_hi, key_lo, pos, place_hi, place_lo, pay_hi, pay_lo, no_places = carve(
            WORK, ((3, ET), I32), *[((ET,), F32)] * 7, ((P + ET,), BF16))
        idxbuf = sb("idxbuf", [P, 4, GT], I32)
        wbuf = sb("wbuf", [P, 4, GT])
        maskbuf = sb("maskbuf", [P, 4, GT * P], BF16)
        ident = sb("ident", [P, P])
        identb = sb("identb", [P, P], BF16)
        ones = sb("ones", [P, P])
        before = sb("before", [P, P])
        upto = sb("upto", [P, P])
        iota_i = sb("iota_i", [P, ET], I32)
        iota_b = sb("iota_b", [P, P], BF16)
        iota_h = sb("iota_h", [P, ET], F16)
        GW = sb("GW", [P, LAYERS, 2, D])
        GB = sb("GB", [P, LAYERS, D])
        MW = sb("MW", [P, LAYERS, 2, D])
        TH1, DF1, W2 = sb("TH1", [P, 2, D]), sb("DF1", [P, 2, D]), sb("W2", [P, 2, D])
        WA = sb("WA", [P, 2, 2 * HEADS])
        TH3, DF3 = sb("TH3", [P, LAYERS, 2, D]), sb("DF3", [P, LAYERS, 2, D])
        CHB, MB = sb("CHB", [P, LAYERS, D]), sb("MB", [P, D])
        B1 = sb("B1", [P, 2, D])
        GAM, BET = sb("GAM", [P, LAYERS, D]), sb("BET", [P, LAYERS, D])
        AV = sb("AV", [P, 2, D])
        SRCF, DSTF, WE = sb("SRCF", [P, ET]), sb("DSTF", [P, ET]), sb("WE", [P, ET])
        SRCI, BYSRC = sb("SRCI", [P, ET], I32), sb("BYSRC", [P, ET], I32)
        norm_out, norm_in = sb("norm_out", [P, NT]), sb("norm_in", [P, NT])
        end_sum, end_max, end_src = (sb(n, [P, NT], I32) for n in ("end_sum", "end_max", "end_src"))
        first_dst, first_src = sb("first_dst", [P, NT], I32), sb("first_src", [P, NT], I32)
        carry_row = sb("carry_row", [P, NT], I32)
        MV = sb("MV", [P, NT, 2])

        T = dram("table", [NP, D])
        T2 = dram("table_attention", [NP, TW])
        PR = dram("edge_results", [EP + 2, D])
        PA = dram("edge_results_attention", [EP + 1, RW])
        CR = dram("carry_rows", [ET + 1, RW])
        ERT = dram("er_table", [NP, HEADS])
        ERE = dram("er_edges", [EP, HEADS])
        nst_dst = dram("nst_dst", [1, EP + P], BF16)
        low_dst = dram("low_dst", [1, EP + P], BF16)
        low_src = dram("low_src", [1, EP + P], BF16)
        dst_row = dram("dst_row", [1, EP])
        flag_dst, flag_src = dram("flag_dst", [EP, 1]), dram("flag_src", [EP, 1])
        hist_start, hist_count = dram("hist_start", [2, NP]), dram("hist_count", [2, NP])

        def constants():
            with Stage(nc, "cst") as st:
                zeroed, filled, done = st.sem("zeroed"), st.sem("filled"), st.sem("done")
                copied = st.sem("copied")
                block = st.block()

                @block.gpsimd
                def _(eng):
                    eng.memset(ident[:, :], 0.0).then_inc(zeroed, 1)
                    eng.memset(ones[:, :], 1.0).then_inc(zeroed, 1)
                    eng.iota(iota_i[:, :], pattern=[[1, ET]], base=0, channel_multiplier=0).then_inc(zeroed, 1)
                    eng.wait_ge(zeroed, 3)
                    eng.affine_select(out=ident[:, :], in_=ident[:, :], compare_op=ALU.not_equal, fill=1.0,
                                      base=0, pattern=[[-1, P]], channel_multiplier=1).then_inc(filled, 1)
                    eng.affine_select(out=before[:, :], in_=ones[:, :], compare_op=ALU.is_gt, fill=0.0,
                                      base=0, pattern=[[1, P]], channel_multiplier=-1).then_inc(filled, 1)
                    eng.affine_select(out=upto[:, :], in_=ones[:, :], compare_op=ALU.is_ge, fill=0.0,
                                      base=0, pattern=[[1, P]], channel_multiplier=-1).then_inc(filled, 1)

                @block.vector
                def _(eng):
                    eng.wait_ge(filled, 3)
                    eng.tensor_copy(identb[:, :], ident[:, :]).then_inc(copied, 1)
                    eng.tensor_copy(iota_b[:, :], iota_i[:, 0:P]).then_inc(copied, 1)
                    eng.tensor_copy(iota_h[:, :], iota_i[:, :]).then_inc(copied, 1)

        def weights():
            at = [0]

            def area(*shape):
                n = 1
                for s in shape:
                    n *= s
                v = ARENA[:, at[0]:at[0] + n]
                at[0] += n
                names = "abc"[:len(shape)]
                if len(shape) == 1:
                    return v
                return v.rearrange(f"p ({' '.join(names)}) -> p {' '.join(names)}",
                                   **{k: s for k, s in zip(names[1:], shape[1:])})

            fc, ch = area(LAYERS * 2, D), area(LAYERS * 2, D)
            mlp = area(2, LAYERS * D)
            th1, ph1, w2 = area(2, D), area(2, D), area(2, D)
            th3, ph3 = area(LAYERS * 2, D), area(LAYERS * 2, D)
            fcb = area(LAYERS * 2)
            fcb_wide = area(LAYERS * 2, P)
            prod = area(2, 2, D)
            turns = [(lambda m, k, l=l: mlp[:, m, l * D + k * P:l * D + k * P + P], MW[:, l]) for l in range(LAYERS)]
            turns += [(lambda m, k: th1[:, m, k * P:k * P + P], TH1[:, :, :]),
                      (lambda m, k: ph1[:, m, k * P:k * P + P], DF1[:, :, :]),
                      (lambda m, k: w2[:, m, k * P:k * P + P], W2[:, :, :])]
            turns += [(lambda m, k, l=l: th3[:, 2 * l + m, k * P:k * P + P], TH3[:, l]) for l in range(LAYERS)]
            turns += [(lambda m, k, l=l: ph3[:, 2 * l + m, k * P:k * P + P], DF3[:, l]) for l in range(LAYERS)]
            banks = len(turns) + 2 * LAYERS
            with Stage(nc, "w") as st:
                loaded, zeroed, ready = st.sem("loaded"), st.sem("zeroed"), st.sem("ready")
                made, moved, chain = st.sem("made"), st.sem("moved"), st.sem("chain")
                ps = st.stack.enter_context(nc.psum_tensor("w_ps", [P, 4, 512], F32))
                block = st.block()

                @block.sync
                def _(eng):
                    n = 0

                    def load(dst, src):
                        nonlocal n
                        eng.dma_start(dst, src).then_inc(loaded, 16)
                        n += 16

                    load(X[:, 0:NT - 1, :], a["x"][0:(NT - 1) * P, :].rearrange("(t p) d -> p t d", p=P))
                    eng.wait_ge(zeroed, 2)
                    load(X[0:LAST, NT - 1, :], a["x"][(NT - 1) * P:N, :])
                    load(fc, a["L0_gnn_fc_w"].rearrange("l (k p) i -> p (l k) i", p=P))
                    for c in range(4):
                        for l in range(LAYERS):
                            load(ch[64 * (c % 2):64 * (c % 2) + 64, 2 * l + c // 2, 64 * c:64 * c + 64],
                                 a["L0_gnn_ch_w"][l, c])
                    load(mlp, a["L0_gnn_mlp_w"].rearrange("(m p) i -> p m i", p=P))
                    with nc.allow_non_contiguous_dma("a bias across the partitions"):
                        load(fcb, a["L0_gnn_fc_b"].rearrange("l (k p) -> p (l k)", p=P))
                    for dst, name in ((th1, "L1_gnn_theta_w"), (ph1, "L1_gnn_phi_w"), (w2, "L2_gnn_W")):
                        load(dst, a[name].rearrange("(m p) i -> p m i", p=P))
                    for dst, name in ((th3, "L3_gnn_thetas"), (ph3, "L3_gnn_phis")):
                        load(dst, a[name].rearrange("l (m p) i -> p (l m) i", p=P))

                    def spread(dst, src, width):
                        load(dst, src.broadcast_to([P, width]))

                    spread(CHB[:, :, :].rearrange("p l d -> p (l d)"),
                           a["L0_gnn_ch_b"].rearrange("(o l) c d -> o (l c d)", o=1), LAYERS * D)
                    spread(MB[:, :], a["L0_gnn_mlp_b"].rearrange("(o d) -> o d", o=1), D)
                    spread(B1[:, 0, :], a["L1_gnn_theta_b"].rearrange("(o d) -> o d", o=1), D)
                    spread(B1[:, 1, :], a["L1_gnn_phi_b"].rearrange("(o d) -> o d", o=1), D)
                    spread(AV[:, 0, :], a["L2_gnn_a_left"].rearrange("(o h) c -> o (h c)", o=1), D)
                    spread(AV[:, 1, :], a["L2_gnn_a_right"].rearrange("(o h) c -> o (h c)", o=1), D)
                    spread(GAM[:, :, :].rearrange("p l d -> p (l d)"),
                           a["L3_gnn_gammas"].rearrange("(o l) d -> o (l d)", o=1), LAYERS * D)
                    spread(BET[:, :, :].rearrange("p l d -> p (l d)"),
                           a["L3_gnn_betas"].rearrange("(o l) d -> o (l d)", o=1), LAYERS * D)
                    eng.wait_ge(loaded, n)
                    eng.sem_inc(ready, 1)

                @block.gpsimd
                def _(eng):
                    eng.memset(X[:, NT - 1, :], 0.0).then_inc(zeroed, 1)
                    eng.memset(ch, 0.0).then_inc(zeroed, 1)

                @block.vector
                def _(eng):
                    c = Count(eng, chain)
                    eng.wait_ge(ready, 1)
                    c.inc(eng.tensor_tensor(ph1, ph1, th1, ALU.subtract))
                    c.inc(eng.tensor_tensor(ph3, ph3, th3, ALU.subtract))
                    c.inc(eng.tensor_tensor(B1[:, 0, :], B1[:, 0, :], B1[:, 1, :], ALU.add))
                    for q in range(2 * LAYERS):
                        c.inc(eng.tensor_scalar(fcb_wide[:, q, :], ones[:, :], fcb[:, q:q + 1], None, ALU.mult))
                    assert c.n == 3 + 2 * LAYERS
                    eng.wait_ge(moved, banks)
                    for s in range(2):
                        c.link(eng.tensor_tensor(prod[:, s], W2[:, :, :],
                                                 AV[:, s:s + 1, :].broadcast_to([P, 2, D]), ALU.mult))
                        c.inc(eng.tensor_reduce(WA[:, :, HEADS * s:HEADS * s + HEADS],
                                                prod[:, s].rearrange("p k (h c) -> p k h c", h=HEADS),
                                                AX.X, ALU.add))

                @block.tensor
                def _(eng):
                    eng.wait_ge(ready, 1)
                    eng.wait_ge(chain, 3 + 2 * LAYERS)
                    b = 0
                    for nat, _ in turns:
                        if b >= 4:
                            eng.wait_ge(moved, b - 3)
                        for k in range(2):
                            for m in range(2):
                                last = eng.transpose(ps[:, b % 4, k * D + m * P:k * D + m * P + P], nat(m, k), ident[:, :])
                        last.then_inc(made, 1)
                        b += 1
                    for l in range(LAYERS):
                        eng.wait_ge(moved, b - 3)
                        for m in range(2):
                            for k in range(2):
                                last = eng.matmul(ps[:, b % 4, m * D:m * D + D], fc[:, 2 * l + k, m * P:m * P + P],
                                                  ch[:, 2 * l + k, :], start=k == 0, stop=k == 1)
                        last.then_inc(made, 1)
                        b += 1
                        eng.wait_ge(moved, b - 3)
                        for k in range(2):
                            last = eng.matmul(ps[:, b % 4, 0:D], fcb_wide[:, 2 * l + k, :], ch[:, 2 * l + k, :],
                                              start=k == 0, stop=k == 1)
                        last.then_inc(made, 1)
                        b += 1

                @block.scalar
                def _(eng):
                    b = 0
                    for _, dst in turns:
                        eng.wait_ge(made, b + 1)
                        eng.activation(dst, ps[:, b % 4, :].rearrange("p (k d) -> p k d", k=2), ACT.Copy).then_inc(moved, 1)
                        b += 1
                    for l in range(LAYERS):
                        eng.wait_ge(made, b + 1)
                        eng.activation(GW[:, l], ps[:, b % 4, :].rearrange("p (k d) -> p k d", k=2), ACT.Copy).then_inc(moved, 1)
                        b += 1
                        eng.wait_ge(made, b + 1)
                        eng.activation(GB[:, l, :], ps[:, b % 4, 0:D], ACT.Copy).then_inc(moved, 1)
                        b += 1

        def edge_columns():
            CH = ET // 4
            whole = E // P - 3 * CH
            part = E % P
            rows_i = ARENA[0:CH, 0:8 * P].bitcast(I32).rearrange("p (s c e) -> p s c e", s=2, c=4)
            rows_f = ARENA[0:CH, 8 * P:20 * P].rearrange("p (s c e) -> p s c e", s=3, c=4)
            zero = ARENA[:, 20 * P:20 * P + 4 * ET]
            sent = ARENA[0:1, 20 * P + 4 * ET:20 * P + 4 * ET + RW]
            low_sent = ARENA[0:1, 20 * P + 4 * ET + RW:20 * P + 4 * ET + RW + D]
            with Stage(nc, "col") as st:
                padded, loaded, cast = st.sem("padded"), st.sem("loaded"), st.sem("cast")
                turned, moved, stored = st.sem("turned"), st.sem("moved"), st.sem("stored")
                zeroed = st.sem("zeroed")
                ps = st.stack.enter_context(nc.psum_tensor("col_ps", [P, 3, 512], F32))
                block = st.block()

                @block.gpsimd
                def _(eng):
                    eng.memset(rows_i, N).then_inc(padded, 1)
                    eng.memset(rows_f[:, 2], 0.0).then_inc(padded, 1)
                    eng.memset(zero, 0.0).then_inc(zeroed, 1)
                    eng.memset(sent, 0.0).then_inc(zeroed, 1)

                @block.sync
                def _(eng):
                    eng.wait_ge(padded, 2)
                    n = 0
                    for s, name, rows in ((0, "src", rows_i[:, 0]), (1, "dst", rows_i[:, 1]), (2, "edge_weight", rows_f[:, 2])):
                        flat = a[name]
                        eng.dma_start(rows[:, 0:3, :], flat[0:3 * CH * P].rearrange("(c p e) -> p c e", c=3, e=P)).then_inc(loaded, 16)
                        eng.dma_start(rows[0:whole, 3, :],
                                      flat[3 * CH * P:(3 * CH + whole) * P].rearrange("(p e) -> p e", e=P)).then_inc(loaded, 16)
                        eng.dma_start(rows[whole:whole + 1, 3, 0:part],
                                      flat[(3 * CH + whole) * P:E].rearrange("(o e) -> o e", o=1)).then_inc(loaded, 16)
                        n += 48
                    eng.wait_ge(zeroed, 2)
                    k = 0
                    for flag in (flag_dst, flag_src):
                        eng.dma_start(flag.rearrange("(p c) o -> p (c o)", p=P), zero[:, 0:ET]).then_inc(stored, 16)
                        k += 16
                    for half in range(2):
                        eng.dma_start(ERE.rearrange("(p c) h -> p (c h)", p=P)[:, half * 4 * ET:(half + 1) * 4 * ET],
                                      zero).then_inc(stored, 16)
                        k += 16
                    for h in (hist_start, hist_count):
                        eng.dma_start(h[:, HI * LO:NP], zero[0:2, 0:NP - HI * LO]).then_inc(stored, 16)
                        k += 16
                    eng.dma_start(PR[ROW_ZERO:ROW_ZERO + 1, :], zero[0:1, 0:D]).then_inc(stored, 16)
                    eng.wait_ge(cast, 2)
                    eng.dma_start(dst_row.rearrange("o (c p e) -> p (o c) e", c=4, e=P), rows_f[:, 1]).then_inc(stored, 16)
                    eng.wait_ge(zeroed, 4)
                    eng.dma_start(PR[ROW_LOW:ROW_LOW + 1, :], low_sent).then_inc(stored, 16)
                    eng.dma_start(PA[ROW_ZERO:ROW_ZERO + 1, :], sent[0:1, :]).then_inc(stored, 16)
                    eng.dma_start(CR[ET:ET + 1, :], sent[0:1, :]).then_inc(stored, 16)
                    eng.wait_ge(stored, k + 16 * 5)

                @block.vector
                def _(eng):
                    eng.wait_ge(zeroed, 2)
                    eng.memset(low_sent, LOW).then_inc(zeroed, 1)
                    eng.memset(sent[0:1, D + HEADS:RW], LOW).then_inc(zeroed, 1)
                    eng.wait_ge(loaded, 144)
                    for s in range(2):
                        eng.tensor_copy(rows_f[:, s], rows_i[:, s]).then_inc(cast, 1)
                    for s, dst in ((0, SRCF), (1, DSTF), (2, WE)):
                        eng.wait_ge(turned, s + 1)
                        eng.tensor_copy(dst[:, :], ps[:, s, 0:ET]).then_inc(moved, 1)
                    eng.wait_ge(moved, 1)
                    eng.tensor_copy(SRCI[:, :], SRCF[:, :]).then_inc(moved, 1)

                @block.tensor
                def _(eng):
                    eng.wait_ge(cast, 2)
                    eng.wait_ge(loaded, 144)
                    for s in range(3):
                        for c in range(4):
                            last = eng.transpose(ps[:, s, c * CH:(c + 1) * CH], rows_f[:, s, c, :], ident[0:CH, 0:CH])
                        last.then_inc(turned, 1)

        def split_key(c, key, hi, lo, tmp):
            c.link(c.eng.tensor_copy(tmp[:, 0], key[:, :]))
            c.inc(c.eng.tensor_scalar(tmp[:, 1], tmp[:, 0], LO.bit_length() - 1, None, ALU.arith_shift_right))
            c.link(c.eng.tensor_scalar(tmp[:, 2], tmp[:, 0], LO - 1, None, ALU.bitwise_and))
            c.inc(c.eng.tensor_copy(hi[:, :], tmp[:, 1]))
            c.link(c.eng.tensor_copy(lo[:, :], tmp[:, 2]))

        count = sb("count", [HI, LO])
        startv = sb("startv", [HI, LO])
        small = sb("small", [HI, LO + 2])

        def one_hot(eng, dst, key, t, n, width):
            return eng.tensor_tensor(dst, key[:, ds(t, n)].unsqueeze(2).broadcast_to([P, n, width]),
                                     iota_b[:, 0:width].unsqueeze(1).broadcast_to([P, n, width]), ALU.is_equal)

        def histogram(which, key):
            steps = ET // HB
            with Stage(nc, f"hist{which}") as st:
                chain, hot, made, moved = (st.sem(n) for n in ("chain", "hot", "made", "moved"))
                passed, stored, rows_done = st.sem("passed"), st.sem("stored"), st.sem("rows")
                ps = st.stack.enter_context(nc.psum_tensor(f"hist{which}_ps", [HI, 2, 512], F32))
                rs = st.stack.enter_context(nc.psum_tensor(f"hist{which}_rs", [HI, 512], F32))
                block = st.block()

                @block.vector
                def _(eng):
                    c = Count(eng, chain)
                    split_key(c, key, key_hi, key_lo, key_tmp)
                    with eng.Fori(0, steps // 2) as i:
                        for b in range(2):
                            eng.wait_ge(made, i * 2 + (b + 1))
                            one_hot(eng, oh_hi[:, b], key_hi, i * (2 * HB) + b * HB, HB, HI).then_inc(hot, 1)
                            one_hot(eng, oh_lo[:, b], key_lo, i * (2 * HB) + b * HB, HB, LO).then_inc(hot, 1)
                    eng.wait_ge(moved, steps + 2)
                    c.link(eng.tensor_reduce(count[:, :], HIST[0:HI].rearrange("p t l -> p l t"), AX.X, ALU.add))
                    c.link(eng.tensor_tensor_scan(small[:, 0:LO], ones[0:HI, 0:LO], count[:, :], 0.0, ALU.mult, ALU.add))
                    c.link(eng.tensor_tensor(startv[:, :], small[:, 0:LO], count[:, :], ALU.subtract))
                    eng.sem_inc(rows_done, 1)
                    eng.wait_ge(rows_done, 2)
                    c.link(eng.tensor_copy(small[:, LO:LO + 1], rs[:, 0:1]))
                    c.link(eng.tensor_scalar(startv[:, :], startv[:, :], small[:, LO:LO + 1], None, ALU.add))
                    eng.sem_inc(rows_done, 1)

                @block.tensor
                def _(eng):
                    eng.sem_inc(made, 2)
                    with eng.Fori(0, steps // 2) as i:
                        for b in range(2):
                            eng.wait_ge(moved, i * 2 + (b + 1))
                            eng.wait_ge(hot, i * 4 + (2 * b + 2))
                            for k in range(HB):
                                last = eng.matmul(ps[:, b, k * LO:(k + 1) * LO], oh_hi[:, b, k, :], oh_lo[:, b, k, :],
                                                  start=True, stop=True)
                            last.then_inc(made, 1)
                    eng.wait_ge(rows_done, 1)
                    eng.matmul(rs[:, 0:1], before[0:HI, 0:HI], small[:, LO - 1:LO], start=True, stop=True).then_inc(rows_done, 1)

                @block.scalar
                def _(eng):
                    eng.sem_inc(moved, 2)
                    with eng.Fori(0, steps // 2) as i:
                        for b in range(2):
                            eng.wait_ge(made, i * 2 + (b + 3))
                            eng.sem_inc(passed, 1)
                            eng.activation(HIST[0:HI, ds(i * (2 * HB) + b * HB, HB), :],
                                           ps[:, b, 0:HB * LO].rearrange("p (k l) -> p k l", l=LO), ACT.Copy).then_inc(moved, 1)

                @block.sync
                def _(eng):
                    eng.wait_ge(rows_done, 3)
                    eng.dma_start(hist_start[which:which + 1, 0:HI * LO].rearrange("o (h l) -> (o h) l", l=LO), startv[:, :]).then_inc(stored, 16)
                    eng.dma_start(hist_count[which:which + 1, 0:HI * LO].rearrange("o (h l) -> (o h) l", l=LO), count[:, :]).then_inc(stored, 16)
                    eng.wait_ge(stored, 32)

        node_f = sb("node_f", [P, 6, NT])

        def node_indices():
            START, CNT, HAS, LASTE, T1, T2_ = range(6)
            MASKS = ARENA[:, 0:ET * 2]
            with Stage(nc, "node") as st:
                loaded, chain, ready = (st.sem(n) for n in ("loaded", "chain", "ready"))
                marked = gathered[0]
                flags_in, made, stored, rooted = (st.sem(n) for n in ("flags_in", "made", "stored", "rooted"))
                fl = ARENA[:, 0:2 * ET].rearrange("p (s e) -> p s e", s=2)
                mk = ARENA[:, 2 * ET:4 * ET].bitcast(BF16).rearrange("p (s e) -> p s e", e=ET)
                block = st.block()

                @block.sync
                def _(eng):
                    with nc.allow_non_contiguous_dma("node numbers across the partitions"):
                        for w in range(2):
                            if w:
                                eng.wait_ge(ready, 1)
                            for k, h in ((START, hist_start), (CNT, hist_count)):
                                eng.dma_start(node_f[:, k, :], h[w:w + 1, :].rearrange("o (t p) -> p (o t)", p=P)).then_inc(loaded, 16)
                    marked.arrived(eng, 2 * NT)
                    for s, flag in enumerate((flag_dst, flag_src)):
                        eng.dma_start(fl[:, s, :], flag.rearrange("(p c) o -> p (c o)", p=P)).then_inc(flags_in, 16)
                    eng.wait_ge(made, 4)
                    for k, row in ((0, nst_dst), (1, low_dst), (2, low_src)):
                        eng.dma_start(row[:, 0:EP].rearrange("o (p c) -> (o p) c", p=P), mk[:, k, :]).then_inc(stored, 16)
                        eng.dma_start(row[:, EP:EP + P], mk[0:1, 3, 0:P]).then_inc(stored, 16)
                    eng.wait_ge(stored, 96)

                @block.vector
                def _(eng):
                    c = Count(eng, chain)
                    f = node_f
                    for w, norm, first in ((0, norm_in, first_dst), (1, norm_out, first_src)):
                        eng.wait_ge(loaded, 32 * (w + 1))
                        c.inc(eng.tensor_scalar(norm[:, :], f[:, CNT, :], 1.0, None, ALU.max))
                        c.inc(eng.tensor_scalar(f[:, HAS, :], f[:, CNT, :], 1.0, None, ALU.min))
                        c.link(eng.tensor_tensor(f[:, LASTE, :], f[:, START, :], f[:, CNT, :], ALU.add))
                        c.link(eng.tensor_scalar(f[:, T1, :], f[:, START, :], -OOB, None, ALU.add))
                        c.link(eng.tensor_tensor(f[:, T1, :], f[:, T1, :], f[:, HAS, :], ALU.mult))
                        c.link(eng.tensor_scalar(f[:, T1, :], f[:, T1, :], OOB, None, ALU.add))
                        c.link(eng.tensor_copy(first[:, :], f[:, T1, :]))
                        for row, dst in (((ROW_ZERO, end_sum), (ROW_LOW, end_max)) if w == 0 else ((ROW_LOW, end_src),)):
                            c.link(eng.tensor_scalar(f[:, T1, :], f[:, LASTE, :], -(row + 1.0), None, ALU.add))
                            c.link(eng.tensor_tensor(f[:, T1, :], f[:, T1, :], f[:, HAS, :], ALU.mult))
                            c.link(eng.tensor_scalar(f[:, T1, :], f[:, T1, :], float(row), None, ALU.add))
                            c.link(eng.tensor_copy(dst[:, :], f[:, T1, :]))
                        if w == 0:
                            c.link(eng.tensor_scalar(f[:, T1, :], f[:, LASTE, :], -1.0, None, ALU.add))
                            c.link(eng.tensor_scalar(f[:, T1, :], f[:, T1, :], 0.0, None, ALU.max))
                            c.link(eng.tensor_copy(carry_row[:, :], f[:, T1, :]))
                            c.link(eng.tensor_scalar(carry_row[:, :], carry_row[:, :], 7, None, ALU.arith_shift_right))
                            c.link(eng.tensor_copy(f[:, T1, :], carry_row[:, :]))
                            c.link(eng.tensor_scalar(f[:, T2_, :], f[:, T1, :], float(P), None, ALU.mult))
                            c.link(eng.tensor_tensor(f[:, T2_, :], f[:, START, :], f[:, T2_, :], ALU.is_lt))
                            c.link(eng.tensor_tensor(f[:, T2_, :], f[:, T2_, :], f[:, HAS, :], ALU.mult))
                            c.link(eng.tensor_scalar(f[:, T1, :], f[:, T1, :], -(ET + 1.0), None, ALU.add))
                            c.link(eng.tensor_tensor(f[:, T1, :], f[:, T1, :], f[:, T2_, :], ALU.mult))
                            c.link(eng.tensor_scalar(f[:, T1, :], f[:, T1, :], float(ET), None, ALU.add))
                            c.link(eng.tensor_copy(carry_row[:, :], f[:, T1, :]))
                        eng.sem_inc(ready, 1)
                    eng.wait_ge(rooted, 2)
                    for norm in (norm_in, norm_out):
                        eng.reciprocal(norm[:, :], norm[:, :])
                    eng.wait_ge(flags_in, 32)
                    eng.tensor_scalar(mk[:, 0, :], fl[:, 0, :], -1.0, 1.0, ALU.mult, ALU.add).then_inc(made, 1)
                    eng.tensor_scalar(mk[:, 1, :], fl[:, 0, :], LOW, None, ALU.mult).then_inc(made, 1)
                    eng.tensor_scalar(mk[:, 2, :], fl[:, 1, :], LOW, None, ALU.mult).then_inc(made, 1)
                    eng.memset(mk[:, 3, :], 0.0).then_inc(made, 1)

                @block.scalar
                def _(eng):
                    eng.wait_ge(ready, 2)
                    for norm in (norm_in, norm_out):
                        eng.activation(norm[:, :], norm[:, :], ACT.Sqrt).then_inc(rooted, 1)

                @block.gpsimd
                def _(eng):
                    eng.wait_ge(ready, 2)
                    for first, flag in ((first_dst, flag_dst), (first_src, flag_src)):
                        for t in range(NT):
                            eng.indirect_dma_start(flag, bass.IndirectOffsetOnAxis(ap=first[:, t:t + 1], axis=0),
                                                   ones[:, 0:1], None, bounds_check=EP - 1, oob_is_err=False).then_inc(marked.sem, 16)
            marked.close(2 * NT)


        rank = sb("rank", [P, 2, 2, RB])

        def sort_places():
            steps = ET // RB
            with Stage(nc, "rank") as st:
                names = ("scanned", "hot", "turned", "ot", "made", "chain", "passed", "done")
                scanned, hot, turned, ot, made, chain, passed, done = (st.sem(n) for n in names)
                tps = st.stack.enter_context(nc.psum_tensor("rank_t", [P, 2, 2, RB * P], BF16))
                gps = st.stack.enter_context(nc.psum_tensor("rank_g", [P, 2, 512], F32))
                lps = st.stack.enter_context(nc.psum_tensor("rank_l", [P, 2, 512], F32))
                block = st.block()

                @block.vector
                def _(eng):
                    c = Count(eng, chain)
                    for lo in range(LO):
                        c.inc(eng.tensor_tensor_scan(S[0:HI, 0, 0, 1:ET] if lo % 2 == 0 else S[0:HI, 0, 1, 1:ET],
                                                     ones[0:HI, 0:1].broadcast_to([HI, ET - 1]),
                                                     HIST[0:HI, 0:ET - 1, lo], startv[:, lo:lo + 1], ALU.mult, ALU.add))
                        c.wait()
                        c.inc(eng.tensor_copy(HIST[0:HI, 1:ET, lo], S[0:HI, 0, lo % 2, 1:ET]))
                        c.wait()
                        c.inc(eng.tensor_copy(HIST[0:HI, 0, lo:lo + 1], startv[:, lo:lo + 1]))
                    c.wait()
                    eng.sem_inc(scanned, 1)

                    def hot_step(t, b, _):
                        eng.wait_ge(done, t + 1)
                        one_hot(eng, oh_hi[:, b, 0:RB], key_hi, t * RB, RB, HI).then_inc(hot, 1)
                        one_hot(eng, oh_lo[:, b, 0:RB], key_lo, t * RB, RB, LO).then_inc(hot, 1)

                    def rank_step(t, b, _):
                        eng.wait_ge(made, t + 1)
                        for k in range(RB):
                            eng.scalar_tensor_tensor(rank_tmp[:, b, k, :], gps[:, b, k * P:(k + 1) * P], 2.0, before[:, :],
                                                     ALU.is_equal, ALU.mult, accum_out=rank[:, b, 0, k:k + 1]).then_inc(passed, 1)
                        eng.tensor_tensor(sel[:, b], lps[:, b, 0:RB * LO].rearrange("p (k l) -> p k l", l=LO),
                                          oh_lo[:, b, 0:RB, :], ALU.mult).then_inc(passed, 1)
                        eng.wait_ge(passed, t * 6 + 5)
                        eng.tensor_reduce(rank[:, b, 1, :], sel[:, b], AX.X, ALU.add).then_inc(passed, 1)
                        eng.wait_ge(passed, t * 6 + 6)
                        eng.tensor_tensor(pos[:, ds(t * RB, RB)], rank[:, b, 0, :], rank[:, b, 1, :], ALU.add).then_inc(done, 1)

                    eng.sem_inc(done, 2)
                    pipelined(steps, 2, eng, (hot_step, 1), (rank_step, 0))

                @block.tensor
                def _(eng):
                    eng.wait_ge(scanned, 1)

                    def turn(t, b, _):
                        eng.wait_ge(hot, t * 2 + 2)
                        eng.wait_ge(ot, t + 1)
                        for k in range(RB):
                            eng.transpose(tps[0:HI, b, 0, k * P:(k + 1) * P], oh_hi[:, b, k, :], identb[:, :])
                            last = eng.transpose(tps[0:LO, b, 1, k * P:(k + 1) * P], oh_lo[:, b, k, :], identb[:, :])
                        last.then_inc(turned, 1)

                    def product(t, b, _):
                        eng.wait_ge(ot, t + 3)
                        eng.wait_ge(done, t + 1)
                        for k in range(RB):
                            cols = slice(k * P, (k + 1) * P)
                            eng.matmul(gps[:, b, cols], oh_t[0:HI, b, 0, cols], oh_t[0:HI, b, 0, cols], start=True, stop=False)
                            eng.matmul(gps[:, b, cols], oh_t[0:LO, b, 1, cols], oh_t[0:LO, b, 1, cols], start=False, stop=True)
                            last = eng.matmul(lps[:, b, k * LO:(k + 1) * LO], oh_tf[0:HI, b, cols], HIST[0:HI, ds(t * RB + k, 1), :].rearrange("p o l -> p (o l)"),
                                              start=True, stop=True)
                        last.then_inc(made, 1)

                    pipelined(steps, 2, eng, (turn, 1), (product, 0))

                @block.scalar
                def _(eng):
                    eng.sem_inc(ot, 2)

                    def move(t, b, _):
                        eng.wait_ge(turned, t + 1)
                        eng.wait_ge(done, t + 1)
                        eng.activation(oh_t[0:HI, b, 0, :], tps[0:HI, b, 0, :], ACT.Copy)
                        eng.activation(oh_t[0:LO, b, 1, :], tps[0:LO, b, 1, :], ACT.Copy)
                        last = eng.activation(oh_tf[0:HI, b, :], tps[0:HI, b, 0, :], ACT.Copy)
                        last.then_inc(ot, 1)

                    pipelined(steps, 2, eng, (move, 0))


        def sort_edges():
            with Stage(nc, "sort") as st:
                chain, ready, made, free, opened = (st.sem(n) for n in ("chain", "ready", "made", "free", "opened"))
                digits = [st.stack.enter_context(nc.psum_tensor(f"sort_{n}", [P, ET], F32)) for n in ("hi", "lo")]
                block = st.block()

                def digits_of(c, src, shift, hi, lo):
                    c.link(c.eng.tensor_copy(key_tmp[:, 0], src[:, :]))
                    c.inc(c.eng.tensor_scalar(key_tmp[:, 1], key_tmp[:, 0], shift, None, ALU.arith_shift_right))
                    c.link(c.eng.tensor_scalar(key_tmp[:, 2], key_tmp[:, 0], (1 << shift) - 1, None, ALU.bitwise_and))
                    c.inc(c.eng.tensor_copy(hi[:, :], key_tmp[:, 1]))
                    c.link(c.eng.tensor_copy(lo[:, :], key_tmp[:, 2]))

                @block.vector
                def _(eng):
                    c = Count(eng, chain)
                    digits_of(c, pos, 7, place_hi, place_lo)
                    digits_of(c, DSTF, 6, pay_hi, pay_lo)
                    c.link(eng.memset(no_places[:, :], 0.0))
                    eng.sem_inc(opened, 1)
                    with eng.Fori(0, ET // 4) as i:
                        for b in range(4):
                            eng.wait_ge(free, i * 4 + (b + 1))
                            t = i * 4 + b
                            eng.tensor_scalar(ohp[:, b, :], iota_b[:, :], place_lo[:, ds(t, 1)], None, ALU.is_equal)
                            eng.tensor_scalar(val[:, b, 0, :], iota_h[:, :], place_hi[:, ds(t, 1)], pay_hi[:, ds(t, 1)], ALU.is_equal, ALU.mult)
                            eng.tensor_scalar(val[:, b, 1, :], iota_h[:, :], place_hi[:, ds(t, 1)], pay_lo[:, ds(t, 1)], ALU.is_equal, ALU.mult).then_inc(ready, 1)
                    eng.wait_ge(made, 1)
                    c.link(eng.tensor_scalar(place_hi[:, :], digits[0][:, :], 64.0, None, ALU.mult))
                    c.link(eng.tensor_tensor(place_hi[:, :], digits[1][:, :], place_hi[:, :], ALU.add))
                    c.link(eng.tensor_copy(BYSRC[:, :], place_hi[:, :]))

                @block.tensor
                def _(eng):
                    eng.wait_ge(opened, 1)
                    for d in range(2):
                        eng.matmul(digits[d][:, :], no_places[:, 0:P], no_places[:, P:P + ET], start=True, stop=False)
                    eng.sem_inc(free, 4)
                    with eng.Fori(0, ET // 4) as i:
                        for b in range(4):
                            eng.wait_ge(ready, i * 4 + (b + 1))
                            for d in range(2):
                                last = eng.matmul(digits[d][:, :], ohp[:, b, :], val[:, b, d, :], start=False, stop=False)
                            last.then_inc(free, 1)
                    for d in range(2):
                        last = eng.matmul(digits[d][:, :], no_places[:, 0:P], no_places[:, P:P + ET], start=False, stop=True)
                    last.then_inc(made, 1)

        def node_products(name, stage, w1, out1, w2=None, out2=None, gather=None, table=None, table2=None):
            n2 = 0 if w2 is None else w2.shape[2]
            u = NODE_UNROLL
            with Stage(nc, name) as st:
                names = ("staged", "turned", "xt", "made", "moved", "done", "chain", "passed", "stored", "passed2")
                staged, turned, xt, made, moved, done, chain, passed, stored, passed2 = (st.sem(n) for n in names)
                got = gathered[0:NT // u]
                tps = st.stack.enter_context(nc.psum_tensor(f"{name}_t", [P, 3, 512], F32))
                mps = st.stack.enter_context(nc.psum_tensor(f"{name}_m", [P, u, 512], F32))
                tp = [tps[:, j % 3, 0:D] for j in range(u)]
                block = st.block()

                if gather is not None:
                    @block.gpsimd
                    def _(eng):
                        rows, index = gather
                        for t in range(NT):
                            eng.indirect_dma_start(AGG[:, t, :], None, rows,
                                                   bass.IndirectOffsetOnAxis(ap=index[:, t:t + 1], axis=0)).then_inc(got[t // u].sem, 16)

                @block.vector
                def _(eng):
                    eng.sem_inc(done, u)
                    if gather is not None:
                        for k in range(NT // u):
                            got[k].arrived(eng, u)

                    def ahead(t, slot, _):
                        eng.wait_ge(turned, t + 1)
                        stage(eng, t, slot, chain, staged)

                    def behind(t, slot, _):
                        eng.wait_ge(moved, t + 1)
                        eng.wait_ge(made, t + 1)
                        out2(eng, t, slot, mps[:, slot, :], done)

                    pipelined(NT, u, eng, (ahead, 2), (behind, 0))

                @block.tensor
                def _(eng):
                    eng.sem_inc(turned, u)

                    def turn(t, slot, _):
                        eng.wait_ge(staged, t + 1)
                        eng.wait_ge(xt, t + (u - 1))
                        for k in range(2):
                            last = eng.transpose(tp[slot][:, k * P:(k + 1) * P], R[:, slot, k * P:(k + 1) * P], ident[:, :])
                        last.then_inc(turned, 1)

                    def product(t, slot, _):
                        eng.wait_ge(xt, t + (u + 1))
                        eng.wait_ge(done, t + 1)
                        for k in range(2):
                            last = eng.matmul(mps[:, slot, 0:D], XT[:, slot, k * P:(k + 1) * P], w1[:, k, :],
                                              start=k == 0, stop=k == 1)
                        if n2:
                            for k in range(2):
                                last = eng.matmul(mps[:, slot, D:D + n2], XT[:, slot, k * P:(k + 1) * P], w2[:, k, :],
                                                  start=k == 0, stop=k == 1)
                        last.then_inc(made, 1)

                    pipelined(NT, u, eng, (turn, 1), (product, 0))

                @block.scalar
                def _(eng):
                    eng.sem_inc(xt, u)

                    def ahead(t, slot, _):
                        eng.wait_ge(turned, t + (u + 1))
                        eng.wait_ge(made_free, t + 1)
                        eng.activation(XT[:, slot, :], tp[slot], ACT.Copy).then_inc(xt, 1)

                    def behind(t, slot, _):
                        eng.wait_ge(made, t + 1)
                        eng.wait_ge(done, t + 1)
                        eng.sem_inc(passed, 1)
                        out1(eng, t, slot, mps[:, slot, 0:D]).then_inc(moved, 1)

                    made_free = done
                    pipelined(NT, u, eng, (ahead, 1), (behind, 0))

                tables = [x for x in (table, table2) if x is not None]
                if tables:
                    @block.sync
                    def _(eng):
                        for k in range(NT // u):
                            eng.wait_ge(done, u + (k + 1) * u)
                            for src, dst in tables:
                                eng.dma_start(dst[k * u * P:(k + 1) * u * P, :].rearrange("(t p) d -> p t d", p=P),
                                              src[:, k * u:(k + 1) * u, :]).then_inc(stored, 16)
                        eng.wait_ge(stored, NT // u * 16 * len(tables))
            if gather is not None:
                for g in got:
                    g.close(NODE_UNROLL)


        def tile_of(view, t):
            return view[:, ds(t, 1), :].rearrange("p o d -> p (o d)") if not isinstance(t, int) else view[:, t, :]

        def stage_copy(src):
            def stage(eng, t, slot, chain, staged):
                eng.tensor_copy(R[:, slot, :], tile_of(src, t)).then_inc(staged, 1)
            return stage

        def stage_gcn(layer):
            def stage(eng, t, slot, chain, staged):
                eng.scalar_tensor_tensor(TMP2[:, slot, :], tile_of(AGG, t), norm_in[:, ds(t, 1)], CHB[:, layer, :],
                                         ALU.mult, ALU.add).then_inc(chain, 1)
                eng.wait_ge(chain, t + 1)
                eng.tensor_scalar(R[:, slot, :], TMP2[:, slot, :], 0.0, None, ALU.max).then_inc(staged, 1)
            return stage

        def gcn_table(layer, with_mlp):
            def out1(eng, t, slot, ps):
                return eng.activation(TMP[:, slot, :], ps, ACT.Copy, scale=norm_out[:, ds(t, 1)])

            def out2(eng, t, slot, ps, done):
                if with_mlp:
                    eng.tensor_tensor(tile_of(X, t), ps[:, D:2 * D], tile_of(X, t), ALU.add)
                eng.scalar_tensor_tensor(tile_of(AGG, t), GB[:, layer, :], norm_out[:, ds(t, 1)], TMP[:, slot, :],
                                         ALU.mult, ALU.add).then_inc(done, 1)
            return out1, out2

        def edge_pass(name, index, ops, mask, weighted):
            op0, op1 = ops
            with Stage(nc, name) as st:
                got = gathered[0:4]
                ready = [st.sem(f"ready{q}") for q in range(4)]
                names = ("scaled", "turned", "scanned", "back", "pairs", "o_free", "stored", "go_pool", "go_act", "go_sp")
                scaled, turned, scanned, back, pairs, o_free, stored, go_pool, go_act, go_sp = (st.sem(n) for n in names)
                fm = st.stack.enter_context(nc.psum_tensor(f"{name}_fm", [P, 2, 2, GT * P], F32))
                em = st.stack.enter_context(nc.psum_tensor(f"{name}_em", [P, 2, 2, D], F32))
                out_rows = PR[0:EP, :].rearrange("(t p) d -> p t d", p=P)
                uses = 3 if weighted else 2
                block = st.block()

                @block.sync
                def _(eng):
                    def prefetch(g, q):
                        eng.dma_start(idxbuf[:, q, :], index[:, ds(g * GT, GT)]).then_inc(ready[q], 16)
                        eng.dma_start(maskbuf[:, q, :], mask[0:1, ds(g * (GT * P), GT * P)].broadcast_to([P, GT * P])).then_inc(ready[q], 16)
                        if weighted:
                            eng.dma_start(wbuf[:, q, :], WE[:, ds(g * GT, GT)]).then_inc(ready[q], 16)

                    for q in range(4):
                        prefetch(q, q)

                    def store(g, q):
                        eng.wait_ge(pairs, g * 2 + 6)
                        eng.sem_inc(go_sp, 1)
                        eng.dma_start(out_rows[:, ds(g * GT, GT), :], O[:, q % 2, :, 0:D]).then_inc(stored, 16)
                        if not isinstance(g, int) or g + 4 < NG:
                            prefetch(g + 4, q)
                        eng.wait_ge(stored, g * 16 + 16)
                        eng.sem_inc(o_free, 1)

                    with eng.Fori(0, (NG - 4) // 4) as i:
                        for q in range(4):
                            store(i * 4 + q, q)
                    for g in range((NG - 4) // 4 * 4, NG):
                        store(g, g % 4)

                @block.gpsimd
                def _(eng):
                    def gather(g, q, turn):
                        eng.wait_ge(ready[q], turn * (16 * uses) + 16 * uses)
                        eng.sem_inc(go_pool, 1)
                        for k in range(GT):
                            eng.indirect_dma_start(G[:, q * GT + k, 0:D], None, T,
                                                   bass.IndirectOffsetOnAxis(ap=idxbuf[:, q, k:k + 1], axis=0)).then_inc(got[q].sem, 16)

                    pipelined(NG, 4, eng, (gather, 0))

                @block.tensor
                def _(eng):
                    def forth(g, q, turn):
                        if weighted:
                            eng.wait_ge(scaled, g + 1)
                        else:
                            got[q].arrived(eng, turn * GT + GT)
                        eng.wait_ge(scanned, g + 1)
                        for k in range(GT):
                            for h in range(2):
                                last = eng.transpose(fm[:, q % 2, h, k * P:(k + 1) * P], G[:, q * GT + k, h * P:(h + 1) * P], ident[:, :])
                        last.then_inc(turned, 1)

                    def hither(g, q, turn):
                        eng.wait_ge(scanned, g + 3)
                        for pair in range(2):
                            eng.wait_ge(pairs, g * 2 + (pair + 3))
                            for k in range(2):
                                for h in range(2):
                                    last = eng.transpose(em[:, pair, k, h * P:(h + 1) * P],
                                                         S[:, q % 2, h, (2 * pair + k) * P:(2 * pair + k + 1) * P], ident[:, :])
                            last.then_inc(back, 1)

                    pipelined(NG, 4, eng, (forth, 1), (hither, 0))

                @block.vector
                def _(eng):
                    eng.memset(S[:, 1, :, GT * P - 1:GT * P], 0.0).then_inc(scanned, 1)
                    eng.wait_ge(scanned, 1)
                    eng.sem_inc(scanned, 1)

                    def scan(g, q, turn):
                        eng.wait_ge(turned, g + 1)
                        eng.wait_ge(pairs, g * 2 + 2)
                        eng.wait_ge(scanned, g + 2)
                        for h in range(2):
                            last = eng.tensor_tensor_scan(S[:, q % 2, h, :], maskbuf[:, q, :], fm[:, q % 2, h, :],
                                                          S[:, 1 - q % 2, h, GT * P - 1:GT * P], op0, op1)
                        last.then_inc(scanned, 1)

                    pipelined(NG, 4, eng, (scan, 0))

                @block.scalar
                def _(eng):
                    eng.sem_inc(pairs, 4)
                    eng.sem_inc(o_free, 2)

                    def scale(g, q, turn):
                        got[q].arrived(eng, turn * GT + GT)
                        for k in range(GT):
                            last = eng.activation(G[:, q * GT + k, 0:D], G[:, q * GT + k, 0:D], ACT.Copy, scale=wbuf[:, q, k:k + 1])
                        last.then_inc(scaled, 1)

                    def evac(g, q, turn):
                        eng.wait_ge(o_free, g + 1)
                        for pair in range(2):
                            eng.wait_ge(back, g * 2 + (pair + 1))
                            eng.activation(O[:, q % 2, 2 * pair:2 * pair + 2, 0:D], em[:, pair], ACT.Copy).then_inc(pairs, 1)

                    if weighted:
                        pipelined(NG, 4, eng, (scale, 1), (evac, 0))
                    else:
                        pipelined(NG, 4, eng, (evac, 0))
            for q in range(4):
                got[q].close(GT * ((NG - q + 3) // 4))


        RST, NMR = sb("RST", [P, NT]), sb("NMR", [P, NT])
        BS, MV5 = sb("BS", [P, NODE_UNROLL, 6]), sb("MV5", [P, NODE_UNROLL, 2])

        def layer_norm(name, prepare, gather=None, out_rows=None):
            u = NODE_UNROLL
            with Stage(nc, name) as st:
                names = ("chain", "aggregated", "rooted", "scaled", "done", "stored", "apart")
                chain, aggregated, rooted, scaled, done, stored, apart = (st.sem(n) for n in names)
                got = gathered[0:NT // u]
                block = st.block()

                if gather is not None:
                    @block.gpsimd
                    def _(eng):
                        rows, index = gather
                        for t in range(NT):
                            eng.indirect_dma_start(AGG[:, t, :], None, rows,
                                                   bass.IndirectOffsetOnAxis(ap=index[:, t:t + 1], axis=0)).then_inc(got[t // u].sem, 16)

                @block.vector
                def _(eng):
                    if gather is not None:
                        for k in range(NT // u):
                            got[k].arrived(eng, u)
                    c = Count(eng, chain)
                    with c.loop(NT // u, LINKS[prepare] + 3) as i:
                        prepare(c, ds(i * u, u))
                        eng.sem_inc(apart, 1)
                        for j in range(u):
                            last = eng.bn_stats(BS[:, j, :], X[:, ds(i * u + j, 1), :].rearrange("p o d -> p (o d)"))
                        c.link(last)
                        eng.sem_inc(apart, 1)
                        for j in range(u):
                            last = eng.bn_aggr(MV5[:, j, :], BS[:, j, :])
                        c.link(last)
                        c.link(eng.tensor_copy(MV[:, ds(i * u, u), :], MV5[:, :, :]))
                    c.link(eng.tensor_scalar(RST[:, :], MV[:, :, 1], EPS, None, ALU.add))
                    eng.sem_inc(aggregated, 1)
                    eng.wait_ge(rooted, 1)
                    c.link(eng.reciprocal(RST[:, :], RST[:, :]))
                    c.link(eng.tensor_tensor(NMR[:, :], MV[:, :, 0], RST[:, :], ALU.mult))
                    c.link(eng.tensor_scalar(NMR[:, :], NMR[:, :], -1.0, None, ALU.mult))
                    eng.sem_inc(scaled, 1)

                @block.scalar
                def _(eng):
                    eng.wait_ge(aggregated, 1)
                    eng.activation(RST[:, :], RST[:, :], ACT.Sqrt).then_inc(rooted, 1)
                    eng.wait_ge(scaled, 1)
                    with eng.Fori(0, NT // u) as i:
                        for j in range(u):
                            t = i * u + j
                            last = eng.activation(tile_of(X, t), tile_of(X, t), ACT.Identity,
                                                  bias=NMR[:, ds(t, 1)], scale=RST[:, ds(t, 1)])
                        last.then_inc(done, 1)

                if out_rows is not None:
                    @block.sync
                    def _(eng):
                        eng.wait_ge(done, NT // u)
                        eng.dma_start(out_rows[0:(NT - 1) * P, :].rearrange("(t p) d -> p t d", p=P), X[:, 0:NT - 1, :]).then_inc(stored, 16)
                        eng.dma_start(out_rows[(NT - 1) * P:N, :], X[0:LAST, NT - 1, :]).then_inc(stored, 16)
                        eng.wait_ge(stored, 32)
            if gather is not None:
                for g in got:
                    g.close(NODE_UNROLL)


        def none(c, at):
            pass

        def add_bias(c, at):
            c.link(c.eng.tensor_tensor(X[:, at, :], X[:, at, :], MB[:, :].unsqueeze(1).broadcast_to([P, NODE_UNROLL, D]), ALU.add))

        def edge_max(c, at):
            c.link(c.eng.tensor_tensor(AGG[:, at, :], C[:, at, 0:D], AGG[:, at, :], ALU.add))
            c.link(c.eng.scalar_tensor_tensor(X[:, at, :], AGG[:, at, :], 0.0, X[:, at, :], ALU.max, ALU.add))

        def last(c, at):
            c.link(c.eng.scalar_tensor_tensor(X[:, at, :], Y[:, at, :], 0.0, X[:, at, :], ALU.max, ALU.add))

        LINKS = {none: 0, add_bias: 1, edge_max: 2, last: 1}

        mean_b, rstd_b = sb("mean_b", [P, D]), sb("rstd_b", [P, D])

        def batch_norm(name, layer, gather):
            u = NODE_UNROLL
            with Stage(nc, name) as st:
                names = ("chain", "made", "summed", "squared", "dev", "var_ready")
                chain, made, summed, squared, dev, var_ready = (st.sem(n) for n in names)
                got = gathered[0:NT // u]
                ps = st.stack.enter_context(nc.psum_tensor(f"{name}_ps", [P, 2, 512], F32))
                block = st.block()

                @block.gpsimd
                def _(eng):
                    rows, index = gather
                    for t in range(NT):
                        eng.indirect_dma_start(AGG[:, t, :], None, rows,
                                               bass.IndirectOffsetOnAxis(ap=index[:, t:t + 1], axis=0)).then_inc(got[t // u].sem, 16)

                def column_sums(eng, dst, src, ready):
                    for t in range(NT):
                        if t % u == 0:
                            eng.wait_ge(ready, t // u + 1)
                        n = P if t < NT - 1 else LAST
                        last = eng.matmul(dst, ones[0:n, :], src[0:n, t, :], start=t == 0, stop=t == NT - 1)
                    last.then_inc(summed, 1)

                @block.tensor
                def _(eng):
                    column_sums(eng, ps[:, 0, 0:D], Y, made)
                    column_sums(eng, ps[:, 1, 0:D], AGG, squared)

                @block.scalar
                def _(eng):
                    for k in range(NT // u):
                        at = slice(k * u, (k + 1) * u)
                        eng.wait_ge(dev, k + 1)
                        eng.activation(AGG[:, at, :], Y[:, at, :], ACT.Square).then_inc(squared, 1)
                    eng.wait_ge(var_ready, 1)
                    eng.activation(rstd_b[:, :], rstd_b[:, :], ACT.Sqrt).then_inc(var_ready, 1)

                @block.vector
                def _(eng):
                    c = Count(eng, chain)
                    wide = [P, u, D]
                    for k in range(NT // u):
                        at = slice(k * u, (k + 1) * u)
                        got[k].arrived(eng, u)
                        c.link(eng.tensor_tensor(AGG[:, at, :], C[:, at, 0:D], AGG[:, at, :], ALU.add))
                        eng.tensor_scalar(Y[:, at, :], AGG[:, at, :], 0.0, None, ALU.max).then_inc(made, 1)
                    eng.wait_ge(summed, 1)
                    c.link(eng.tensor_scalar(mean_b[:, :], ps[:, 0, 0:D], 1.0 / N, None, ALU.mult))
                    for k in range(NT // u):
                        at = slice(k * u, (k + 1) * u)
                        eng.tensor_tensor(Y[:, at, :], Y[:, at, :], mean_b[:, :].unsqueeze(1).broadcast_to(wide),
                                          ALU.subtract).then_inc(dev, 1)
                    eng.wait_ge(summed, 2)
                    c.link(eng.tensor_scalar(rstd_b[:, :], ps[:, 1, 0:D], 1.0 / N, EPS, ALU.mult, ALU.add))
                    eng.sem_inc(var_ready, 1)
                    eng.wait_ge(var_ready, 2)
                    c.link(eng.reciprocal(rstd_b[:, :], rstd_b[:, :]))
                    c.link(eng.tensor_tensor(rstd_b[:, :], rstd_b[:, :], GAM[:, layer, :], ALU.mult))
                    eng.wait_ge(squared, NT // u)
                    for k in range(NT // u):
                        at = slice(k * u, (k + 1) * u)
                        c.link(eng.tensor_tensor(Y[:, at, :], Y[:, at, :], rstd_b[:, :].unsqueeze(1).broadcast_to(wide), ALU.mult))
                        c.inc(eng.tensor_tensor(Y[:, at, :], Y[:, at, :], BET[:, layer, :].unsqueeze(1).broadcast_to(wide), ALU.add))
            for g in got:
                g.close(NODE_UNROLL)


        def stage_relu(src):
            def stage(eng, t, slot, chain, staged):
                eng.tensor_scalar(R[:, slot, :], tile_of(src, t), 0.0, None, ALU.max).then_inc(staged, 1)
            return stage

        def copy_to(dst):
            def out1(eng, t, slot, ps):
                return eng.activation(tile_of(dst, t), ps, ACT.Copy)
            return out1

        def flow_l0():
            out1, out2 = gcn_table(0, False)
            node_products("n0", stage_copy(X), GW[:, 0], out1, None, out2, table=(AGG, T))
            for l in range(LAYERS):
                edge_pass(f"e{l}", SRCI, (ALU.mult, ALU.add), nst_dst, True)
                if l < LAYERS - 1:
                    out1, out2 = gcn_table(l + 1, True)
                    node_products(f"n{l + 1}", stage_gcn(l), GW[:, l + 1], out1, MW[:, l], out2,
                                  gather=(PR, end_sum), table=(AGG, T))
                else:
                    def out1(eng, t, slot, ps):
                        return eng.activation(TMP[:, slot, :], ps, ACT.Copy)

                    def out2(eng, t, slot, ps, done):
                        eng.tensor_tensor(tile_of(X, t), TMP[:, slot, :], tile_of(X, t), ALU.add).then_inc(done, 1)
                    node_products("n3", stage_gcn(l), MW[:, l], out1, None, out2, gather=(PR, end_sum))
            layer_norm("ln0", add_bias)

        def flow_l1():
            def out2(eng, t, slot, ps, done):
                eng.tensor_tensor(tile_of(C[:, :, 0:D], t), ps[:, D:2 * D], B1[:, 0, :], ALU.add).then_inc(done, 1)
            node_products("n4", stage_copy(X), DF1, copy_to(AGG), TH1, out2, table=(AGG, T))
            edge_pass("e3", SRCI, (ALU.add, ALU.max), low_dst, False)
            layer_norm("ln1", edge_max, gather=(PR, end_max))

        CHK = ET // 4
        MASK3 = dram("attention_masks", [ET * HEADS, 3 * P], BF16)
        last_key = dram("last_key", [1, ET])
        (elbuf, erbuf, dstbuf, same, mask3, run_max, seg_max, er_seg, zed, lrelu, score, prob) = carve(
            YBASE, ((2, GT * HEADS), F32), ((4, GT * HEADS), F32), ((4, GT * P), F32), ((2, GT, P), F32), ((4, 3, P), BF16),
            ((P,), F32), ((2, P), F32), ((P,), F32), ((2, P), F32), ((2, P), F32), ((2, P), F32), ((2, P), F32))
        GH = GT * HEADS

        def attention_masks():
            wide = ARENA[0:CHK, 0:4 * HEADS * 3 * P // 2].bitcast(BF16).rearrange("p (c h k e) -> p c h k e", c=4, h=HEADS, k=3)
            rows = ARENA[0:CHK, 4 * HEADS * 3 * P // 2:4 * HEADS * 3 * P // 2 + 6 * P].bitcast(BF16)\
                .rearrange("p (k c e) -> p k c e", k=3, c=4)
            with Stage(nc, "am") as st:
                loaded, spread, stored = (st.sem(n) for n in ("loaded", "spread", "stored"))
                block = st.block()

                @block.sync
                def _(eng):
                    for k, (row, shift) in enumerate(((nst_dst, 0), (low_dst, 0), (low_dst, 1))):
                        eng.dma_start(rows[:, k], row[:, shift:shift + EP].rearrange("o (c p e) -> p (o c) e", c=4, e=P)).then_inc(loaded, 16)
                    eng.wait_ge(spread, 4)
                    for c in range(4):
                        eng.dma_start(MASK3[c * CHK * HEADS:(c + 1) * CHK * HEADS, :].rearrange("(p h) k -> p (h k)", h=HEADS),
                                      wide[:, c].rearrange("p h k e -> p (h k e)")).then_inc(stored, 16)
                    eng.wait_ge(stored, 64)

                @block.vector
                def _(eng):
                    eng.wait_ge(loaded, 48)
                    for c in range(4):
                        for k in range(3):
                            last_ = eng.tensor_copy(wide[:, c, :, k, :], rows[:, k, c, :].unsqueeze(1).broadcast_to([CHK, HEADS, P]))
                        last_.then_inc(spread, 1)

        tile_key = sb("tile_key", [CHK, 2, 4])
        tile_key_i = sb("tile_key_i", [CHK, 2, 4], I32)
        tile_er = sb("tile_er", [CHK, 2, 4, HEADS])

        def attention_er():
            with Stage(nc, "er") as st:
                loaded, cast, stored = (st.sem(n) for n in ("loaded", "cast", "stored"))
                placed, got = gathered[0:2]
                block = st.block()

                @block.sync
                def _(eng):
                    with nc.allow_non_contiguous_dma("one element a tile"):
                        for s, e in ((0, 0), (1, P - 1)):
                            eng.dma_start(tile_key[:, s, :], dst_row.rearrange("o (c p e) -> p (o c) e", c=4, e=P)[:, :, e]).then_inc(loaded, 16)
                        eng.wait_ge(cast, 1)
                        eng.dma_start(last_key.rearrange("o (c p) -> p (o c)", c=4), tile_key[:, 1, :]).then_inc(stored, 16)
                    placed.arrived(eng, NT)
                    got.arrived(eng, 8)
                    eng.dma_start(ERE.rearrange("(c p e) h -> p c e h", c=4, e=P)[:, :, 0, :], tile_er[:, 0]).then_inc(stored, 16)
                    eng.wait_ge(stored, 32)

                @block.vector
                def _(eng):
                    eng.wait_ge(loaded, 32)
                    eng.tensor_copy(tile_key_i[:, :, :], tile_key[:, :, :]).then_inc(cast, 1)

                @block.gpsimd
                def _(eng):
                    for t in range(NT):
                        eng.indirect_dma_start(ERE, bass.IndirectOffsetOnAxis(ap=first_dst[:, t:t + 1], axis=0),
                                               C[:, t, D + HEADS:RW], None, bounds_check=EP - 1, oob_is_err=False).then_inc(placed.sem, 16)
                    eng.wait_ge(cast, 1)
                    for s in range(2):
                        for c in range(4):
                            eng.indirect_dma_start(tile_er[:, s, c, :], None, ERT,
                                                   bass.IndirectOffsetOnAxis(ap=tile_key_i[:, s, c:c + 1], axis=0)).then_inc(got.sem, 16)
            placed.close(NT)
            got.close(8)


        def attention_pass():
            SL = slice(0, GH)
            with Stage(nc, "att") as st:
                got = gathered[0:4]
                ready = [st.sem(f"ready{q}") for q in range(4)]
                names = ("turned", "scored", "chain", "expd", "spread", "masked", "made", "moved", "o_free", "stored", "go_pool", "go_sp", "packed", "go_pe")
                turned, scored, chain, expd, spread, masked, made, moved, o_free, stored, go_pool, go_sp, packed, go_pe = (st.sem(n) for n in names)
                ta = st.stack.enter_context(nc.psum_tensor("att_a", [P, 2, 512], F32))
                tb = st.stack.enter_context(nc.psum_tensor("att_b", [P, 2, 512], F32))
                po = st.stack.enter_context(nc.psum_tensor("att_o", [P, GT, 512], F32))
                out_rows = PA[0:EP, :].rearrange("(t p) d -> p t d", p=P)
                er_rows = ERE.rearrange("(t p) h -> p t h", p=P)
                block = st.block()

                @block.sync
                def _(eng):
                    def prefetch(g, q):
                        eng.dma_start(idxbuf[:, q, :], SRCI[:, ds(g * GT, GT)]).then_inc(ready[q], 16)
                        eng.dma_start(dstbuf[:, q, :], dst_row[0:1, ds(g * (GT * P), GT * P)].broadcast_to([P, GT * P])).then_inc(ready[q], 16)
                        eng.dma_start(erbuf[:, q, :].rearrange("p (t h) -> p t h", h=HEADS), er_rows[:, ds(g * GT, GT), :]).then_inc(ready[q], 16)
                        eng.dma_start(mask3[SL, q].rearrange("p k e -> p (k e)"), MASK3[ds(g * GH, GH), :]).then_inc(ready[q], 16)

                    for q in range(4):
                        prefetch(q, q)

                    def store(g, q, _):
                        eng.wait_ge(moved, g * 4 + 8)
                        eng.sem_inc(go_sp, 1)
                        eng.dma_start(out_rows[:, ds(g * GT, GT), :], O[:, q % 2, :, :]).then_inc(stored, 16)
                        if not isinstance(g, int) or g + 4 < NG:
                            prefetch(g + 4, q)
                        eng.wait_ge(stored, g * 16 + 16)
                        eng.sem_inc(o_free, 1)

                    with eng.Fori(0, (NG - 4) // 4) as i:
                        for q in range(4):
                            store(i * 4 + q, q, i)
                    for g in range((NG - 4) // 4 * 4, NG):
                        store(g, g % 4, 0)

                @block.gpsimd
                def _(eng):
                    def gather(g, q, turn):
                        eng.wait_ge(ready[q], turn * 64 + 64)
                        eng.sem_inc(go_pool, 1)
                        for k in range(GT):
                            eng.indirect_dma_start(G[:, q * GT + k, :], None, T2,
                                                   bass.IndirectOffsetOnAxis(ap=idxbuf[:, q, k:k + 1], axis=0)).then_inc(got[q].sem, 16)

                    pipelined(NG, 4, eng, (gather, 0))

                @block.tensor
                def _(eng):
                    eng.sem_inc(made, 8)
                    eng.sem_inc(turned, 2)

                    def turn_el(g, q, turn):
                        eng.wait_ge(packed, g + 1)
                        eng.wait_ge(scored, g + 1)
                        eng.transpose(ta[SL, q % 2, 0:P], elbuf[:, q % 2, :], ident[:, :])
                        eng.transpose(ta[SL, q % 2, P:2 * P], erbuf[:, q, :], ident[:, :]).then_inc(turned, 1)

                    def turn_p(g, q, turn):
                        eng.wait_ge(expd, g + 1)
                        eng.wait_ge(masked, g + 1)
                        eng.sem_inc(go_pe, 1)
                        eng.transpose(tb[:, q % 2, 0:GH], prob[SL, q % 2, :], ident[SL, SL])
                        eng.transpose(tb[:, q % 2, GH:2 * GH], seg_max[SL, q % 2, :], ident[SL, SL]).then_inc(spread, 1)

                    def product(g, q, turn):
                        eng.wait_ge(masked, g + 3)
                        for k in range(GT):
                            eng.wait_ge(moved, g * 4 + (k + 1))
                            eng.matmul(po[:, k, 0:TW], same[:, q % 2, k, :], G[:, q * GT + k, :], start=True, stop=True).then_inc(made, 1)

                    pipelined(NG, 4, eng, (turn_el, 2), (turn_p, 1), (product, 0))

                @block.vector
                def _(eng):
                    eng.sem_inc(scored, 2)
                    eng.sem_inc(masked, 2)

                    def score_step(g, q, turn):
                        b = q % 2
                        rev = slice(None, None, -1)
                        eng.wait_ge(turned, g + 3)
                        eng.tensor_tensor_scan(run_max[SL, :], mask3[SL, q, 1, :], ta[SL, b, 0:P], LOW, ALU.add, ALU.max).then_inc(chain, 1)
                        eng.tensor_tensor_scan(er_seg[SL, :], mask3[SL, q, 0, :], ta[SL, b, P:2 * P], 0.0, ALU.mult, ALU.add).then_inc(chain, 1)
                        eng.wait_ge(chain, g * 6 + 2)
                        eng.tensor_tensor(zed[SL, 0, :], ta[SL, b, 0:P], er_seg[SL, :], ALU.add).then_inc(chain, 1)
                        eng.wait_ge(spread, g + 1)
                        eng.tensor_tensor_scan(seg_max[SL, b, rev], mask3[SL, q, 2, rev], run_max[SL, rev], LOW, ALU.add, ALU.max).then_inc(chain, 1)
                        eng.wait_ge(chain, g * 6 + 4)
                        eng.tensor_tensor(zed[SL, 1, :], seg_max[SL, b, :], er_seg[SL, :], ALU.add).then_inc(chain, 1)
                        eng.wait_ge(chain, g * 6 + 5)
                        eng.scalar_tensor_tensor(lrelu[SL, :, :], zed[SL, :, :], 0.2, zed[SL, :, :], ALU.mult, ALU.max).then_inc(chain, 1)
                        eng.wait_ge(chain, g * 6 + 6)
                        eng.tensor_tensor(score[SL, b, :], lrelu[SL, 0, :], lrelu[SL, 1, :], ALU.subtract).then_inc(scored, 1)

                    def weight_step(g, q, turn):
                        b = q % 2
                        eng.wait_ge(spread, g + 3)
                        eng.wait_ge(made, g * 4 + 4)
                        eng.wait_ge(o_free, g + 1)
                        p = tb[:, b, 0:GH].rearrange("p (t h) -> p t h", h=HEADS)
                        rows = G[:, q * GT:(q + 1) * GT, :]
                        eng.tensor_tensor(rows[:, :, 0:D].rearrange("p t (h c) -> p t h c", h=HEADS),
                                          rows[:, :, 0:D].rearrange("p t (h c) -> p t h c", h=HEADS),
                                          p.unsqueeze(3).broadcast_to([P, GT, HEADS, D // HEADS]), ALU.mult)
                        eng.tensor_copy(rows[:, :, D:TW], p)
                        eng.tensor_copy(O[:, b, :, TW:RW], tb[:, b, GH:2 * GH].rearrange("p (t h) -> p t h", h=HEADS))
                        for k in range(GT):
                            last_ = eng.scalar_tensor_tensor(same[:, b, k, :], dstbuf[:, q, k * P:(k + 1) * P],
                                                             DSTF[:, ds(g * GT + k, 1)], upto[:, :], ALU.is_equal, ALU.mult)
                        last_.then_inc(masked, 1)

                    pipelined(NG, 4, eng, (score_step, 1), (weight_step, 0))

                @block.scalar
                def _(eng):
                    eng.sem_inc(moved, 4)
                    eng.sem_inc(o_free, 2)
                    eng.sem_inc(spread, 2)

                    def pack(g, q, turn):
                        got[q].arrived(eng, turn * GT + GT)
                        eng.wait_ge(turned, g + 1)
                        eng.activation(elbuf[:, q % 2, :].rearrange("p (t h) -> p t h", h=HEADS),
                                       G[:, q * GT:(q + 1) * GT, D:TW], ACT.Copy).then_inc(packed, 1)

                    def exp_step(g, q, turn):
                        eng.wait_ge(scored, g + 3)
                        eng.activation(prob[SL, q % 2, :], score[SL, q % 2, :], ACT.Exp).then_inc(expd, 1)

                    def move(g, q, turn):
                        eng.wait_ge(o_free, g + 1)
                        for k in range(GT):
                            eng.wait_ge(made, g * 4 + (k + 9))
                            eng.activation(O[:, q % 2, k, 0:TW], po[:, k, 0:TW], ACT.Copy).then_inc(moved, 1)

                    pipelined(NG, 4, eng, (pack, 2), (exp_step, 1), (move, 0))
            for q in range(4):
                got[q].close(GT * ((NG - q + 3) // 4))


        def attention_carry():
            at = [0]
            rows, key_all, same_t, prod_t, s8, res = carve(
                YBASE, ((4, RW), F32), ((ET,), F32), ((10, CHK), F32), ((2, 4, HEADS), F32), ((3, ET + 2), F32), ((4, RW), F32))
            z4 = sb("z4", [CHK, 4, 4, HEADS])
            H8 = slice(0, HEADS)
            CS = slice(0, CHK)
            rev = slice(None, None, -1)
            pairs = [(a_, c_) for c_ in range(4) for a_ in range(c_ + 1)]
            with Stage(nc, "car") as st:
                names = ("loaded", "chain", "turned", "back", "expd", "weighted", "made", "moved", "stored", "maxed", "scored")
                loaded, chain, turned, back, expd, weighted, made, moved, stored, maxed, scored = (st.sem(n) for n in names)
                t8 = st.stack.enter_context(nc.psum_tensor("car_8", [P, 512], F32))
                tk = st.stack.enter_context(nc.psum_tensor("car_k", [P, 512], F32))
                po = st.stack.enter_context(nc.psum_tensor("car_o", [P, 4, 512], F32))
                block = st.block()

                @block.sync
                def _(eng):
                    eng.dma_start(rows[CS], PA[0:EP, :].rearrange("(c p e) d -> p c e d", c=4, e=P)[:, :, P - 1, :]).then_inc(loaded, 16)
                    eng.dma_start(key_all[CS, :], last_key.broadcast_to([CHK, ET])).then_inc(loaded, 16)
                    eng.wait_ge(moved, 5)
                    eng.dma_start(CR[0:ET, :].rearrange("(c p) d -> p c d", c=4), res[CS]).then_inc(stored, 16)
                    eng.wait_ge(stored, 16)

                @block.tensor
                def _(eng):
                    eng.wait_ge(loaded, 32)
                    for c in range(4):
                        last_ = eng.transpose(t8[H8, c * CHK:(c + 1) * CHK], rows[CS, c, TW:RW], ident[CS, CS])
                    last_.then_inc(turned, 1)
                    eng.wait_ge(maxed, 1)
                    for c in range(4):
                        last_ = eng.transpose(tk[CS, c * HEADS:(c + 1) * HEADS], s8[H8, 2, c * CHK:(c + 1) * CHK], ident[H8, H8])
                    last_.then_inc(back, 1)
                    eng.wait_ge(weighted, 1)
                    for n, (a_, c_) in enumerate(pairs):
                        last_ = eng.matmul(po[CS, c_, 0:TW], same_t[CS, n, :], rows[CS, a_, 0:TW], start=a_ == 0, stop=a_ == c_)
                    last_.then_inc(made, 1)

                @block.scalar
                def _(eng):
                    eng.wait_ge(scored, 1)
                    eng.activation(prod_t[CS, 0], z4[:, 2], ACT.Exp).then_inc(expd, 1)
                    eng.wait_ge(made, 1)
                    for c in range(4):
                        eng.activation(res[CS, c, 0:TW], po[CS, c, 0:TW], ACT.Copy).then_inc(moved, 1)

                @block.vector
                def _(eng):
                    c = Count(eng, chain)
                    eng.wait_ge(loaded, 32)
                    c.link(eng.tensor_tensor(s8[H8, 0, 1:ET], key_all[H8, 1:ET], key_all[H8, 0:ET - 1], ALU.not_equal))
                    c.link(eng.tensor_scalar(s8[H8, 0, 1:ET], s8[H8, 0, 1:ET], LOW, None, ALU.mult))
                    c.inc(eng.memset(s8[H8, 0, 0:1], LOW))
                    c.inc(eng.memset(s8[H8, 0, ET:ET + 2], LOW))
                    for n, (a_, c_) in enumerate(pairs):
                        there = key_all[CS, c_ * CHK:(c_ + 1) * CHK]
                        c.inc(eng.scalar_tensor_tensor(same_t[CS, n, :], there, tile_key[:, 1, a_:a_ + 1],
                                                       upto[CS, CS] if a_ == c_ else ones[CS, CS], ALU.is_equal, ALU.mult))
                    c.wait()
                    eng.wait_ge(turned, 1)
                    c.link(eng.tensor_tensor_scan(s8[H8, 1, 0:ET], s8[H8, 0, 0:ET], t8[H8, 0:ET], LOW, ALU.add, ALU.max))
                    c.link(eng.tensor_tensor_scan(s8[H8, 2, 0:ET][:, rev],
                                                  s8[H8, 0, 1:ET + 1][:, rev], s8[H8, 1, 0:ET][:, rev], LOW, ALU.add, ALU.max))
                    eng.sem_inc(maxed, 1)
                    eng.wait_ge(back, 1)
                    mk = tk[CS, 0:4 * HEADS].rearrange("p (c h) -> p c h", h=HEADS)
                    eng.tensor_copy(res[CS, :, TW:RW], mk).then_inc(moved, 1)
                    er = tile_er[:, 1]
                    c.inc(eng.tensor_tensor(z4[:, 0], rows[CS, :, TW:RW], er, ALU.add))
                    c.link(eng.tensor_tensor(z4[:, 1], mk, er, ALU.add))
                    c.link(eng.scalar_tensor_tensor(z4[:, 2:4], z4[:, 0:2], 0.2, z4[:, 0:2], ALU.mult, ALU.max))
                    c.link(eng.tensor_tensor(z4[:, 2], z4[:, 2], z4[:, 3], ALU.subtract))
                    eng.sem_inc(scored, 1)
                    eng.wait_ge(expd, 1)
                    w = prod_t[CS, 0]
                    c.inc(eng.tensor_tensor(rows[CS, :, 0:D].rearrange("p c (h d) -> p c h d", h=HEADS),
                                            rows[CS, :, 0:D].rearrange("p c (h d) -> p c h d", h=HEADS),
                                            w.unsqueeze(3).broadcast_to([CHK, 4, HEADS, D // HEADS]), ALU.mult))
                    c.inc(eng.tensor_tensor(rows[CS, :, D:TW], rows[CS, :, D:TW], w, ALU.mult))
                    c.wait()
                    eng.sem_inc(weighted, 1)

        def attention_combine():
            with Stage(nc, "comb") as st:
                chain, expd, scored = (st.sem(n) for n in ("chain", "expd", "scored"))
                got = gathered[0]
                m4, z_, l_, e_, den = carve(WORK, ((4, NT, HEADS), F32), ((4, NT, HEADS), F32), ((4, NT, HEADS), F32),
                                            ((4, NT, HEADS), F32), ((2, NT, HEADS), F32))
                block = st.block()

                @block.gpsimd
                def _(eng):
                    for t in range(NT):
                        eng.indirect_dma_start(YW[:, t, :], None, PA, bass.IndirectOffsetOnAxis(ap=end_sum[:, t:t + 1], axis=0)).then_inc(got.sem, 16)
                        eng.indirect_dma_start(AGW[:, t, :], None, CR, bass.IndirectOffsetOnAxis(ap=carry_row[:, t:t + 1], axis=0)).then_inc(got.sem, 16)

                @block.scalar
                def _(eng):
                    eng.wait_ge(scored, 1)
                    eng.activation(e_[:, 0:3], z_[:, 0:3], ACT.Exp).then_inc(expd, 1)

                @block.vector
                def _(eng):
                    c = Count(eng, chain)
                    er = C[:, :, TW:RW]
                    got.arrived(eng, 2 * NT)
                    c.inc(eng.tensor_copy(m4[:, 0], YW[:, :, TW:RW]))
                    c.inc(eng.tensor_copy(m4[:, 1], AGW[:, :, TW:RW]))
                    c.link(eng.tensor_copy(m4[:, 2], C[:, :, D:TW]))
                    c.link(eng.tensor_tensor(m4[:, 3], m4[:, 0], m4[:, 1], ALU.max))
                    c.link(eng.tensor_tensor(m4[:, 3], m4[:, 3], m4[:, 2], ALU.max))
                    for k in range(4):
                        c.inc(eng.tensor_tensor(z_[:, k], m4[:, k], er, ALU.add))
                    c.wait()
                    c.link(eng.scalar_tensor_tensor(l_[:, :], z_[:, :], 0.2, z_[:, :], ALU.mult, ALU.max))
                    for k in range(3):
                        c.inc(eng.tensor_tensor(z_[:, k], l_[:, k], l_[:, 3], ALU.subtract))
                    c.wait()
                    eng.sem_inc(scored, 1)
                    eng.wait_ge(expd, 1)
                    c.inc(eng.tensor_tensor(l_[:, 0], e_[:, 0], YW[:, :, D:TW], ALU.mult))
                    c.link(eng.tensor_tensor(l_[:, 1], e_[:, 1], AGW[:, :, D:TW], ALU.mult))
                    c.link(eng.tensor_tensor(den[:, 0], l_[:, 0], l_[:, 1], ALU.add))
                    c.link(eng.tensor_tensor(den[:, 0], den[:, 0], e_[:, 2], ALU.add))
                    c.link(eng.tensor_scalar(den[:, 0], den[:, 0], 1e-16, None, ALU.add))
                    c.link(eng.reciprocal(den[:, 1], den[:, 0]))
                    for k in range(3):
                        c.inc(eng.tensor_tensor(e_[:, k], e_[:, k], den[:, 1], ALU.mult))
                    c.wait()
                    for k, part in enumerate((YW, AGW, C)):
                        v = part[:, :, 0:D].rearrange("p t (h d) -> p t h d", h=HEADS)
                        c.link(eng.tensor_tensor(v, v, e_[:, k].unsqueeze(3).broadcast_to([P, NT, HEADS, D // HEADS]), ALU.mult))
                        c.link(eng.tensor_tensor(X[:, :, :], X[:, :, :], part[:, :, 0:D], ALU.add))
            got.close(2 * NT)


        def flow_l2():
            def out2(eng, t, slot, ps, done):
                eng.tensor_copy(tile_of(C[:, :, D:RW], t), ps[:, D:D + 2 * HEADS]).then_inc(done, 1)
            node_products("n5", stage_copy(X), W2, copy_to(C[:, :, 0:D]), WA, out2, table=(C[:, :, 0:TW], T2), table2=(C[:, :, TW:RW], ERT))
            attention_er()
            attention_pass()
            attention_carry()
            attention_combine()
            layer_norm("ln2", none)

        def flow_l3():
            for l in range(LAYERS):
                def out2(eng, t, slot, ps, done):
                    eng.tensor_copy(tile_of(C[:, :, 0:D], t), ps[:, D:2 * D]).then_inc(done, 1)
                node_products(f"n{6 + l}", stage_copy(X) if l == 0 else stage_relu(Y), TH3[:, l], copy_to(AGG),
                              DF3[:, l], out2, table=(AGG, T))
                edge_pass(f"e{5 + l}", BYSRC, (ALU.add, ALU.max), low_src, False)
                batch_norm(f"bn{l}", l, gather=(PR, end_src))
            layer_norm("ln3", last, out_rows=out)

        build_flow = dict(locals())
        run(build_flow)


def run(f):
    f["constants"]()
    f["weights"]()
    f["edge_columns"]()
    f["histogram"](0, f["DSTF"])
    f["histogram"](1, f["SRCF"])
    if STOP > 0:
        f["sort_places"]()
        f["sort_edges"]()
        f["node_indices"]()
    if STOP > 1:
        f["flow_l0"]()
    if STOP > 2:
        f["flow_l1"]()
    if STOP > 3:
        f["attention_masks"]()
        f["flow_l2"]()
    if STOP > 4:
        f["flow_l3"]()


STOP = 9


INPUTS = ["x", "src", "dst", "edge_weight",
          "L0_gnn_fc_w", "L0_gnn_fc_b", "L0_gnn_ch_w", "L0_gnn_ch_b", "L0_gnn_mlp_w", "L0_gnn_mlp_b",
          "L1_gnn_theta_w", "L1_gnn_theta_b", "L1_gnn_phi_w", "L1_gnn_phi_b",
          "L2_gnn_W", "L2_gnn_a_left", "L2_gnn_a_right",
          "L3_gnn_thetas", "L3_gnn_phis", "L3_gnn_gammas", "L3_gnn_betas"]


def kernel(**inputs):
    import numpy as np
    import concourse.bacc as bacc
    from concourse.bass_utils import run_bass_kernel_spmd

    nc = bacc.Bacc("TRN2", target_bir_lowering=False, num_devices=1)
    arrays, a = {}, {}
    for name in INPUTS:
        v = np.ascontiguousarray(inputs[name])
        arrays[f"in_{name}"] = v
        a[name] = nc.dram_tensor(f"in_{name}", v.shape, mybir.dt.from_np(v.dtype), kind="ExternalInput").ap()
    out = nc.dram_tensor("out_0", (N, D), F32, kind="ExternalOutput").ap()
    build(nc, a, out)
    r = run_bass_kernel_spmd(nc, [arrays], core_ids=[0])
    return r.results[0]["out_0"]
```

```python
import concourse.bass as bass
from concourse import mybir
from contextlib import ExitStack, contextmanager

F32 = mybir.dt.float32
BF16 = mybir.dt.bfloat16
F16 = mybir.dt.float16
I32 = mybir.dt.int32
ALU = mybir.AluOpType
ACT = mybir.ActivationFunctionType
AX = mybir.AxisListType
ds = bass.ds

P = 128
N = 3125
E = 50000
D = 256
NT = (N + P - 1) // P
NP = NT * P
LAST = N - (NT - 1) * P
GT = 4
NG = -(-E // (P * GT))
SETS = 6
ET = NG * GT
EP = ET * P
ROW_ZERO = EP
ROW_LOW = EP + 1
LOW = -1e38
HEADS = 8
TW = D + HEADS
RW = D + 2 * HEADS
LO = 32
HI = -(-(N + 1) // LO)
LAYERS = 3
NODE_UNROLL = 5
EPS = 1e-5
OOB = 60000.0


class Count:

    def __init__(self, eng, sem):
        self.eng, self.sem, self.n, self.turn, self.per, self.at = eng, sem, 0, 0, 0, 0

    def inc(self, ins):
        self.n += 1
        ins.then_inc(self.sem, 1)
        return ins

    def value(self):
        return self.turn * self.per + self.n if self.per else self.n

    def wait(self):
        self.eng.wait_ge(self.sem, self.value())

    def link(self, ins):
        self.inc(ins)
        self.wait()

    @contextmanager
    def loop(self, turns, per):
        start = self.n
        with self.eng.Fori(0, turns) as i:
            self.turn, self.per = i, per
            yield i
            assert self.n - start == per, (self.n, start, per)
        self.turn, self.per, self.n = 0, 0, start + turns * per


def pipelined(total, unroll, eng, *steps):
    most = max(lead for _, lead in steps)
    turns = (total - max(most, 3)) // unroll

    def straight(s):
        for fn, lead in steps:
            if 0 <= s + lead < total:
                fn(s + lead, (s + lead) % unroll, (s + lead) // unroll)

    for s in range(-most, 0):
        straight(s)
    with eng.Fori(0, turns) as i:
        for j in range(unroll):
            for fn, lead in steps:
                fn(i * unroll + (j + lead), (j + lead) % unroll, i + (j + lead) // unroll)
    for s in range(turns * unroll, total):
        straight(s)


class Gathered:

    def __init__(self, sem):
        self.sem, self.before = sem, 0

    def arrived(self, eng, dmas):
        eng.wait_ge(self.sem, dmas * 16 + self.before)

    def close(self, dmas):
        self.before += 16 * dmas


class Stage:

    used = []
    def __init__(self, nc, name):
        self.nc, self.name, self.stack, self.sems = nc, name, ExitStack(), []

    def sem(self, name):
        self.sems.append(self.stack.enter_context(self.nc.semaphore(f"{self.name}_{name}")))
        return self.sems[-1]

    def __enter__(self):
        return self

    def block(self):
        block = self.stack.enter_context(self.nc.Block())
        before, Stage.used = Stage.used, sorted(s.num for s in self.sems)
        assert not set(before) & set(Stage.used)

        @block.gpsimd
        def _(eng):
            while before:
                n = 1
                while n < len(before) and before[n] == before[0] + n:
                    n += 1
                eng.sem_clear(range(before[0], before[0] + n))
                del before[:n]

        return block

    def __exit__(self, *a):
        return self.stack.__exit__(*a)


def build(nc, a, out):
    top = ExitStack()
    Stage.used = []
    with top:
        gathered = [Gathered(top.enter_context(nc.semaphore(f"gathered_{k}"))) for k in range(SETS)]
        def sb(name, shape, dt=F32):
            return top.enter_context(nc.sbuf_tensor(name, shape, dt))

        def dram(name, shape, dt=F32):
            return nc.dram_tensor(name, shape, dt).ap()

        def carve(base, *wanted):
            at, made = 0, []
            for shape, dt in wanted:
                n = 1
                for k in shape:
                    n *= k
                words = n if dt in (F32, I32) else -(-n // 2)
                v = base[:, at:at + words]
                if dt != F32:
                    v = v.bitcast(dt)
                names = "abcd"[:len(shape)]
                if len(shape) > 1:
                    v = v.rearrange(f"p ({' '.join(names)}) -> p {' '.join(names)}", **dict(zip(names, shape)))
                made.append(v)
                at += words
            assert at <= base.shape[1], (at, base.shape)
            return made

        X = sb("X", [P, NT, D])
        ARENA = sb("ARENA", [P, NT * 3 * RW])
        AGW_BASE = ARENA[:, 0:NT * RW]
        AGW = AGW_BASE.rearrange("p (t d) -> p t d", d=RW)
        AGG = AGW[:, :, 0:D]
        C = ARENA[:, NT * RW:NT * 2 * RW].rearrange("p (t d) -> p t d", d=RW)
        YBASE = ARENA[:, NT * 2 * RW:NT * 3 * RW]
        YW = YBASE[:, :].rearrange("p (t d) -> p t d", d=RW)
        Y = YW[:, :, 0:D]
        WORK = sb("WORK", [P, SETS * GT * TW + 4 * GT * P + 2 * GT * RW])
        G, S, O = carve(WORK, ((SETS * GT, TW), F32), ((2, 2, GT * P), F32), ((2, GT, RW), F32))
        SBASE = WORK[:, SETS * GT * TW:SETS * GT * TW + 4 * GT * P]
        R, XT, TMP, TMP2 = carve(WORK, *[((NODE_UNROLL, D), F32)] * 4)
        HB = 14
        RB = GT
        HIST, key_hi, key_lo = carve(ARENA[:, NT * RW:NT * 3 * RW], ((ET, LO), F32), ((ET,), F32), ((ET,), F32))
        oh_hi, oh_lo, = carve(AGW_BASE, ((2, HB, HI), BF16), ((2, HB, LO), BF16))
        rank_hi, rank_lo, rank_t, rank_tf, rank_tmp, sel, rank = carve(
            AGW_BASE, ((2, RB, HI), BF16), ((2, RB, LO), BF16), ((2, 2, RB * P), BF16), ((2, RB * P), F32),
            ((RB, P), BF16), ((RB, LO), F32), ((2, RB), F32))
        place_hi, place_lo, pay_hi, pay_lo, oh_place, oh_pay, no_places, digit_tmp = carve(
            YBASE, *[((ET,), F32)] * 4, ((2, GT, ET), BF16), ((2, GT, 2, P), BF16), ((P + ET,), BF16), ((3, ET), I32))
        key_tmp, iota_i, SRCF = carve(WORK, ((3, ET), I32), ((ET,), I32), ((ET,), F32))
        idxbuf = sb("idxbuf", [P, SETS, GT], I32)
        wbuf = sb("wbuf", [P, SETS, GT])
        maskbuf = sb("maskbuf", [P, SETS, GT * P], BF16)
        ident = sb("ident", [P, P])
        identb = sb("identb", [P, P], BF16)
        ones = sb("ones", [P, P])
        before = sb("before", [P, P])
        upto = sb("upto", [P, P])
        iota_b = sb("iota_b", [P, P], BF16)
        iota_h = sb("iota_h", [P, ET], F16)
        GW = sb("GW", [P, LAYERS, 2, D])
        GB = sb("GB", [P, LAYERS, D])
        MW = sb("MW", [P, LAYERS, 2, D])
        TH1, DF1, W2 = sb("TH1", [P, 2, D]), sb("DF1", [P, 2, D]), sb("W2", [P, 2, D])
        WA = sb("WA", [P, 2, 2 * HEADS])
        TH3, DF3 = sb("TH3", [P, LAYERS, 2, D]), sb("DF3", [P, LAYERS, 2, D])
        CHB, MB = sb("CHB", [P, LAYERS, D]), sb("MB", [P, D])
        B1 = sb("B1", [P, D])
        GAM, BET = sb("GAM", [P, LAYERS, D]), sb("BET", [P, LAYERS, D])
        DSTF, WE = sb("DSTF", [P, ET]), sb("WE", [P, ET])
        SRCI, BYSRC = sb("SRCI", [P, ET], I32), sb("BYSRC", [P, ET], I32)
        pos = BYSRC[:, :].bitcast(F32)
        norm_out, norm_in = sb("norm_out", [P, NT]), sb("norm_in", [P, NT])
        end_sum, end_max, end_src = (sb(n, [P, NT], I32) for n in ("end_sum", "end_max", "end_src"))
        first_dst, first_src = sb("first_dst", [P, NT], I32), sb("first_src", [P, NT], I32)
        carry_row = sb("carry_row", [P, NT], I32)
        MV = sb("MV", [P, NT, 2])

        T = dram("table", [NP, D])
        T2 = dram("table_attention", [NP, TW])
        PR = dram("edge_results", [EP + 2, D])
        PA = dram("edge_results_attention", [EP + 1, RW])
        CR = dram("carry_rows", [ET + 1, RW])
        ERT = dram("er_table", [NP, HEADS])
        ERE = dram("er_edges", [EP, HEADS])
        nst_dst = dram("nst_dst", [1, EP + P], BF16)
        low_dst = dram("low_dst", [1, EP + P], BF16)
        low_src = dram("low_src", [1, EP + P], BF16)
        dst_row = dram("dst_row", [1, EP])
        flag_dst, flag_src = dram("flag_dst", [EP, 1]), dram("flag_src", [EP, 1])
        hist_start, hist_count = dram("hist_start", [2, NP]), dram("hist_count", [2, NP])

        def constants():
            with Stage(nc, "cst") as st:
                zeroed, filled, done = st.sem("zeroed"), st.sem("filled"), st.sem("done")
                copied = st.sem("copied")
                block = st.block()

                @block.gpsimd
                def _(eng):
                    eng.memset(ident[:, :], 0.0).then_inc(zeroed, 1)
                    eng.memset(ones[:, :], 1.0).then_inc(zeroed, 1)
                    eng.iota(iota_i[:, :], pattern=[[1, ET]], base=0, channel_multiplier=0).then_inc(zeroed, 1)
                    eng.wait_ge(zeroed, 3)
                    eng.affine_select(out=ident[:, :], in_=ident[:, :], compare_op=ALU.not_equal, fill=1.0,
                                      base=0, pattern=[[-1, P]], channel_multiplier=1).then_inc(filled, 1)
                    eng.affine_select(out=before[:, :], in_=ones[:, :], compare_op=ALU.is_gt, fill=0.0,
                                      base=0, pattern=[[1, P]], channel_multiplier=-1).then_inc(filled, 1)
                    eng.affine_select(out=upto[:, :], in_=ones[:, :], compare_op=ALU.is_ge, fill=0.0,
                                      base=0, pattern=[[1, P]], channel_multiplier=-1).then_inc(filled, 1)

                @block.vector
                def _(eng):
                    eng.wait_ge(filled, 3)
                    eng.tensor_copy(identb[:, :], ident[:, :]).then_inc(copied, 1)
                    eng.tensor_copy(iota_b[:, :], iota_i[:, 0:P]).then_inc(copied, 1)
                    eng.tensor_copy(iota_h[:, :], iota_i[:, :]).then_inc(copied, 1)

        def weights():
            at = [0]

            def area(*shape):
                n = 1
                for s in shape:
                    n *= s
                v = ARENA[:, at[0]:at[0] + n]
                at[0] += n
                names = "abc"[:len(shape)]
                if len(shape) == 1:
                    return v
                return v.rearrange(f"p ({' '.join(names)}) -> p {' '.join(names)}",
                                   **{k: s for k, s in zip(names[1:], shape[1:])})

            fc, ch = area(LAYERS * 2, D), area(LAYERS * 2, D)
            mlp = area(2, LAYERS * D)
            th1, ph1, w2 = area(2, D), area(2, D), area(2, D)
            th3, ph3 = area(LAYERS * 2, D), area(LAYERS * 2, D)
            fcb = area(LAYERS * 2)
            fcb_wide = area(LAYERS * 2, P)
            prod = area(2, 2, D)
            AV, B1b = area(2, D), area(D)
            turns = [(lambda m, k, l=l: mlp[:, m, l * D + k * P:l * D + k * P + P], MW[:, l]) for l in range(LAYERS)]
            turns += [(lambda m, k: th1[:, m, k * P:k * P + P], TH1[:, :, :]),
                      (lambda m, k: ph1[:, m, k * P:k * P + P], DF1[:, :, :]),
                      (lambda m, k: w2[:, m, k * P:k * P + P], W2[:, :, :])]
            turns += [(lambda m, k, l=l: th3[:, 2 * l + m, k * P:k * P + P], TH3[:, l]) for l in range(LAYERS)]
            turns += [(lambda m, k, l=l: ph3[:, 2 * l + m, k * P:k * P + P], DF3[:, l]) for l in range(LAYERS)]
            banks = len(turns) + 2 * LAYERS
            with Stage(nc, "w") as st:
                loaded, zeroed, ready = st.sem("loaded"), st.sem("zeroed"), st.sem("ready")
                made, moved, chain = st.sem("made"), st.sem("moved"), st.sem("chain")
                ps = st.stack.enter_context(nc.psum_tensor("w_ps", [P, 4, 512], F32))
                block = st.block()

                @block.sync
                def _(eng):
                    n = 0

                    def load(dst, src):
                        nonlocal n
                        eng.dma_start(dst, src).then_inc(loaded, 16)
                        n += 16

                    load(X[:, 0:NT - 1, :], a["x"][0:(NT - 1) * P, :].rearrange("(t p) d -> p t d", p=P))
                    eng.wait_ge(zeroed, 2)
                    load(X[0:LAST, NT - 1, :], a["x"][(NT - 1) * P:N, :])
                    load(fc, a["L0_gnn_fc_w"].rearrange("l (k p) i -> p (l k) i", p=P))
                    for c in range(4):
                        for l in range(LAYERS):
                            load(ch[64 * (c % 2):64 * (c % 2) + 64, 2 * l + c // 2, 64 * c:64 * c + 64],
                                 a["L0_gnn_ch_w"][l, c])
                    load(mlp, a["L0_gnn_mlp_w"].rearrange("(m p) i -> p m i", p=P))
                    with nc.allow_non_contiguous_dma("a bias across the partitions"):
                        load(fcb, a["L0_gnn_fc_b"].rearrange("l (k p) -> p (l k)", p=P))
                    for dst, name in ((th1, "L1_gnn_theta_w"), (ph1, "L1_gnn_phi_w"), (w2, "L2_gnn_W")):
                        load(dst, a[name].rearrange("(m p) i -> p m i", p=P))
                    for dst, name in ((th3, "L3_gnn_thetas"), (ph3, "L3_gnn_phis")):
                        load(dst, a[name].rearrange("l (m p) i -> p (l m) i", p=P))

                    def spread(dst, src, width):
                        load(dst, src.broadcast_to([P, width]))

                    spread(CHB[:, :, :].rearrange("p l d -> p (l d)"),
                           a["L0_gnn_ch_b"].rearrange("(o l) c d -> o (l c d)", o=1), LAYERS * D)
                    spread(MB[:, :], a["L0_gnn_mlp_b"].rearrange("(o d) -> o d", o=1), D)
                    spread(B1[:, :], a["L1_gnn_theta_b"].rearrange("(o d) -> o d", o=1), D)
                    spread(B1b, a["L1_gnn_phi_b"].rearrange("(o d) -> o d", o=1), D)
                    spread(AV[:, 0, :], a["L2_gnn_a_left"].rearrange("(o h) c -> o (h c)", o=1), D)
                    spread(AV[:, 1, :], a["L2_gnn_a_right"].rearrange("(o h) c -> o (h c)", o=1), D)
                    spread(GAM[:, :, :].rearrange("p l d -> p (l d)"),
                           a["L3_gnn_gammas"].rearrange("(o l) d -> o (l d)", o=1), LAYERS * D)
                    spread(BET[:, :, :].rearrange("p l d -> p (l d)"),
                           a["L3_gnn_betas"].rearrange("(o l) d -> o (l d)", o=1), LAYERS * D)
                    eng.wait_ge(loaded, n)
                    eng.sem_inc(ready, 1)

                @block.gpsimd
                def _(eng):
                    eng.memset(X[:, NT - 1, :], 0.0).then_inc(zeroed, 1)
                    eng.memset(ch, 0.0).then_inc(zeroed, 1)

                @block.vector
                def _(eng):
                    c = Count(eng, chain)
                    eng.wait_ge(ready, 1)
                    c.inc(eng.tensor_tensor(ph1, ph1, th1, ALU.subtract))
                    c.inc(eng.tensor_tensor(ph3, ph3, th3, ALU.subtract))
                    c.inc(eng.tensor_tensor(B1[:, :], B1[:, :], B1b, ALU.add))
                    for q in range(2 * LAYERS):
                        c.inc(eng.tensor_scalar(fcb_wide[:, q, :], ones[:, :], fcb[:, q:q + 1], None, ALU.mult))
                    assert c.n == 3 + 2 * LAYERS
                    eng.wait_ge(moved, banks)
                    for s in range(2):
                        c.link(eng.tensor_tensor(prod[:, s], W2[:, :, :],
                                                 AV[:, s:s + 1, :].broadcast_to([P, 2, D]), ALU.mult))
                        c.inc(eng.tensor_reduce(WA[:, :, HEADS * s:HEADS * s + HEADS],
                                                prod[:, s].rearrange("p k (h c) -> p k h c", h=HEADS),
                                                AX.X, ALU.add))

                @block.tensor
                def _(eng):
                    eng.wait_ge(ready, 1)
                    eng.wait_ge(chain, 3 + 2 * LAYERS)
                    b = 0
                    for nat, _ in turns:
                        if b >= 4:
                            eng.wait_ge(moved, b - 3)
                        for k in range(2):
                            for m in range(2):
                                last = eng.transpose(ps[:, b % 4, k * D + m * P:k * D + m * P + P], nat(m, k), ident[:, :])
                        last.then_inc(made, 1)
                        b += 1
                    for l in range(LAYERS):
                        eng.wait_ge(moved, b - 3)
                        for m in range(2):
                            for k in range(2):
                                last = eng.matmul(ps[:, b % 4, m * D:m * D + D], fc[:, 2 * l + k, m * P:m * P + P],
                                                  ch[:, 2 * l + k, :], start=k == 0, stop=k == 1)
                        last.then_inc(made, 1)
                        b += 1
                        eng.wait_ge(moved, b - 3)
                        for k in range(2):
                            last = eng.matmul(ps[:, b % 4, 0:D], fcb_wide[:, 2 * l + k, :], ch[:, 2 * l + k, :],
                                              start=k == 0, stop=k == 1)
                        last.then_inc(made, 1)
                        b += 1

                @block.scalar
                def _(eng):
                    b = 0
                    for _, dst in turns:
                        eng.wait_ge(made, b + 1)
                        eng.activation(dst, ps[:, b % 4, :].rearrange("p (k d) -> p k d", k=2), ACT.Copy).then_inc(moved, 1)
                        b += 1
                    for l in range(LAYERS):
                        eng.wait_ge(made, b + 1)
                        eng.activation(GW[:, l], ps[:, b % 4, :].rearrange("p (k d) -> p k d", k=2), ACT.Copy).then_inc(moved, 1)
                        b += 1
                        eng.wait_ge(made, b + 1)
                        eng.activation(GB[:, l, :], ps[:, b % 4, 0:D], ACT.Copy).then_inc(moved, 1)
                        b += 1

        def edge_columns():
            CH = ET // 4
            whole = E // P - 3 * CH
            part = E % P
            rows_i = ARENA[0:CH, 0:8 * P].bitcast(I32).rearrange("p (s c e) -> p s c e", s=2, c=4)
            rows_f = ARENA[0:CH, 8 * P:20 * P].rearrange("p (s c e) -> p s c e", s=3, c=4)
            zero = ARENA[:, 20 * P:20 * P + 4 * ET]
            sent = ARENA[0:1, 20 * P + 4 * ET:20 * P + 4 * ET + RW]
            low_sent = ARENA[0:1, 20 * P + 4 * ET + RW:20 * P + 4 * ET + RW + D]
            with Stage(nc, "col") as st:
                padded, loaded, cast = st.sem("padded"), st.sem("loaded"), st.sem("cast")
                turned, moved, stored = st.sem("turned"), st.sem("moved"), st.sem("stored")
                zeroed = st.sem("zeroed")
                ps = st.stack.enter_context(nc.psum_tensor("col_ps", [P, 3, 512], F32))
                block = st.block()

                @block.gpsimd
                def _(eng):
                    eng.memset(rows_i, N).then_inc(padded, 1)
                    eng.memset(rows_f[:, 2], 0.0).then_inc(padded, 1)
                    eng.memset(zero, 0.0).then_inc(zeroed, 1)
                    eng.memset(sent, 0.0).then_inc(zeroed, 1)

                @block.sync
                def _(eng):
                    eng.wait_ge(padded, 2)
                    n = 0
                    for s, name, rows in ((0, "src", rows_i[:, 0]), (1, "dst", rows_i[:, 1]), (2, "edge_weight", rows_f[:, 2])):
                        flat = a[name]
                        eng.dma_start(rows[:, 0:3, :], flat[0:3 * CH * P].rearrange("(c p e) -> p c e", c=3, e=P)).then_inc(loaded, 16)
                        eng.dma_start(rows[0:whole, 3, :],
                                      flat[3 * CH * P:(3 * CH + whole) * P].rearrange("(p e) -> p e", e=P)).then_inc(loaded, 16)
                        eng.dma_start(rows[whole:whole + 1, 3, 0:part],
                                      flat[(3 * CH + whole) * P:E].rearrange("(o e) -> o e", o=1)).then_inc(loaded, 16)
                        n += 48
                    eng.wait_ge(zeroed, 2)
                    k = 0
                    for flag in (flag_dst, flag_src):
                        eng.dma_start(flag.rearrange("(p c) o -> p (c o)", p=P), zero[:, 0:ET]).then_inc(stored, 16)
                        k += 16
                    for half in range(2):
                        eng.dma_start(ERE.rearrange("(p c) h -> p (c h)", p=P)[:, half * 4 * ET:(half + 1) * 4 * ET],
                                      zero).then_inc(stored, 16)
                        k += 16
                    for h in (hist_start, hist_count):
                        eng.dma_start(h[:, HI * LO:NP], zero[0:2, 0:NP - HI * LO]).then_inc(stored, 16)
                        k += 16
                    eng.dma_start(PR[ROW_ZERO:ROW_ZERO + 1, :], zero[0:1, 0:D]).then_inc(stored, 16)
                    eng.wait_ge(cast, 2)
                    eng.dma_start(dst_row.rearrange("o (c p e) -> p (o c) e", c=4, e=P), rows_f[:, 1]).then_inc(stored, 16)
                    eng.wait_ge(zeroed, 4)
                    eng.dma_start(PR[ROW_LOW:ROW_LOW + 1, :], low_sent).then_inc(stored, 16)
                    eng.dma_start(PA[ROW_ZERO:ROW_ZERO + 1, :], sent[0:1, :]).then_inc(stored, 16)
                    eng.dma_start(CR[ET:ET + 1, :], sent[0:1, :]).then_inc(stored, 16)
                    eng.wait_ge(stored, k + 16 * 5)

                @block.vector
                def _(eng):
                    eng.wait_ge(zeroed, 2)
                    eng.memset(low_sent, LOW).then_inc(zeroed, 1)
                    eng.memset(sent[0:1, D + HEADS:RW], LOW).then_inc(zeroed, 1)
                    eng.wait_ge(loaded, 144)
                    for s in range(2):
                        eng.tensor_copy(rows_f[:, s], rows_i[:, s]).then_inc(cast, 1)
                    for s, dst in ((0, SRCF), (1, DSTF), (2, WE)):
                        eng.wait_ge(turned, s + 1)
                        eng.tensor_copy(dst[:, :], ps[:, s, 0:ET]).then_inc(moved, 1)
                    eng.wait_ge(moved, 1)
                    eng.tensor_copy(SRCI[:, :], SRCF[:, :]).then_inc(moved, 1)

                @block.tensor
                def _(eng):
                    eng.wait_ge(cast, 2)
                    eng.wait_ge(loaded, 144)
                    for s in range(3):
                        for c in range(4):
                            last = eng.transpose(ps[:, s, c * CH:(c + 1) * CH], rows_f[:, s, c, :], ident[0:CH, 0:CH])
                        last.then_inc(turned, 1)

        def split_key(c, key, hi, lo, tmp):
            c.link(c.eng.tensor_copy(tmp[:, 0], key[:, :]))
            c.inc(c.eng.tensor_scalar(tmp[:, 1], tmp[:, 0], LO.bit_length() - 1, None, ALU.arith_shift_right))
            c.link(c.eng.tensor_scalar(tmp[:, 2], tmp[:, 0], LO - 1, None, ALU.bitwise_and))
            c.inc(c.eng.tensor_copy(hi[:, :], tmp[:, 1]))
            c.link(c.eng.tensor_copy(lo[:, :], tmp[:, 2]))

        count = sb("count", [HI, LO])
        startv = sb("startv", [HI, LO])
        small = sb("small", [HI, LO + 2])

        def one_hot(eng, dst, key, t, n, width):
            return eng.tensor_tensor(dst, key[:, ds(t, n)].unsqueeze(2).broadcast_to([P, n, width]),
                                     iota_b[:, 0:width].unsqueeze(1).broadcast_to([P, n, width]), ALU.is_equal)

        def histogram(which, key):
            steps = ET // HB
            with Stage(nc, f"hist{which}") as st:
                chain, hot, made, moved = (st.sem(n) for n in ("chain", "hot", "made", "moved"))
                passed, stored, rows_done = st.sem("passed"), st.sem("stored"), st.sem("rows")
                ps = st.stack.enter_context(nc.psum_tensor(f"hist{which}_ps", [HI, 2, 512], F32))
                rs = st.stack.enter_context(nc.psum_tensor(f"hist{which}_rs", [HI, 512], F32))
                block = st.block()

                @block.vector
                def _(eng):
                    c = Count(eng, chain)
                    split_key(c, key, key_hi, key_lo, key_tmp)
                    with eng.Fori(0, steps // 2) as i:
                        for b in range(2):
                            eng.wait_ge(made, i * 2 + (b + 1))
                            one_hot(eng, oh_hi[:, b], key_hi, i * (2 * HB) + b * HB, HB, HI).then_inc(hot, 1)
                            one_hot(eng, oh_lo[:, b], key_lo, i * (2 * HB) + b * HB, HB, LO).then_inc(hot, 1)
                    eng.wait_ge(moved, steps + 2)
                    c.link(eng.tensor_reduce(count[:, :], HIST[0:HI].rearrange("p t l -> p l t"), AX.X, ALU.add))
                    c.link(eng.tensor_tensor_scan(small[:, 0:LO], ones[0:HI, 0:LO], count[:, :], 0.0, ALU.mult, ALU.add))
                    c.link(eng.tensor_tensor(startv[:, :], small[:, 0:LO], count[:, :], ALU.subtract))
                    eng.sem_inc(rows_done, 1)
                    eng.wait_ge(rows_done, 2)
                    c.link(eng.tensor_copy(small[:, LO:LO + 1], rs[:, 0:1]))
                    c.link(eng.tensor_scalar(startv[:, :], startv[:, :], small[:, LO:LO + 1], None, ALU.add))
                    eng.sem_inc(rows_done, 1)

                @block.tensor
                def _(eng):
                    eng.sem_inc(made, 2)
                    with eng.Fori(0, steps // 2) as i:
                        for b in range(2):
                            eng.wait_ge(moved, i * 2 + (b + 1))
                            eng.wait_ge(hot, i * 4 + (2 * b + 2))
                            for k in range(HB):
                                last = eng.matmul(ps[:, b, k * LO:(k + 1) * LO], oh_hi[:, b, k, :], oh_lo[:, b, k, :],
                                                  start=True, stop=True)
                            last.then_inc(made, 1)
                    eng.wait_ge(rows_done, 1)
                    eng.matmul(rs[:, 0:1], before[0:HI, 0:HI], small[:, LO - 1:LO], start=True, stop=True).then_inc(rows_done, 1)

                @block.scalar
                def _(eng):
                    eng.sem_inc(moved, 2)
                    with eng.Fori(0, steps // 2) as i:
                        for b in range(2):
                            eng.wait_ge(made, i * 2 + (b + 3))
                            eng.sem_inc(passed, 1)
                            eng.activation(HIST[0:HI, ds(i * (2 * HB) + b * HB, HB), :],
                                           ps[:, b, 0:HB * LO].rearrange("p (k l) -> p k l", l=LO), ACT.Copy).then_inc(moved, 1)

                @block.sync
                def _(eng):
                    eng.wait_ge(rows_done, 3)
                    eng.dma_start(hist_start[which:which + 1, 0:HI * LO].rearrange("o (h l) -> (o h) l", l=LO), startv[:, :]).then_inc(stored, 16)
                    eng.dma_start(hist_count[which:which + 1, 0:HI * LO].rearrange("o (h l) -> (o h) l", l=LO), count[:, :]).then_inc(stored, 16)
                    eng.wait_ge(stored, 32)

        node_f, = carve(ARENA[:, 4 * ET:4 * ET + 6 * NT], ((6, NT), F32))

        def node_indices():
            START, CNT, HAS, LASTE, T1, T2_ = range(6)
            MASKS = ARENA[:, 0:ET * 2]
            with Stage(nc, "node") as st:
                loaded, chain, ready = (st.sem(n) for n in ("loaded", "chain", "ready"))
                marked = gathered[0]
                flags_in, made, stored, rooted = (st.sem(n) for n in ("flags_in", "made", "stored", "rooted"))
                fl = ARENA[:, 0:2 * ET].rearrange("p (s e) -> p s e", s=2)
                mk = ARENA[:, 2 * ET:4 * ET].bitcast(BF16).rearrange("p (s e) -> p s e", e=ET)
                block = st.block()

                @block.sync
                def _(eng):
                    with nc.allow_non_contiguous_dma("node numbers across the partitions"):
                        for w in range(2):
                            if w:
                                eng.wait_ge(ready, 1)
                            for k, h in ((START, hist_start), (CNT, hist_count)):
                                eng.dma_start(node_f[:, k, :], h[w:w + 1, :].rearrange("o (t p) -> p (o t)", p=P)).then_inc(loaded, 16)
                    marked.arrived(eng, 2 * NT)
                    for s, flag in enumerate((flag_dst, flag_src)):
                        eng.dma_start(fl[:, s, :], flag.rearrange("(p c) o -> p (c o)", p=P)).then_inc(flags_in, 16)
                    eng.wait_ge(made, 4)
                    for k, row in ((0, nst_dst), (1, low_dst), (2, low_src)):
                        eng.dma_start(row[:, 0:EP].rearrange("o (p c) -> (o p) c", p=P), mk[:, k, :]).then_inc(stored, 16)
                        eng.dma_start(row[:, EP:EP + P], mk[0:1, 3, 0:P]).then_inc(stored, 16)
                    eng.wait_ge(stored, 96)

                @block.vector
                def _(eng):
                    c = Count(eng, chain)
                    f = node_f
                    for w, norm, first in ((0, norm_in, first_dst), (1, norm_out, first_src)):
                        eng.wait_ge(loaded, 32 * (w + 1))
                        c.inc(eng.tensor_scalar(norm[:, :], f[:, CNT, :], 1.0, None, ALU.max))
                        c.inc(eng.tensor_scalar(f[:, HAS, :], f[:, CNT, :], 1.0, None, ALU.min))
                        c.link(eng.tensor_tensor(f[:, LASTE, :], f[:, START, :], f[:, CNT, :], ALU.add))
                        c.link(eng.tensor_scalar(f[:, T1, :], f[:, START, :], -OOB, None, ALU.add))
                        c.link(eng.tensor_tensor(f[:, T1, :], f[:, T1, :], f[:, HAS, :], ALU.mult))
                        c.link(eng.tensor_scalar(f[:, T1, :], f[:, T1, :], OOB, None, ALU.add))
                        c.link(eng.tensor_copy(first[:, :], f[:, T1, :]))
                        for row, dst in (((ROW_ZERO, end_sum), (ROW_LOW, end_max)) if w == 0 else ((ROW_LOW, end_src),)):
                            c.link(eng.tensor_scalar(f[:, T1, :], f[:, LASTE, :], -(row + 1.0), None, ALU.add))
                            c.link(eng.tensor_tensor(f[:, T1, :], f[:, T1, :], f[:, HAS, :], ALU.mult))
                            c.link(eng.tensor_scalar(f[:, T1, :], f[:, T1, :], float(row), None, ALU.add))
                            c.link(eng.tensor_copy(dst[:, :], f[:, T1, :]))
                        if w == 0:
                            c.link(eng.tensor_scalar(f[:, T1, :], f[:, LASTE, :], -1.0, None, ALU.add))
                            c.link(eng.tensor_scalar(f[:, T1, :], f[:, T1, :], 0.0, None, ALU.max))
                            c.link(eng.tensor_copy(carry_row[:, :], f[:, T1, :]))
                            c.link(eng.tensor_scalar(carry_row[:, :], carry_row[:, :], 7, None, ALU.arith_shift_right))
                            c.link(eng.tensor_copy(f[:, T1, :], carry_row[:, :]))
                            c.link(eng.tensor_scalar(f[:, T2_, :], f[:, T1, :], float(P), None, ALU.mult))
                            c.link(eng.tensor_tensor(f[:, T2_, :], f[:, START, :], f[:, T2_, :], ALU.is_lt))
                            c.link(eng.tensor_tensor(f[:, T2_, :], f[:, T2_, :], f[:, HAS, :], ALU.mult))
                            c.link(eng.tensor_scalar(f[:, T1, :], f[:, T1, :], -(ET + 1.0), None, ALU.add))
                            c.link(eng.tensor_tensor(f[:, T1, :], f[:, T1, :], f[:, T2_, :], ALU.mult))
                            c.link(eng.tensor_scalar(f[:, T1, :], f[:, T1, :], float(ET), None, ALU.add))
                            c.link(eng.tensor_copy(carry_row[:, :], f[:, T1, :]))
                        eng.sem_inc(ready, 1)
                    for lo in range(LO):
                        c.inc(eng.tensor_tensor_scan(HIST[0:HI, :, lo], ones[0:HI, 0:1].broadcast_to([HI, ET]),
                                                     HIST[0:HI, :, lo], startv[:, lo:lo + 1], ALU.mult, ALU.add))
                    eng.wait_ge(rooted, 2)
                    for norm in (norm_in, norm_out):
                        eng.reciprocal(norm[:, :], norm[:, :])
                    eng.wait_ge(flags_in, 32)
                    eng.tensor_scalar(mk[:, 0, :], fl[:, 0, :], -1.0, 1.0, ALU.mult, ALU.add).then_inc(made, 1)
                    eng.tensor_scalar(mk[:, 1, :], fl[:, 0, :], LOW, None, ALU.mult).then_inc(made, 1)
                    eng.tensor_scalar(mk[:, 2, :], fl[:, 1, :], LOW, None, ALU.mult).then_inc(made, 1)
                    eng.memset(mk[:, 3, :], 0.0).then_inc(made, 1)

                @block.scalar
                def _(eng):
                    eng.wait_ge(ready, 2)
                    for norm in (norm_in, norm_out):
                        eng.activation(norm[:, :], norm[:, :], ACT.Sqrt).then_inc(rooted, 1)

                @block.gpsimd
                def _(eng):
                    eng.wait_ge(ready, 2)
                    for first, flag in ((first_dst, flag_dst), (first_src, flag_src)):
                        for t in range(NT):
                            eng.indirect_dma_start(flag, bass.IndirectOffsetOnAxis(ap=first[:, t:t + 1], axis=0),
                                                   ones[:, 0:1], None, bounds_check=EP - 1, oob_is_err=False).then_inc(marked.sem, 16)
            marked.close(2 * NT)


        RANKS = -(-(ET // RB) // LAYERS)

        def rank_beside(layer):
            first = layer * RANKS
            steps = min(RANKS, ET // RB - first)

            def beside(st, name):
                names = ("hot", "flipped", "taken", "met", "passed", "ranked")
                hot, flipped, taken, met, passed, ranked = (st.sem(n) for n in names)
                pa = st.stack.enter_context(nc.psum_tensor(f"{name}_ra", [P, 512], F32))
                pb = st.stack.enter_context(nc.psum_tensor(f"{name}_rb", [P, 512], F32))
                turned_hot = pa[:, :].bitcast(BF16).rearrange("p (s e) -> p s e", s=2)

                def at(phase, fn):
                    def step(g, q, turn):
                        if q % 3 == phase and not (isinstance(g, int) and g // 3 >= steps):
                            fn(turn * (SETS // 3) + q // 3, q // 3 % 2)
                    return step

                def on_vector(eng):
                    eng.sem_inc(ranked, 2)

                    def one_hots(k, b):
                        eng.wait_ge(ranked, k + 1)
                        one_hot(eng, rank_hi[:, b], key_hi, (k + first) * RB, RB, HI).then_inc(hot, 1)
                        one_hot(eng, rank_lo[:, b], key_lo, (k + first) * RB, RB, LO).then_inc(hot, 1)

                    def places(k, b):
                        eng.wait_ge(met, k + 3)
                        for n in range(RB):
                            eng.scalar_tensor_tensor(rank_tmp[:, n, :], pb[:, n * P:(n + 1) * P], 2.0, upto[:, :],
                                                     ALU.is_equal, ALU.mult, accum_out=rank[:, 0, n:n + 1]).then_inc(passed, 1)
                        eng.tensor_tensor(sel[:, :, :], pa[:, 0:RB * LO].rearrange("p (k l) -> p k l", l=LO),
                                          rank_lo[:, b], ALU.mult).then_inc(passed, 1)
                        eng.wait_ge(passed, k * 6 + 5)
                        eng.tensor_reduce(rank[:, 1, :], sel[:, :, :], AX.X, ALU.add).then_inc(passed, 1)
                        eng.wait_ge(passed, k * 6 + 6)
                        eng.tensor_tensor(pos[:, ds((k + first) * RB, RB)], rank[:, 1, :], rank[:, 0, :], ALU.subtract).then_inc(ranked, 1)

                    return [(at(1, places), 0)], [(at(0, one_hots), 3)]

                def on_tensor(eng):
                    eng.sem_inc(met, 2)

                    def flip(k, b):
                        eng.wait_ge(hot, k * 2 + 2)
                        eng.wait_ge(ranked, k + 2)
                        for n in range(RB):
                            eng.transpose(turned_hot[0:HI, 0, n * P:(n + 1) * P], rank_hi[:, b, n, :], identb[:, :])
                            last = eng.transpose(turned_hot[0:LO, 1, n * P:(n + 1) * P], rank_lo[:, b, n, :], identb[:, :])
                        last.then_inc(flipped, 1)

                    def meet(k, b):
                        eng.wait_ge(taken, k + 1)
                        for n in range(RB):
                            cols = slice(n * P, (n + 1) * P)
                            eng.matmul(pb[:, cols], rank_t[0:HI, b, 0, cols], rank_t[0:HI, b, 0, cols], start=True, stop=False)
                            eng.matmul(pb[:, cols], rank_t[0:LO, b, 1, cols], rank_t[0:LO, b, 1, cols], start=False, stop=True)
                            last = eng.matmul(pa[:, n * LO:(n + 1) * LO], rank_tf[0:HI, b, cols],
                                              HIST[0:HI, ds((k + first) * RB + n, 1), :].rearrange("p o l -> p (o l)"), start=True, stop=True)
                        last.then_inc(met, 1)

                    return [(at(0, meet), 0)], [(at(0, flip), 2)]

                def on_scalar(eng):
                    def take(k, b):
                        eng.wait_ge(flipped, k + 1)
                        eng.wait_ge(met, k + 1)
                        eng.activation(rank_t[0:HI, b, 0, :], turned_hot[0:HI, 0, :], ACT.Copy)
                        eng.activation(rank_t[0:LO, b, 1, :], turned_hot[0:LO, 1, :], ACT.Copy)
                        eng.activation(rank_tf[0:HI, b, :], turned_hot[0:HI, 0, :], ACT.Copy).then_inc(taken, 1)

                    return [(at(0, take), 1)], []

                return on_vector, on_tensor, on_scalar, None, None
            return beside

        def order_beside(st, name):
            payload, placed, opened, summed, digits_chain = (st.sem(n) for n in ("payload", "placed", "opened", "summed", "digits"))
            sums = [st.stack.enter_context(nc.psum_tensor(f"{name}_{n}", [P, ET], F32)) for n in ("hi", "lo")]

            def digits_of(c, src, shift, hi, lo):
                c.link(c.eng.tensor_copy(digit_tmp[:, 0], src))
                c.inc(c.eng.tensor_scalar(digit_tmp[:, 1], digit_tmp[:, 0], shift, None, ALU.arith_shift_right))
                c.link(c.eng.tensor_scalar(digit_tmp[:, 2], digit_tmp[:, 0], (1 << shift) - 1, None, ALU.bitwise_and))
                c.inc(c.eng.tensor_copy(hi, digit_tmp[:, 1]))
                c.link(c.eng.tensor_copy(lo, digit_tmp[:, 2]))

            def on_vector(eng):
                c = Count(eng, digits_chain)
                digits_of(c, pos, 7, place_hi, place_lo)
                digits_of(c, DSTF[:, :], 6, pay_hi, pay_lo)
                c.link(eng.memset(no_places[:, :], 0.0))
                eng.sem_inc(opened, 1)
                eng.sem_inc(placed, 2)

                def one_hots(g, q, turn):
                    b = q % 2
                    eng.wait_ge(placed, g + 1)
                    for n in range(GT):
                        t = g * GT + n
                        eng.tensor_scalar(oh_place[:, b, n, :], iota_h[:, :], place_hi[:, ds(t, 1)], None, ALU.is_equal)
                        eng.tensor_scalar(oh_pay[:, b, n, 0, :], iota_b[:, :], place_lo[:, ds(t, 1)], pay_hi[:, ds(t, 1)], ALU.is_equal, ALU.mult)
                        last = eng.tensor_scalar(oh_pay[:, b, n, 1, :], iota_b[:, :], place_lo[:, ds(t, 1)], pay_lo[:, ds(t, 1)], ALU.is_equal, ALU.mult)
                    last.then_inc(payload, 1)

                return [], [(one_hots, 1)]

            def on_tensor(eng):
                eng.wait_ge(opened, 1)
                for d in range(2):
                    eng.matmul(sums[d][:, :], no_places[:, 0:P], no_places[:, P:P + ET], start=True, stop=False)

                def place(g, q, turn):
                    eng.wait_ge(payload, g + 1)
                    for n in range(GT):
                        for d in range(2):
                            last = eng.matmul(sums[d][:, :], oh_pay[:, q % 2, n, d, :], oh_place[:, q % 2, n, :], start=False, stop=False)
                    last.then_inc(placed, 1)

                return [], [(place, 0)]

            def on_scalar(eng):
                return [], []

            def vector_end(eng):
                c = Count(eng, digits_chain)
                c.n = 11
                eng.wait_ge(summed, 1)
                c.link(eng.tensor_scalar(place_hi, sums[0][:, :], 64.0, None, ALU.mult))
                c.link(eng.tensor_tensor(place_hi, sums[1][:, :], place_hi, ALU.add))
                c.link(eng.tensor_copy(BYSRC[:, :], place_hi))

            def tensor_end(eng):
                for d in range(2):
                    last = eng.matmul(sums[d][:, :], no_places[:, 0:P], no_places[:, P:P + ET], start=False, stop=True)
                last.then_inc(summed, 1)

            return on_vector, on_tensor, on_scalar, vector_end, tensor_end

        def node_products(name, stage, w1, out1, w2=None, out2=None, gather=None, table=None, table2=None):
            n2 = 0 if w2 is None else w2.shape[2]
            u = NODE_UNROLL
            with Stage(nc, name) as st:
                names = ("staged", "turned", "xt", "made", "moved", "done", "chain", "passed", "stored", "passed2")
                staged, turned, xt, made, moved, done, chain, passed, stored, passed2 = (st.sem(n) for n in names)
                got = gathered[0:NT // u]
                tps = st.stack.enter_context(nc.psum_tensor(f"{name}_t", [P, 3, 512], F32))
                mps = st.stack.enter_context(nc.psum_tensor(f"{name}_m", [P, u, 512], F32))
                tp = [tps[:, j % 3, 0:D] for j in range(u)]
                block = st.block()

                if gather is not None:
                    @block.gpsimd
                    def _(eng):
                        rows, index = gather
                        for t in range(NT):
                            got[t % u].arrived(eng, t // u)
                            eng.indirect_dma_start(AGG[:, t, :], None, rows,
                                                   bass.IndirectOffsetOnAxis(ap=index[:, t:t + 1], axis=0)).then_inc(got[t % u].sem, 16)

                @block.vector
                def _(eng):
                    eng.sem_inc(done, u)

                    def ahead(t, slot, turn):
                        if gather is not None:
                            got[slot].arrived(eng, turn + 1)
                        eng.wait_ge(turned, t + 1)
                        stage(eng, t, slot, chain, staged)

                    def behind(t, slot, _):
                        eng.wait_ge(moved, t + 1)
                        eng.wait_ge(made, t + 1)
                        out2(eng, t, slot, mps[:, slot, :], done)

                    pipelined(NT, u, eng, (ahead, 2), (behind, 0))

                @block.tensor
                def _(eng):
                    eng.sem_inc(turned, u)

                    def turn(t, slot, _):
                        eng.wait_ge(staged, t + 1)
                        eng.wait_ge(xt, t + (u - 1))
                        for k in range(2):
                            last = eng.transpose(tp[slot][:, k * P:(k + 1) * P], R[:, slot, k * P:(k + 1) * P], ident[:, :])
                        last.then_inc(turned, 1)

                    def product(t, slot, _):
                        eng.wait_ge(xt, t + (u + 1))
                        eng.wait_ge(done, t + 1)
                        for k in range(2):
                            last = eng.matmul(mps[:, slot, 0:D], XT[:, slot, k * P:(k + 1) * P], w1[:, k, :],
                                              start=k == 0, stop=k == 1)
                        if n2:
                            for k in range(2):
                                last = eng.matmul(mps[:, slot, D:D + n2], XT[:, slot, k * P:(k + 1) * P], w2[:, k, :],
                                                  start=k == 0, stop=k == 1)
                        last.then_inc(made, 1)

                    pipelined(NT, u, eng, (turn, 1), (product, 0))

                @block.scalar
                def _(eng):
                    eng.sem_inc(xt, u)

                    def ahead(t, slot, _):
                        eng.wait_ge(turned, t + (u + 1))
                        eng.wait_ge(made_free, t + 1)
                        eng.activation(XT[:, slot, :], tp[slot], ACT.Copy).then_inc(xt, 1)

                    def behind(t, slot, _):
                        eng.wait_ge(made, t + 1)
                        eng.wait_ge(done, t + 1)
                        eng.sem_inc(passed, 1)
                        out1(eng, t, slot, mps[:, slot, 0:D]).then_inc(moved, 1)

                    made_free = done
                    pipelined(NT, u, eng, (ahead, 1), (behind, 0))

                tables = [x for x in (table, table2) if x is not None]
                if tables:
                    @block.sync
                    def _(eng):
                        for k in range(NT // u):
                            eng.wait_ge(done, u + (k + 1) * u)
                            for src, dst in tables:
                                eng.dma_start(dst[k * u * P:(k + 1) * u * P, :].rearrange("(t p) d -> p t d", p=P),
                                              src[:, k * u:(k + 1) * u, :]).then_inc(stored, 16)
                        eng.wait_ge(stored, NT // u * 16 * len(tables))
            if gather is not None:
                for g in got:
                    g.close(NODE_UNROLL)


        def tile_of(view, t):
            return view[:, ds(t, 1), :].rearrange("p o d -> p (o d)") if not isinstance(t, int) else view[:, t, :]

        def stage_copy(src):
            def stage(eng, t, slot, chain, staged):
                eng.tensor_copy(R[:, slot, :], tile_of(src, t)).then_inc(staged, 1)
            return stage

        def stage_gcn(layer):
            def stage(eng, t, slot, chain, staged):
                eng.scalar_tensor_tensor(TMP2[:, slot, :], tile_of(AGG, t), norm_in[:, ds(t, 1)], CHB[:, layer, :],
                                         ALU.mult, ALU.add).then_inc(chain, 1)
                eng.wait_ge(chain, t + 1)
                eng.tensor_scalar(R[:, slot, :], TMP2[:, slot, :], 0.0, None, ALU.max).then_inc(staged, 1)
            return stage

        def gcn_table(layer, with_mlp):
            def out1(eng, t, slot, ps):
                return eng.activation(TMP[:, slot, :], ps, ACT.Copy, scale=norm_out[:, ds(t, 1)])

            def out2(eng, t, slot, ps, done):
                if with_mlp:
                    eng.tensor_tensor(tile_of(X, t), ps[:, D:2 * D], tile_of(X, t), ALU.add)
                eng.scalar_tensor_tensor(tile_of(AGG, t), GB[:, layer, :], norm_out[:, ds(t, 1)], TMP[:, slot, :],
                                         ALU.mult, ALU.add).then_inc(done, 1)
            return out1, out2

        def nothing_beside(st, name):
            def steps(eng):
                return [], []
            return steps, steps, steps, None, None

        def edge_pass(name, index, ops, mask, weighted, beside=nothing_beside):
            op0, op1 = ops
            with Stage(nc, name) as st:
                got = gathered
                ready = [st.sem(f"ready{q}") for q in range(SETS)]
                names = ("scaled", "turned", "scanned", "back", "pairs", "o_free", "stored", "go_pool", "go_act", "go_sp")
                scaled, turned, scanned, back, pairs, o_free, stored, go_pool, go_act, go_sp = (st.sem(n) for n in names)
                fm = st.stack.enter_context(nc.psum_tensor(f"{name}_fm", [P, 2, 2, GT * P], F32))
                em = st.stack.enter_context(nc.psum_tensor(f"{name}_em", [P, 2, 2, D], F32))
                on_vector, on_tensor, on_scalar, vector_end, tensor_end = beside(st, name)
                out_rows = PR[0:EP, :].rearrange("(t p) d -> p t d", p=P)
                uses = 3 if weighted else 2
                block = st.block()

                @block.sync
                def _(eng):
                    def prefetch(g, q):
                        eng.dma_start(idxbuf[:, q, :], index[:, ds(g * GT, GT)]).then_inc(ready[q], 16)
                        eng.dma_start(maskbuf[:, q, :], mask[0:1, ds(g * (GT * P), GT * P)].broadcast_to([P, GT * P])).then_inc(ready[q], 16)
                        if weighted:
                            eng.dma_start(wbuf[:, q, :], WE[:, ds(g * GT, GT)]).then_inc(ready[q], 16)

                    for q in range(SETS):
                        prefetch(q, q)

                    def store(g, q):
                        eng.wait_ge(pairs, g * 2 + 6)
                        eng.sem_inc(go_sp, 1)
                        eng.dma_start(out_rows[:, ds(g * GT, GT), :], O[:, q % 2, :, 0:D]).then_inc(stored, 16)
                        if not isinstance(g, int) or g + SETS < NG:
                            prefetch(g + SETS, q)
                        eng.wait_ge(stored, g * 16 + 16)
                        eng.sem_inc(o_free, 1)

                    with eng.Fori(0, (NG - SETS) // SETS) as i:
                        for q in range(SETS):
                            store(i * SETS + q, q)
                    for g in range((NG - SETS) // SETS * SETS, NG):
                        store(g, g % SETS)

                @block.gpsimd
                def _(eng):
                    def gather(g, q, turn):
                        eng.wait_ge(ready[q], turn * (16 * uses) + 16 * uses)
                        eng.sem_inc(go_pool, 1)
                        for k in range(GT):
                            eng.indirect_dma_start(G[:, q * GT + k, 0:D], None, T,
                                                   bass.IndirectOffsetOnAxis(ap=idxbuf[:, q, k:k + 1], axis=0)).then_inc(got[q].sem, 16)

                    pipelined(NG, SETS, eng, (gather, 0))

                @block.tensor
                def _(eng):
                    def forth(g, q, turn):
                        if weighted:
                            eng.wait_ge(scaled, g + 1)
                        else:
                            got[q].arrived(eng, turn * GT + GT)
                        eng.wait_ge(scanned, g + 1)
                        for k in range(GT):
                            for h in range(2):
                                last = eng.transpose(fm[:, q % 2, h, k * P:(k + 1) * P], G[:, q * GT + k, h * P:(h + 1) * P], ident[:, :])
                        last.then_inc(turned, 1)

                    def hither(g, q, turn):
                        eng.wait_ge(scanned, g + 3)
                        for pair in range(2):
                            eng.wait_ge(pairs, g * 2 + (pair + 3))
                            for k in range(2):
                                for h in range(2):
                                    last = eng.transpose(em[:, pair, k, h * P:(h + 1) * P],
                                                         S[:, q % 2, h, (2 * pair + k) * P:(2 * pair + k + 1) * P], ident[:, :])
                            last.then_inc(back, 1)

                    early, late = on_tensor(eng)
                    pipelined(NG, SETS, eng, *early, (forth, 1), (hither, 0), *late)
                    if tensor_end:
                        tensor_end(eng)

                @block.vector
                def _(eng):
                    eng.memset(S[:, 1, :, GT * P - 1:GT * P], 0.0).then_inc(scanned, 1)
                    eng.wait_ge(scanned, 1)
                    eng.sem_inc(scanned, 1)

                    def scan(g, q, turn):
                        eng.wait_ge(turned, g + 1)
                        eng.wait_ge(pairs, g * 2 + 2)
                        eng.wait_ge(scanned, g + 2)
                        for h in range(2):
                            last = eng.tensor_tensor_scan(S[:, q % 2, h, :], maskbuf[:, q, :], fm[:, q % 2, h, :],
                                                          S[:, 1 - q % 2, h, GT * P - 1:GT * P], op0, op1)
                        last.then_inc(scanned, 1)

                    early, late = on_vector(eng)
                    pipelined(NG, SETS, eng, *early, (scan, 0), *late)
                    if vector_end:
                        vector_end(eng)

                @block.scalar
                def _(eng):
                    eng.sem_inc(pairs, 4)
                    eng.sem_inc(o_free, 2)

                    def scale(g, q, turn):
                        got[q].arrived(eng, turn * GT + GT)
                        for k in range(GT):
                            last = eng.activation(G[:, q * GT + k, 0:D], G[:, q * GT + k, 0:D], ACT.Copy, scale=wbuf[:, q, k:k + 1])
                        last.then_inc(scaled, 1)

                    def evac(g, q, turn):
                        eng.wait_ge(o_free, g + 1)
                        for pair in range(2):
                            eng.wait_ge(back, g * 2 + (pair + 1))
                            eng.activation(O[:, q % 2, 2 * pair:2 * pair + 2, 0:D], em[:, pair], ACT.Copy).then_inc(pairs, 1)

                    early, late = on_scalar(eng)
                    scaling = [(scale, 2)] if weighted else []
                    pipelined(NG, SETS, eng, *early, *scaling, (evac, 0), *late)
            for q in range(SETS):
                got[q].close(GT * ((NG - q + SETS - 1) // SETS))


        RST, NMR = sb("RST", [P, NT]), sb("NMR", [P, NT])
        BS, MV5 = sb("BS", [P, NODE_UNROLL, 6]), sb("MV5", [P, NODE_UNROLL, 2])

        def layer_norm(name, prepare, gather=None, out_rows=None):
            u = NODE_UNROLL
            with Stage(nc, name) as st:
                names = ("chain", "aggregated", "rooted", "scaled", "done", "stored", "apart")
                chain, aggregated, rooted, scaled, done, stored, apart = (st.sem(n) for n in names)
                got = gathered[0:NT // u]
                block = st.block()

                if gather is not None:
                    @block.gpsimd
                    def _(eng):
                        rows, index = gather
                        for t in range(NT):
                            got[t % u].arrived(eng, t // u)
                            eng.indirect_dma_start(AGG[:, t, :], None, rows,
                                                   bass.IndirectOffsetOnAxis(ap=index[:, t:t + 1], axis=0)).then_inc(got[t % u].sem, 16)

                @block.vector
                def _(eng):
                    c = Count(eng, chain)
                    with c.loop(NT // u, LINKS[prepare] + 3) as i:
                        if gather is not None:
                            for k in range(u):
                                got[k].arrived(eng, i + 1)
                        prepare(c, ds(i * u, u))
                        eng.sem_inc(apart, 1)
                        for j in range(u):
                            last = eng.bn_stats(BS[:, j, :], X[:, ds(i * u + j, 1), :].rearrange("p o d -> p (o d)"))
                        c.link(last)
                        eng.sem_inc(apart, 1)
                        for j in range(u):
                            last = eng.bn_aggr(MV5[:, j, :], BS[:, j, :])
                        c.link(last)
                        c.link(eng.tensor_copy(MV[:, ds(i * u, u), :], MV5[:, :, :]))
                    c.link(eng.tensor_scalar(RST[:, :], MV[:, :, 1], EPS, None, ALU.add))
                    eng.sem_inc(aggregated, 1)
                    eng.wait_ge(rooted, 1)
                    c.link(eng.reciprocal(RST[:, :], RST[:, :]))
                    c.link(eng.tensor_tensor(NMR[:, :], MV[:, :, 0], RST[:, :], ALU.mult))
                    c.link(eng.tensor_scalar(NMR[:, :], NMR[:, :], -1.0, None, ALU.mult))
                    eng.sem_inc(scaled, 1)

                @block.scalar
                def _(eng):
                    eng.wait_ge(aggregated, 1)
                    eng.activation(RST[:, :], RST[:, :], ACT.Sqrt).then_inc(rooted, 1)
                    eng.wait_ge(scaled, 1)
                    with eng.Fori(0, NT // u) as i:
                        for j in range(u):
                            t = i * u + j
                            last = eng.activation(tile_of(X, t), tile_of(X, t), ACT.Identity,
                                                  bias=NMR[:, ds(t, 1)], scale=RST[:, ds(t, 1)])
                        last.then_inc(done, 1)

                if out_rows is not None:
                    @block.sync
                    def _(eng):
                        eng.wait_ge(done, NT // u)
                        eng.dma_start(out_rows[0:(NT - 1) * P, :].rearrange("(t p) d -> p t d", p=P), X[:, 0:NT - 1, :]).then_inc(stored, 16)
                        eng.dma_start(out_rows[(NT - 1) * P:N, :], X[0:LAST, NT - 1, :]).then_inc(stored, 16)
                        eng.wait_ge(stored, 32)
            if gather is not None:
                for g in got:
                    g.close(NODE_UNROLL)


        def none(c, at):
            pass

        def add_bias(c, at):
            c.link(c.eng.tensor_tensor(X[:, at, :], X[:, at, :], MB[:, :].unsqueeze(1).broadcast_to([P, NODE_UNROLL, D]), ALU.add))

        def edge_max(c, at):
            c.link(c.eng.tensor_tensor(AGG[:, at, :], C[:, at, 0:D], AGG[:, at, :], ALU.add))
            c.link(c.eng.scalar_tensor_tensor(X[:, at, :], AGG[:, at, :], 0.0, X[:, at, :], ALU.max, ALU.add))

        def last(c, at):
            c.link(c.eng.scalar_tensor_tensor(X[:, at, :], Y[:, at, :], 0.0, X[:, at, :], ALU.max, ALU.add))

        LINKS = {none: 0, add_bias: 1, edge_max: 2, last: 1}

        mean_b, rstd_b = carve(WORK, ((D,), F32), ((D,), F32))

        def batch_norm(name, layer, gather):
            u = NODE_UNROLL
            with Stage(nc, name) as st:
                names = ("chain", "made", "summed", "squared", "dev", "var_ready")
                chain, made, summed, squared, dev, var_ready = (st.sem(n) for n in names)
                got = gathered[0:NT // u]
                ps = st.stack.enter_context(nc.psum_tensor(f"{name}_ps", [P, 2, 512], F32))
                block = st.block()

                @block.gpsimd
                def _(eng):
                    rows, index = gather
                    for t in range(NT):
                        got[t % u].arrived(eng, t // u)
                        eng.indirect_dma_start(AGG[:, t, :], None, rows,
                                               bass.IndirectOffsetOnAxis(ap=index[:, t:t + 1], axis=0)).then_inc(got[t % u].sem, 16)

                def column_sums(eng, dst, src, ready):
                    for t in range(NT):
                        if t % u == 0:
                            eng.wait_ge(ready, t // u + 1)
                        n = P if t < NT - 1 else LAST
                        last = eng.matmul(dst, ones[0:n, :], src[0:n, t, :], start=t == 0, stop=t == NT - 1)
                    last.then_inc(summed, 1)

                @block.tensor
                def _(eng):
                    column_sums(eng, ps[:, 0, 0:D], Y, made)
                    column_sums(eng, ps[:, 1, 0:D], AGG, squared)

                @block.scalar
                def _(eng):
                    for k in range(NT // u):
                        at = slice(k * u, (k + 1) * u)
                        eng.wait_ge(dev, k + 1)
                        eng.activation(AGG[:, at, :], Y[:, at, :], ACT.Square).then_inc(squared, 1)
                    eng.wait_ge(var_ready, 1)
                    eng.activation(rstd_b[:, :], rstd_b[:, :], ACT.Sqrt).then_inc(var_ready, 1)

                @block.vector
                def _(eng):
                    c = Count(eng, chain)
                    wide = [P, u, D]
                    for k in range(NT // u):
                        at = slice(k * u, (k + 1) * u)
                        for g in got:
                            g.arrived(eng, k + 1)
                        c.link(eng.tensor_tensor(AGG[:, at, :], C[:, at, 0:D], AGG[:, at, :], ALU.add))
                        eng.tensor_scalar(Y[:, at, :], AGG[:, at, :], 0.0, None, ALU.max).then_inc(made, 1)
                    eng.wait_ge(summed, 1)
                    c.link(eng.tensor_scalar(mean_b[:, :], ps[:, 0, 0:D], 1.0 / N, None, ALU.mult))
                    for k in range(NT // u):
                        at = slice(k * u, (k + 1) * u)
                        eng.tensor_tensor(Y[:, at, :], Y[:, at, :], mean_b[:, :].unsqueeze(1).broadcast_to(wide),
                                          ALU.subtract).then_inc(dev, 1)
                    eng.wait_ge(summed, 2)
                    c.link(eng.tensor_scalar(rstd_b[:, :], ps[:, 1, 0:D], 1.0 / N, EPS, ALU.mult, ALU.add))
                    eng.sem_inc(var_ready, 1)
                    eng.wait_ge(var_ready, 2)
                    c.link(eng.reciprocal(rstd_b[:, :], rstd_b[:, :]))
                    c.link(eng.tensor_tensor(rstd_b[:, :], rstd_b[:, :], GAM[:, layer, :], ALU.mult))
                    eng.wait_ge(squared, NT // u)
                    for k in range(NT // u):
                        at = slice(k * u, (k + 1) * u)
                        c.link(eng.tensor_tensor(Y[:, at, :], Y[:, at, :], rstd_b[:, :].unsqueeze(1).broadcast_to(wide), ALU.mult))
                        c.inc(eng.tensor_tensor(Y[:, at, :], Y[:, at, :], BET[:, layer, :].unsqueeze(1).broadcast_to(wide), ALU.add))
            for g in got:
                g.close(NODE_UNROLL)


        def stage_relu(src):
            def stage(eng, t, slot, chain, staged):
                eng.tensor_scalar(R[:, slot, :], tile_of(src, t), 0.0, None, ALU.max).then_inc(staged, 1)
            return stage

        def copy_to(dst):
            def out1(eng, t, slot, ps):
                return eng.activation(tile_of(dst, t), ps, ACT.Copy)
            return out1

        def flow_l0():
            out1, out2 = gcn_table(0, False)
            node_products("n0", stage_copy(X), GW[:, 0], out1, None, out2, table=(AGG, T))
            for l in range(LAYERS):
                edge_pass(f"e{l}", SRCI, (ALU.mult, ALU.add), nst_dst, True, rank_beside(l))
                if l < LAYERS - 1:
                    out1, out2 = gcn_table(l + 1, True)
                    node_products(f"n{l + 1}", stage_gcn(l), GW[:, l + 1], out1, MW[:, l], out2,
                                  gather=(PR, end_sum), table=(AGG, T))
                else:
                    def out1(eng, t, slot, ps):
                        return eng.activation(TMP[:, slot, :], ps, ACT.Copy)

                    def out2(eng, t, slot, ps, done):
                        eng.tensor_tensor(tile_of(X, t), TMP[:, slot, :], tile_of(X, t), ALU.add).then_inc(done, 1)
                    node_products("n3", stage_gcn(l), MW[:, l], out1, None, out2, gather=(PR, end_sum))
            layer_norm("ln0", add_bias)

        def flow_l1():
            def out2(eng, t, slot, ps, done):
                eng.tensor_tensor(tile_of(C[:, :, 0:D], t), ps[:, D:2 * D], B1[:, :], ALU.add).then_inc(done, 1)
            node_products("n4", stage_copy(X), DF1, copy_to(AGG), TH1, out2, table=(AGG, T))
            edge_pass("e3", SRCI, (ALU.add, ALU.max), low_dst, False, order_beside)
            layer_norm("ln1", edge_max, gather=(PR, end_max))

        CHK = ET // 4
        MASK3 = dram("attention_masks", [ET * HEADS, 3 * P], BF16)
        last_key = dram("last_key", [1, ET])
        elbuf, erbuf, dstbuf, mask3, run_max, seg_max, er_seg = carve(
            YBASE, ((2, GT * HEADS), F32), ((SETS, GT * HEADS), F32), ((SETS, GT * P), F32), ((SETS, 3, P), BF16),
            ((P,), F32), ((2, P), F32), ((P,), F32))
        same, zed, lrelu, score, prob = carve(SBASE, ((2, GT, P), F32), *[((2, P), F32)] * 4)
        GH = GT * HEADS

        def attention_masks():
            wide = ARENA[0:CHK, 0:4 * HEADS * 3 * P // 2].bitcast(BF16).rearrange("p (c h k e) -> p c h k e", c=4, h=HEADS, k=3)
            rows = ARENA[0:CHK, 4 * HEADS * 3 * P // 2:4 * HEADS * 3 * P // 2 + 6 * P].bitcast(BF16)\
                .rearrange("p (k c e) -> p k c e", k=3, c=4)
            with Stage(nc, "am") as st:
                loaded, spread, stored = (st.sem(n) for n in ("loaded", "spread", "stored"))
                block = st.block()

                @block.sync
                def _(eng):
                    for k, (row, shift) in enumerate(((nst_dst, 0), (low_dst, 0), (low_dst, 1))):
                        eng.dma_start(rows[:, k], row[:, shift:shift + EP].rearrange("o (c p e) -> p (o c) e", c=4, e=P)).then_inc(loaded, 16)
                    eng.wait_ge(spread, 4)
                    for c in range(4):
                        eng.dma_start(MASK3[c * CHK * HEADS:(c + 1) * CHK * HEADS, :].rearrange("(p h) k -> p (h k)", h=HEADS),
                                      wide[:, c].rearrange("p h k e -> p (h k e)")).then_inc(stored, 16)
                    eng.wait_ge(stored, 64)

                @block.vector
                def _(eng):
                    eng.wait_ge(loaded, 48)
                    for c in range(4):
                        for k in range(3):
                            last_ = eng.tensor_copy(wide[:, c, :, k, :], rows[:, k, c, :].unsqueeze(1).broadcast_to([CHK, HEADS, P]))
                        last_.then_inc(spread, 1)

        tile_key, tile_key_i, tile_er, z4 = (v[0:CHK] for v in carve(
            YBASE[:, YBASE.shape[1] - 224:YBASE.shape[1]], ((2, 4), F32), ((2, 4), I32), ((2, 4, HEADS), F32), ((4, 4, HEADS), F32)))

        def attention_er():
            with Stage(nc, "er") as st:
                loaded, cast, stored = (st.sem(n) for n in ("loaded", "cast", "stored"))
                placed, got = gathered[0:2]
                block = st.block()

                @block.sync
                def _(eng):
                    with nc.allow_non_contiguous_dma("one element a tile"):
                        for s, e in ((0, 0), (1, P - 1)):
                            eng.dma_start(tile_key[:, s, :], dst_row.rearrange("o (c p e) -> p (o c) e", c=4, e=P)[:, :, e]).then_inc(loaded, 16)
                        eng.wait_ge(cast, 1)
                        eng.dma_start(last_key.rearrange("o (c p) -> p (o c)", c=4), tile_key[:, 1, :]).then_inc(stored, 16)
                    placed.arrived(eng, NT)
                    got.arrived(eng, 8)
                    eng.dma_start(ERE.rearrange("(c p e) h -> p c e h", c=4, e=P)[:, :, 0, :], tile_er[:, 0]).then_inc(stored, 16)
                    eng.wait_ge(stored, 32)

                @block.vector
                def _(eng):
                    eng.wait_ge(loaded, 32)
                    eng.tensor_copy(tile_key_i[:, :, :], tile_key[:, :, :]).then_inc(cast, 1)

                @block.gpsimd
                def _(eng):
                    for t in range(NT):
                        eng.indirect_dma_start(ERE, bass.IndirectOffsetOnAxis(ap=first_dst[:, t:t + 1], axis=0),
                                               C[:, t, D + HEADS:RW], None, bounds_check=EP - 1, oob_is_err=False).then_inc(placed.sem, 16)
                    eng.wait_ge(cast, 1)
                    for s in range(2):
                        for c in range(4):
                            eng.indirect_dma_start(tile_er[:, s, c, :], None, ERT,
                                                   bass.IndirectOffsetOnAxis(ap=tile_key_i[:, s, c:c + 1], axis=0)).then_inc(got.sem, 16)
            placed.close(NT)
            got.close(8)


        def attention_pass():
            SL = slice(0, GH)
            with Stage(nc, "att") as st:
                got = gathered
                ready = [st.sem(f"ready{q}") for q in range(SETS)]
                names = ("turned", "scored", "chain", "expd", "spread", "masked", "made", "moved", "o_free", "stored", "go_pool", "go_sp", "packed", "go_pe")
                turned, scored, chain, expd, spread, masked, made, moved, o_free, stored, go_pool, go_sp, packed, go_pe = (st.sem(n) for n in names)
                ta = st.stack.enter_context(nc.psum_tensor("att_a", [P, 2, 512], F32))
                tb = st.stack.enter_context(nc.psum_tensor("att_b", [P, 2, 512], F32))
                po = st.stack.enter_context(nc.psum_tensor("att_o", [P, GT, 512], F32))
                out_rows = PA[0:EP, :].rearrange("(t p) d -> p t d", p=P)
                er_rows = ERE.rearrange("(t p) h -> p t h", p=P)
                block = st.block()

                @block.sync
                def _(eng):
                    def prefetch(g, q):
                        eng.dma_start(idxbuf[:, q, :], SRCI[:, ds(g * GT, GT)]).then_inc(ready[q], 16)
                        eng.dma_start(dstbuf[:, q, :], dst_row[0:1, ds(g * (GT * P), GT * P)].broadcast_to([P, GT * P])).then_inc(ready[q], 16)
                        eng.dma_start(erbuf[:, q, :].rearrange("p (t h) -> p t h", h=HEADS), er_rows[:, ds(g * GT, GT), :]).then_inc(ready[q], 16)
                        eng.dma_start(mask3[SL, q].rearrange("p k e -> p (k e)"), MASK3[ds(g * GH, GH), :]).then_inc(ready[q], 16)

                    for q in range(SETS):
                        prefetch(q, q)

                    def store(g, q):
                        eng.wait_ge(moved, g * 4 + 8)
                        eng.sem_inc(go_sp, 1)
                        eng.dma_start(out_rows[:, ds(g * GT, GT), :], O[:, q % 2, :, :]).then_inc(stored, 16)
                        if not isinstance(g, int) or g + SETS < NG:
                            prefetch(g + SETS, q)
                        eng.wait_ge(stored, g * 16 + 16)
                        eng.sem_inc(o_free, 1)

                    with eng.Fori(0, (NG - SETS) // SETS) as i:
                        for q in range(SETS):
                            store(i * SETS + q, q)
                    for g in range((NG - SETS) // SETS * SETS, NG):
                        store(g, g % SETS)

                @block.gpsimd
                def _(eng):
                    def gather(g, q, turn):
                        eng.wait_ge(ready[q], turn * 64 + 64)
                        eng.sem_inc(go_pool, 1)
                        for k in range(GT):
                            eng.indirect_dma_start(G[:, q * GT + k, :], None, T2,
                                                   bass.IndirectOffsetOnAxis(ap=idxbuf[:, q, k:k + 1], axis=0)).then_inc(got[q].sem, 16)

                    pipelined(NG, SETS, eng, (gather, 0))

                @block.tensor
                def _(eng):
                    eng.sem_inc(made, 8)
                    eng.sem_inc(turned, 2)

                    def turn_el(g, q, turn):
                        eng.wait_ge(packed, g + 1)
                        eng.wait_ge(scored, g + 1)
                        eng.transpose(ta[SL, q % 2, 0:P], elbuf[:, q % 2, :], ident[:, :])
                        eng.transpose(ta[SL, q % 2, P:2 * P], erbuf[:, q, :], ident[:, :]).then_inc(turned, 1)

                    def turn_p(g, q, turn):
                        eng.wait_ge(expd, g + 1)
                        eng.wait_ge(masked, g + 1)
                        eng.sem_inc(go_pe, 1)
                        eng.transpose(tb[:, q % 2, 0:GH], prob[SL, q % 2, :], ident[SL, SL])
                        eng.transpose(tb[:, q % 2, GH:2 * GH], seg_max[SL, q % 2, :], ident[SL, SL]).then_inc(spread, 1)

                    def product(g, q, turn):
                        eng.wait_ge(masked, g + 3)
                        for k in range(GT):
                            eng.wait_ge(moved, g * 4 + (k + 1))
                            eng.matmul(po[:, k, 0:TW], same[:, q % 2, k, :], G[:, q * GT + k, :], start=True, stop=True).then_inc(made, 1)

                    pipelined(NG, SETS, eng, (turn_el, 2), (turn_p, 1), (product, 0))

                @block.vector
                def _(eng):
                    eng.sem_inc(scored, 2)
                    eng.sem_inc(masked, 2)

                    def score_step(g, q, turn):
                        b = q % 2
                        rev = slice(None, None, -1)
                        eng.wait_ge(turned, g + 3)
                        eng.tensor_tensor_scan(run_max[SL, :], mask3[SL, q, 1, :], ta[SL, b, 0:P], LOW, ALU.add, ALU.max).then_inc(chain, 1)
                        eng.tensor_tensor_scan(er_seg[SL, :], mask3[SL, q, 0, :], ta[SL, b, P:2 * P], 0.0, ALU.mult, ALU.add).then_inc(chain, 1)
                        eng.wait_ge(chain, g * 6 + 2)
                        eng.tensor_tensor(zed[SL, 0, :], ta[SL, b, 0:P], er_seg[SL, :], ALU.add).then_inc(chain, 1)
                        eng.wait_ge(spread, g + 1)
                        eng.tensor_tensor_scan(seg_max[SL, b, rev], mask3[SL, q, 2, rev], run_max[SL, rev], LOW, ALU.add, ALU.max).then_inc(chain, 1)
                        eng.wait_ge(chain, g * 6 + 4)
                        eng.tensor_tensor(zed[SL, 1, :], seg_max[SL, b, :], er_seg[SL, :], ALU.add).then_inc(chain, 1)
                        eng.wait_ge(chain, g * 6 + 5)
                        eng.scalar_tensor_tensor(lrelu[SL, :, :], zed[SL, :, :], 0.2, zed[SL, :, :], ALU.mult, ALU.max).then_inc(chain, 1)
                        eng.wait_ge(chain, g * 6 + 6)
                        eng.tensor_tensor(score[SL, b, :], lrelu[SL, 0, :], lrelu[SL, 1, :], ALU.subtract).then_inc(scored, 1)

                    def weight_step(g, q, turn):
                        b = q % 2
                        eng.wait_ge(spread, g + 3)
                        eng.wait_ge(made, g * 4 + 4)
                        eng.wait_ge(o_free, g + 1)
                        p = tb[:, b, 0:GH].rearrange("p (t h) -> p t h", h=HEADS)
                        rows = G[:, q * GT:(q + 1) * GT, :]
                        eng.tensor_tensor(rows[:, :, 0:D].rearrange("p t (h c) -> p t h c", h=HEADS),
                                          rows[:, :, 0:D].rearrange("p t (h c) -> p t h c", h=HEADS),
                                          p.unsqueeze(3).broadcast_to([P, GT, HEADS, D // HEADS]), ALU.mult)
                        eng.tensor_copy(rows[:, :, D:TW], p)
                        eng.tensor_copy(O[:, b, :, TW:RW], tb[:, b, GH:2 * GH].rearrange("p (t h) -> p t h", h=HEADS))
                        for k in range(GT):
                            last_ = eng.scalar_tensor_tensor(same[:, b, k, :], dstbuf[:, q, k * P:(k + 1) * P],
                                                             DSTF[:, ds(g * GT + k, 1)], upto[:, :], ALU.is_equal, ALU.mult)
                        last_.then_inc(masked, 1)

                    pipelined(NG, SETS, eng, (score_step, 1), (weight_step, 0))

                @block.scalar
                def _(eng):
                    eng.sem_inc(moved, 4)
                    eng.sem_inc(o_free, 2)
                    eng.sem_inc(spread, 2)

                    def pack(g, q, turn):
                        got[q].arrived(eng, turn * GT + GT)
                        eng.wait_ge(turned, g + 1)
                        eng.activation(elbuf[:, q % 2, :].rearrange("p (t h) -> p t h", h=HEADS),
                                       G[:, q * GT:(q + 1) * GT, D:TW], ACT.Copy).then_inc(packed, 1)

                    def exp_step(g, q, turn):
                        eng.wait_ge(scored, g + 3)
                        eng.activation(prob[SL, q % 2, :], score[SL, q % 2, :], ACT.Exp).then_inc(expd, 1)

                    def move(g, q, turn):
                        eng.wait_ge(o_free, g + 1)
                        for k in range(GT):
                            eng.wait_ge(made, g * 4 + (k + 9))
                            eng.activation(O[:, q % 2, k, 0:TW], po[:, k, 0:TW], ACT.Copy).then_inc(moved, 1)

                    pipelined(NG, SETS, eng, (pack, 2), (exp_step, 1), (move, 0))
            for q in range(SETS):
                got[q].close(GT * ((NG - q + SETS - 1) // SETS))


        def attention_carry():
            at = [0]
            rows, key_all, same_t, prod_t, s8, res = carve(
                YBASE, ((4, RW), F32), ((ET,), F32), ((10, CHK), F32), ((2, 4, HEADS), F32), ((3, ET + 2), F32), ((4, RW), F32))
            H8 = slice(0, HEADS)
            CS = slice(0, CHK)
            rev = slice(None, None, -1)
            pairs = [(a_, c_) for c_ in range(4) for a_ in range(c_ + 1)]
            with Stage(nc, "car") as st:
                names = ("loaded", "chain", "turned", "back", "expd", "weighted", "made", "moved", "stored", "maxed", "scored")
                loaded, chain, turned, back, expd, weighted, made, moved, stored, maxed, scored = (st.sem(n) for n in names)
                t8 = st.stack.enter_context(nc.psum_tensor("car_8", [P, 512], F32))
                tk = st.stack.enter_context(nc.psum_tensor("car_k", [P, 512], F32))
                po = st.stack.enter_context(nc.psum_tensor("car_o", [P, 4, 512], F32))
                block = st.block()

                @block.sync
                def _(eng):
                    eng.dma_start(rows[CS], PA[0:EP, :].rearrange("(c p e) d -> p c e d", c=4, e=P)[:, :, P - 1, :]).then_inc(loaded, 16)
                    eng.dma_start(key_all[CS, :], last_key.broadcast_to([CHK, ET])).then_inc(loaded, 16)
                    eng.wait_ge(moved, 5)
                    eng.dma_start(CR[0:ET, :].rearrange("(c p) d -> p c d", c=4), res[CS]).then_inc(stored, 16)
                    eng.wait_ge(stored, 16)

                @block.tensor
                def _(eng):
                    eng.wait_ge(loaded, 32)
                    for c in range(4):
                        last_ = eng.transpose(t8[H8, c * CHK:(c + 1) * CHK], rows[CS, c, TW:RW], ident[CS, CS])
                    last_.then_inc(turned, 1)
                    eng.wait_ge(maxed, 1)
                    for c in range(4):
                        last_ = eng.transpose(tk[CS, c * HEADS:(c + 1) * HEADS], s8[H8, 2, c * CHK:(c + 1) * CHK], ident[H8, H8])
                    last_.then_inc(back, 1)
                    eng.wait_ge(weighted, 1)
                    for n, (a_, c_) in enumerate(pairs):
                        last_ = eng.matmul(po[CS, c_, 0:TW], same_t[CS, n, :], rows[CS, a_, 0:TW], start=a_ == 0, stop=a_ == c_)
                    last_.then_inc(made, 1)

                @block.scalar
                def _(eng):
                    eng.wait_ge(scored, 1)
                    eng.activation(prod_t[CS, 0], z4[:, 2], ACT.Exp).then_inc(expd, 1)
                    eng.wait_ge(made, 1)
                    for c in range(4):
                        eng.activation(res[CS, c, 0:TW], po[CS, c, 0:TW], ACT.Copy).then_inc(moved, 1)

                @block.vector
                def _(eng):
                    c = Count(eng, chain)
                    eng.wait_ge(loaded, 32)
                    c.link(eng.tensor_tensor(s8[H8, 0, 1:ET], key_all[H8, 1:ET], key_all[H8, 0:ET - 1], ALU.not_equal))
                    c.link(eng.tensor_scalar(s8[H8, 0, 1:ET], s8[H8, 0, 1:ET], LOW, None, ALU.mult))
                    c.inc(eng.memset(s8[H8, 0, 0:1], LOW))
                    c.inc(eng.memset(s8[H8, 0, ET:ET + 2], LOW))
                    for n, (a_, c_) in enumerate(pairs):
                        there = key_all[CS, c_ * CHK:(c_ + 1) * CHK]
                        c.inc(eng.scalar_tensor_tensor(same_t[CS, n, :], there, tile_key[:, 1, a_:a_ + 1],
                                                       upto[CS, CS] if a_ == c_ else ones[CS, CS], ALU.is_equal, ALU.mult))
                    c.wait()
                    eng.wait_ge(turned, 1)
                    c.link(eng.tensor_tensor_scan(s8[H8, 1, 0:ET], s8[H8, 0, 0:ET], t8[H8, 0:ET], LOW, ALU.add, ALU.max))
                    c.link(eng.tensor_tensor_scan(s8[H8, 2, 0:ET][:, rev],
                                                  s8[H8, 0, 1:ET + 1][:, rev], s8[H8, 1, 0:ET][:, rev], LOW, ALU.add, ALU.max))
                    eng.sem_inc(maxed, 1)
                    eng.wait_ge(back, 1)
                    mk = tk[CS, 0:4 * HEADS].rearrange("p (c h) -> p c h", h=HEADS)
                    eng.tensor_copy(res[CS, :, TW:RW], mk).then_inc(moved, 1)
                    er = tile_er[:, 1]
                    c.inc(eng.tensor_tensor(z4[:, 0], rows[CS, :, TW:RW], er, ALU.add))
                    c.link(eng.tensor_tensor(z4[:, 1], mk, er, ALU.add))
                    c.link(eng.scalar_tensor_tensor(z4[:, 2:4], z4[:, 0:2], 0.2, z4[:, 0:2], ALU.mult, ALU.max))
                    c.link(eng.tensor_tensor(z4[:, 2], z4[:, 2], z4[:, 3], ALU.subtract))
                    eng.sem_inc(scored, 1)
                    eng.wait_ge(expd, 1)
                    w = prod_t[CS, 0]
                    c.inc(eng.tensor_tensor(rows[CS, :, 0:D].rearrange("p c (h d) -> p c h d", h=HEADS),
                                            rows[CS, :, 0:D].rearrange("p c (h d) -> p c h d", h=HEADS),
                                            w.unsqueeze(3).broadcast_to([CHK, 4, HEADS, D // HEADS]), ALU.mult))
                    c.inc(eng.tensor_tensor(rows[CS, :, D:TW], rows[CS, :, D:TW], w, ALU.mult))
                    c.wait()
                    eng.sem_inc(weighted, 1)

        def attention_combine():
            with Stage(nc, "comb") as st:
                chain, expd, scored = (st.sem(n) for n in ("chain", "expd", "scored"))
                got = gathered[0]
                m4, z_, l_, e_, den = carve(WORK, ((4, NT, HEADS), F32), ((4, NT, HEADS), F32), ((4, NT, HEADS), F32),
                                            ((4, NT, HEADS), F32), ((2, NT, HEADS), F32))
                block = st.block()

                @block.gpsimd
                def _(eng):
                    for t in range(NT):
                        eng.indirect_dma_start(YW[:, t, :], None, PA, bass.IndirectOffsetOnAxis(ap=end_sum[:, t:t + 1], axis=0)).then_inc(got.sem, 16)
                        eng.indirect_dma_start(AGW[:, t, :], None, CR, bass.IndirectOffsetOnAxis(ap=carry_row[:, t:t + 1], axis=0)).then_inc(got.sem, 16)

                @block.scalar
                def _(eng):
                    eng.wait_ge(scored, 1)
                    eng.activation(e_[:, 0:3], z_[:, 0:3], ACT.Exp).then_inc(expd, 1)

                @block.vector
                def _(eng):
                    c = Count(eng, chain)
                    er = C[:, :, TW:RW]
                    got.arrived(eng, 2 * NT)
                    c.inc(eng.tensor_copy(m4[:, 0], YW[:, :, TW:RW]))
                    c.inc(eng.tensor_copy(m4[:, 1], AGW[:, :, TW:RW]))
                    c.link(eng.tensor_copy(m4[:, 2], C[:, :, D:TW]))
                    c.link(eng.tensor_tensor(m4[:, 3], m4[:, 0], m4[:, 1], ALU.max))
                    c.link(eng.tensor_tensor(m4[:, 3], m4[:, 3], m4[:, 2], ALU.max))
                    for k in range(4):
                        c.inc(eng.tensor_tensor(z_[:, k], m4[:, k], er, ALU.add))
                    c.wait()
                    c.link(eng.scalar_tensor_tensor(l_[:, :], z_[:, :], 0.2, z_[:, :], ALU.mult, ALU.max))
                    for k in range(3):
                        c.inc(eng.tensor_tensor(z_[:, k], l_[:, k], l_[:, 3], ALU.subtract))
                    c.wait()
                    eng.sem_inc(scored, 1)
                    eng.wait_ge(expd, 1)
                    c.inc(eng.tensor_tensor(l_[:, 0], e_[:, 0], YW[:, :, D:TW], ALU.mult))
                    c.link(eng.tensor_tensor(l_[:, 1], e_[:, 1], AGW[:, :, D:TW], ALU.mult))
                    c.link(eng.tensor_tensor(den[:, 0], l_[:, 0], l_[:, 1], ALU.add))
                    c.link(eng.tensor_tensor(den[:, 0], den[:, 0], e_[:, 2], ALU.add))
                    c.link(eng.tensor_scalar(den[:, 0], den[:, 0], 1e-16, None, ALU.add))
                    c.link(eng.reciprocal(den[:, 1], den[:, 0]))
                    for k in range(3):
                        c.inc(eng.tensor_tensor(e_[:, k], e_[:, k], den[:, 1], ALU.mult))
                    c.wait()
                    for k, part in enumerate((YW, AGW, C)):
                        v = part[:, :, 0:D].rearrange("p t (h d) -> p t h d", h=HEADS)
                        c.link(eng.tensor_tensor(v, v, e_[:, k].unsqueeze(3).broadcast_to([P, NT, HEADS, D // HEADS]), ALU.mult))
                        c.link(eng.tensor_tensor(X[:, :, :], X[:, :, :], part[:, :, 0:D], ALU.add))
            got.close(2 * NT)


        def flow_l2():
            def out2(eng, t, slot, ps, done):
                eng.tensor_copy(tile_of(C[:, :, D:RW], t), ps[:, D:D + 2 * HEADS]).then_inc(done, 1)
            node_products("n5", stage_copy(X), W2, copy_to(C[:, :, 0:D]), WA, out2, table=(C[:, :, 0:TW], T2), table2=(C[:, :, TW:RW], ERT))
            attention_er()
            attention_pass()
            attention_carry()
            attention_combine()
            layer_norm("ln2", none)

        def flow_l3():
            for l in range(LAYERS):
                def out2(eng, t, slot, ps, done):
                    eng.tensor_copy(tile_of(C[:, :, 0:D], t), ps[:, D:2 * D]).then_inc(done, 1)
                node_products(f"n{6 + l}", stage_copy(X) if l == 0 else stage_relu(Y), TH3[:, l], copy_to(AGG),
                              DF3[:, l], out2, table=(AGG, T))
                edge_pass(f"e{5 + l}", BYSRC, (ALU.add, ALU.max), low_src, False)
                batch_norm(f"bn{l}", l, gather=(PR, end_src))
            layer_norm("ln3", last, out_rows=out)

        build_flow = dict(locals())
        run(build_flow)


def run(f):
    f["constants"]()
    f["weights"]()
    f["edge_columns"]()
    f["histogram"](0, f["DSTF"])
    f["histogram"](1, f["SRCF"])
    if STOP > 0:
        f["node_indices"]()
    if STOP > 1:
        f["flow_l0"]()
    if STOP > 2:
        f["flow_l1"]()
    if STOP > 3:
        f["attention_masks"]()
        f["flow_l2"]()
    if STOP > 4:
        f["flow_l3"]()


STOP = 9


INPUTS = ["x", "src", "dst", "edge_weight",
          "L0_gnn_fc_w", "L0_gnn_fc_b", "L0_gnn_ch_w", "L0_gnn_ch_b", "L0_gnn_mlp_w", "L0_gnn_mlp_b",
          "L1_gnn_theta_w", "L1_gnn_theta_b", "L1_gnn_phi_w", "L1_gnn_phi_b",
          "L2_gnn_W", "L2_gnn_a_left", "L2_gnn_a_right",
          "L3_gnn_thetas", "L3_gnn_phis", "L3_gnn_gammas", "L3_gnn_betas"]


def kernel(**inputs):
    import numpy as np
    import concourse.bacc as bacc
    from concourse.bass_utils import run_bass_kernel_spmd

    nc = bacc.Bacc("TRN2", target_bir_lowering=False, num_devices=1)
    arrays, a = {}, {}
    for name in INPUTS:
        v = np.ascontiguousarray(inputs[name])
        arrays[f"in_{name}"] = v
        a[name] = nc.dram_tensor(f"in_{name}", v.shape, mybir.dt.from_np(v.dtype), kind="ExternalInput").ap()
    out = nc.dram_tensor("out_0", (N, D), F32, kind="ExternalOutput").ap()
    build(nc, a, out)
    r = run_bass_kernel_spmd(nc, [arrays], core_ids=[0])
    return r.results[0]["out_0"]
```

```python
import concourse.bass as bass
from concourse import mybir
from contextlib import ExitStack, contextmanager

F32 = mybir.dt.float32
BF16 = mybir.dt.bfloat16
F16 = mybir.dt.float16
I32 = mybir.dt.int32
ALU = mybir.AluOpType
ACT = mybir.ActivationFunctionType
AX = mybir.AxisListType
ds = bass.ds

P = 128
N = 3125
E = 50000
D = 256
NT = (N + P - 1) // P
NP = NT * P
LAST = N - (NT - 1) * P
GT = 4
NG = -(-E // (P * GT))
SETS = 6
ET = NG * GT
EP = ET * P
ROW_ZERO = EP
ROW_LOW = EP + 1
LOW = -1e38
HEADS = 8
TW = D + HEADS
RW = D + 2 * HEADS
LO = 32
HI = -(-(N + 1) // LO)
LAYERS = 3
NODE_UNROLL = 5
EPS = 1e-5
OOB = 60000.0


class Count:

    def __init__(self, eng, sem):
        self.eng, self.sem, self.n, self.turn, self.per, self.at = eng, sem, 0, 0, 0, 0

    def inc(self, ins):
        self.n += 1
        ins.then_inc(self.sem, 1)
        return ins

    def value(self):
        return self.turn * self.per + self.n if self.per else self.n

    def wait(self):
        self.eng.wait_ge(self.sem, self.value())

    def link(self, ins):
        self.inc(ins)
        self.wait()

    @contextmanager
    def loop(self, turns, per):
        start = self.n
        with self.eng.Fori(0, turns) as i:
            self.turn, self.per = i, per
            yield i
            assert self.n - start == per, (self.n, start, per)
        self.turn, self.per, self.n = 0, 0, start + turns * per


def pipelined(total, unroll, eng, *steps):
    most = max(lead for _, lead in steps)
    turns = (total - max(most, 3)) // unroll

    def straight(s):
        for fn, lead in steps:
            if 0 <= s + lead < total:
                fn(s + lead, (s + lead) % unroll, (s + lead) // unroll)

    for s in range(-most, 0):
        straight(s)
    with eng.Fori(0, turns) as i:
        for j in range(unroll):
            for fn, lead in steps:
                fn(i * unroll + (j + lead), (j + lead) % unroll, i + (j + lead) // unroll)
    for s in range(turns * unroll, total):
        straight(s)


class Gathered:

    def __init__(self, sem):
        self.sem, self.before = sem, 0

    def arrived(self, eng, dmas):
        eng.wait_ge(self.sem, dmas * 16 + self.before)

    def close(self, dmas):
        self.before += 16 * dmas


class Stage:

    used = []
    def __init__(self, nc, name):
        self.nc, self.name, self.stack, self.sems = nc, name, ExitStack(), []

    def sem(self, name):
        self.sems.append(self.stack.enter_context(self.nc.semaphore(f"{self.name}_{name}")))
        return self.sems[-1]

    def __enter__(self):
        return self

    def block(self):
        block = self.stack.enter_context(self.nc.Block())
        before, Stage.used = Stage.used, sorted(s.num for s in self.sems)
        assert not set(before) & set(Stage.used)

        @block.gpsimd
        def _(eng):
            while before:
                n = 1
                while n < len(before) and before[n] == before[0] + n:
                    n += 1
                eng.sem_clear(range(before[0], before[0] + n))
                del before[:n]

        return block

    def __exit__(self, *a):
        return self.stack.__exit__(*a)


def build(nc, a, out):
    top = ExitStack()
    Stage.used = []
    with top:
        gathered = [Gathered(top.enter_context(nc.semaphore(f"gathered_{k}"))) for k in range(SETS)]
        def sb(name, shape, dt=F32):
            return top.enter_context(nc.sbuf_tensor(name, shape, dt))

        def dram(name, shape, dt=F32):
            return nc.dram_tensor(name, shape, dt).ap()

        def carve(base, *wanted):
            at, made = 0, []
            for shape, dt in wanted:
                n = 1
                for k in shape:
                    n *= k
                words = n if dt in (F32, I32) else -(-n // 2)
                v = base[:, at:at + words]
                if dt != F32:
                    v = v.bitcast(dt)
                names = "abcd"[:len(shape)]
                if len(shape) > 1:
                    v = v.rearrange(f"p ({' '.join(names)}) -> p {' '.join(names)}", **dict(zip(names, shape)))
                made.append(v)
                at += words
            assert at <= base.shape[1], (at, base.shape)
            return made

        X = sb("X", [P, NT, D])
        ARENA = sb("ARENA", [P, NT * 3 * RW])
        AGW_BASE = ARENA[:, 0:NT * RW]
        AGW = AGW_BASE.rearrange("p (t d) -> p t d", d=RW)
        AGG = AGW[:, :, 0:D]
        C = ARENA[:, NT * RW:NT * 2 * RW].rearrange("p (t d) -> p t d", d=RW)
        YBASE = ARENA[:, NT * 2 * RW:NT * 3 * RW]
        YW = YBASE[:, :].rearrange("p (t d) -> p t d", d=RW)
        Y = YW[:, :, 0:D]
        WORK = sb("WORK", [P, SETS * GT * TW + 4 * GT * P + 2 * GT * RW])
        G, S, O = carve(WORK, ((SETS * GT, TW), F32), ((2, 2, GT * P), F32), ((2, GT, RW), F32))
        SBASE = WORK[:, SETS * GT * TW:SETS * GT * TW + 4 * GT * P]
        R, XT, TMP, TMP2 = carve(WORK, *[((NODE_UNROLL, D), F32)] * 4)
        HB = 14
        RB = GT
        HIST, key_hi, key_lo = carve(ARENA[:, NT * RW:NT * 3 * RW], ((ET, LO), F32), ((ET,), F32), ((ET,), F32))
        oh_hi, oh_lo, = carve(AGW_BASE, ((2, HB, HI), BF16), ((2, HB, LO), BF16))
        rank_hi, rank_lo, rank_t, rank_tf, rank_tmp, sel, rank = carve(
            AGW_BASE, ((2, RB, HI), BF16), ((2, RB, LO), BF16), ((2, 2, RB * P), BF16), ((2, RB * P), F32),
            ((RB, P), BF16), ((RB, LO), F32), ((2, RB), F32))
        place_hi, place_lo, pay_hi, pay_lo, oh_place, oh_pay, no_places, digit_tmp = carve(
            YBASE, *[((ET,), F32)] * 4, ((2, GT, ET), BF16), ((2, GT, 2, P), BF16), ((P + ET,), BF16), ((3, ET), I32))
        key_tmp, iota_i, SRCF = carve(WORK, ((3, ET), I32), ((ET,), I32), ((ET,), F32))
        idxbuf = sb("idxbuf", [P, SETS, GT], I32)
        wbuf = sb("wbuf", [P, SETS, GT])
        maskbuf = sb("maskbuf", [P, SETS, GT * P], BF16)
        ident = sb("ident", [P, P])
        identb = sb("identb", [P, P], BF16)
        ones = sb("ones", [P, P])
        before = sb("before", [P, P])
        upto = sb("upto", [P, P])
        iota_b = sb("iota_b", [P, P], BF16)
        iota_h = sb("iota_h", [P, ET], F16)
        GW = sb("GW", [P, LAYERS, 2, D])
        GB = sb("GB", [P, LAYERS, D])
        MW = sb("MW", [P, LAYERS, 2, D])
        TH1, DF1, W2 = sb("TH1", [P, 2, D]), sb("DF1", [P, 2, D]), sb("W2", [P, 2, D])
        WA = sb("WA", [P, 2, 2 * HEADS])
        TH3, DF3 = sb("TH3", [P, LAYERS, 2, D]), sb("DF3", [P, LAYERS, 2, D])
        CHB, MB = sb("CHB", [P, LAYERS, D]), sb("MB", [P, D])
        B1 = sb("B1", [P, D])
        GAM, BET = sb("GAM", [P, LAYERS, D]), sb("BET", [P, LAYERS, D])
        DSTF, WE = sb("DSTF", [P, ET]), sb("WE", [P, ET])
        SRCI, BYSRC = sb("SRCI", [P, ET], I32), sb("BYSRC", [P, ET], I32)
        pos = BYSRC[:, :].bitcast(F32)
        norm_out, norm_in = sb("norm_out", [P, NT]), sb("norm_in", [P, NT])
        end_sum, end_max, end_src = (sb(n, [P, NT], I32) for n in ("end_sum", "end_max", "end_src"))
        first_dst, first_src = sb("first_dst", [P, NT], I32), sb("first_src", [P, NT], I32)
        carry_row = sb("carry_row", [P, NT], I32)
        MV = sb("MV", [P, NT, 2])

        T = dram("table", [NP, D])
        T2 = dram("table_attention", [NP, TW])
        PR = dram("edge_results", [EP + 2, D])
        PA = dram("edge_results_attention", [EP + 1, RW])
        CR = dram("carry_rows", [ET + 1, RW])
        ERT = dram("er_table", [NP, HEADS])
        ERE = dram("er_edges", [EP, HEADS])
        nst_dst = dram("nst_dst", [1, EP + P], BF16)
        low_dst = dram("low_dst", [1, EP + P], BF16)
        low_src = dram("low_src", [1, EP + P], BF16)
        dst_row = dram("dst_row", [1, EP])
        flag_dst, flag_src = dram("flag_dst", [EP, 1]), dram("flag_src", [EP, 1])
        hist_start, hist_count = dram("hist_start", [2, NP]), dram("hist_count", [2, NP])

        def constants():
            with Stage(nc, "cst") as st:
                zeroed, filled, done = st.sem("zeroed"), st.sem("filled"), st.sem("done")
                copied = st.sem("copied")
                block = st.block()

                @block.gpsimd
                def _(eng):
                    eng.memset(ident[:, :], 0.0).then_inc(zeroed, 1)
                    eng.memset(ones[:, :], 1.0).then_inc(zeroed, 1)
                    eng.iota(iota_i[:, :], pattern=[[1, ET]], base=0, channel_multiplier=0).then_inc(zeroed, 1)
                    eng.wait_ge(zeroed, 3)
                    eng.affine_select(out=ident[:, :], in_=ident[:, :], compare_op=ALU.not_equal, fill=1.0,
                                      base=0, pattern=[[-1, P]], channel_multiplier=1).then_inc(filled, 1)
                    eng.affine_select(out=before[:, :], in_=ones[:, :], compare_op=ALU.is_gt, fill=0.0,
                                      base=0, pattern=[[1, P]], channel_multiplier=-1).then_inc(filled, 1)
                    eng.affine_select(out=upto[:, :], in_=ones[:, :], compare_op=ALU.is_ge, fill=0.0,
                                      base=0, pattern=[[1, P]], channel_multiplier=-1).then_inc(filled, 1)

                @block.vector
                def _(eng):
                    eng.wait_ge(filled, 3)
                    eng.tensor_copy(identb[:, :], ident[:, :]).then_inc(copied, 1)
                    eng.tensor_copy(iota_b[:, :], iota_i[:, 0:P]).then_inc(copied, 1)
                    eng.tensor_copy(iota_h[:, :], iota_i[:, :]).then_inc(copied, 1)

        def weights_beside():
            fc, ch, mlp, th1, ph1, w2, fcb, fcb_wide, prod, AV = carve(
                WORK[:, 5 * ET:WORK.shape[1]], ((LAYERS * 2, D), F32), ((LAYERS * 2, D), F32), ((2, LAYERS * D), F32),
                ((2, D), F32), ((2, D), F32), ((2, D), F32), ((LAYERS * 2,), F32), ((LAYERS * 2, P), F32),
                ((2, 2, D), F32), ((2, D), F32))
            th3, ph3, B1b = carve(AGW_BASE[:, HB * (HI + LO):NT * RW], ((LAYERS * 2, D), F32), ((LAYERS * 2, D), F32), ((D,), F32))
            turns = [(lambda m, k, l=l: mlp[:, m, l * D + k * P:l * D + k * P + P], MW[:, l]) for l in range(LAYERS)]
            turns += [(lambda m, k: th1[:, m, k * P:k * P + P], TH1[:, :, :]),
                      (lambda m, k: ph1[:, m, k * P:k * P + P], DF1[:, :, :]),
                      (lambda m, k: w2[:, m, k * P:k * P + P], W2[:, :, :])]
            turns += [(lambda m, k, l=l: th3[:, 2 * l + m, k * P:k * P + P], TH3[:, l]) for l in range(LAYERS)]
            turns += [(lambda m, k, l=l: ph3[:, 2 * l + m, k * P:k * P + P], DF3[:, l]) for l in range(LAYERS)]
            banks = len(turns) + 2 * LAYERS

            def load_stage(st):
                loaded, zeroed = st.sem("loaded"), st.sem("zeroed")

                def on_sync(eng):
                    n = 0

                    def load(dst, src):
                        nonlocal n
                        eng.dma_start(dst, src).then_inc(loaded, 16)
                        n += 16

                    load(X[:, 0:NT - 1, :], a["x"][0:(NT - 1) * P, :].rearrange("(t p) d -> p t d", p=P))
                    eng.wait_ge(zeroed, 2)
                    load(X[0:LAST, NT - 1, :], a["x"][(NT - 1) * P:N, :])
                    load(fc, a["L0_gnn_fc_w"].rearrange("l (k p) i -> p (l k) i", p=P))
                    for c in range(4):
                        for l in range(LAYERS):
                            load(ch[64 * (c % 2):64 * (c % 2) + 64, 2 * l + c // 2, 64 * c:64 * c + 64],
                                 a["L0_gnn_ch_w"][l, c])
                    load(mlp, a["L0_gnn_mlp_w"].rearrange("(m p) i -> p m i", p=P))
                    with nc.allow_non_contiguous_dma("a bias across the partitions"):
                        load(fcb, a["L0_gnn_fc_b"].rearrange("l (k p) -> p (l k)", p=P))
                    for dst, name in ((th1, "L1_gnn_theta_w"), (ph1, "L1_gnn_phi_w"), (w2, "L2_gnn_W")):
                        load(dst, a[name].rearrange("(m p) i -> p m i", p=P))
                    for dst, name in ((th3, "L3_gnn_thetas"), (ph3, "L3_gnn_phis")):
                        load(dst, a[name].rearrange("l (m p) i -> p (l m) i", p=P))

                    def spread(dst, src, width):
                        load(dst, src.broadcast_to([P, width]))

                    spread(CHB[:, :, :].rearrange("p l d -> p (l d)"),
                           a["L0_gnn_ch_b"].rearrange("(o l) c d -> o (l c d)", o=1), LAYERS * D)
                    spread(MB[:, :], a["L0_gnn_mlp_b"].rearrange("(o d) -> o d", o=1), D)
                    spread(B1[:, :], a["L1_gnn_theta_b"].rearrange("(o d) -> o d", o=1), D)
                    spread(B1b, a["L1_gnn_phi_b"].rearrange("(o d) -> o d", o=1), D)
                    spread(AV[:, 0, :], a["L2_gnn_a_left"].rearrange("(o h) c -> o (h c)", o=1), D)
                    spread(AV[:, 1, :], a["L2_gnn_a_right"].rearrange("(o h) c -> o (h c)", o=1), D)
                    spread(GAM[:, :, :].rearrange("p l d -> p (l d)"),
                           a["L3_gnn_gammas"].rearrange("(o l) d -> o (l d)", o=1), LAYERS * D)
                    spread(BET[:, :, :].rearrange("p l d -> p (l d)"),
                           a["L3_gnn_betas"].rearrange("(o l) d -> o (l d)", o=1), LAYERS * D)
                    eng.wait_ge(loaded, n)

                def on_gpsimd(eng):
                    eng.memset(X[:, NT - 1, :], 0.0).then_inc(zeroed, 1)
                    eng.memset(ch, 0.0).then_inc(zeroed, 1)

                return dict(sync=on_sync, gpsimd=on_gpsimd)

            def turn_stage(st):
                weights_chain, weights_made, weights_moved = (st.sem(f"weights_{n}") for n in ("chain", "made", "moved"))
                ps = st.stack.enter_context(nc.psum_tensor("w_ps", [P, 4, 512], F32))

                def vector_first(eng):
                    c = Count(eng, weights_chain)
                    c.inc(eng.tensor_tensor(ph1, ph1, th1, ALU.subtract))
                    c.inc(eng.tensor_tensor(ph3, ph3, th3, ALU.subtract))
                    c.inc(eng.tensor_tensor(B1[:, :], B1[:, :], B1b, ALU.add))
                    for q in range(2 * LAYERS):
                        c.inc(eng.tensor_scalar(fcb_wide[:, q, :], ones[:, :], fcb[:, q:q + 1], None, ALU.mult))

                def vector_last(eng):
                    c = Count(eng, weights_chain)
                    c.n = 3 + 2 * LAYERS
                    eng.wait_ge(weights_moved, banks)
                    for s in range(2):
                        c.link(eng.tensor_tensor(prod[:, s], W2[:, :, :],
                                                 AV[:, s:s + 1, :].broadcast_to([P, 2, D]), ALU.mult))
                        c.inc(eng.tensor_reduce(WA[:, :, HEADS * s:HEADS * s + HEADS],
                                                prod[:, s].rearrange("p k (h c) -> p k h c", h=HEADS),
                                                AX.X, ALU.add))

                def on_tensor(eng):
                    eng.wait_ge(weights_chain, 3 + 2 * LAYERS)
                    b = 0
                    for nat, _ in turns:
                        if b >= 4:
                            eng.wait_ge(weights_moved, b - 3)
                        for k in range(2):
                            for m in range(2):
                                last = eng.transpose(ps[:, b % 4, k * D + m * P:k * D + m * P + P], nat(m, k), ident[:, :])
                        last.then_inc(weights_made, 1)
                        b += 1
                    for l in range(LAYERS):
                        eng.wait_ge(weights_moved, b - 3)
                        for m in range(2):
                            for k in range(2):
                                last = eng.matmul(ps[:, b % 4, m * D:m * D + D], fc[:, 2 * l + k, m * P:m * P + P],
                                                  ch[:, 2 * l + k, :], start=k == 0, stop=k == 1)
                        last.then_inc(weights_made, 1)
                        b += 1
                        eng.wait_ge(weights_moved, b - 3)
                        for k in range(2):
                            last = eng.matmul(ps[:, b % 4, 0:D], fcb_wide[:, 2 * l + k, :], ch[:, 2 * l + k, :],
                                              start=k == 0, stop=k == 1)
                        last.then_inc(weights_made, 1)
                        b += 1

                def on_scalar(eng):
                    b = 0
                    for _, dst in turns:
                        eng.wait_ge(weights_made, b + 1)
                        eng.activation(dst, ps[:, b % 4, :].rearrange("p (k d) -> p k d", k=2), ACT.Copy).then_inc(weights_moved, 1)
                        b += 1
                    for l in range(LAYERS):
                        eng.wait_ge(weights_made, b + 1)
                        eng.activation(GW[:, l], ps[:, b % 4, :].rearrange("p (k d) -> p k d", k=2), ACT.Copy).then_inc(weights_moved, 1)
                        b += 1
                        eng.wait_ge(weights_made, b + 1)
                        eng.activation(GB[:, l, :], ps[:, b % 4, 0:D], ACT.Copy).then_inc(weights_moved, 1)
                        b += 1

                return dict(vector_first=vector_first, vector_last=vector_last, tensor=on_tensor, scalar=on_scalar)

            return load_stage, turn_stage

        def edge_columns():
            CH = ET // 4
            whole = E // P - 3 * CH
            part = E % P
            rows_i = ARENA[0:CH, 0:8 * P].bitcast(I32).rearrange("p (s c e) -> p s c e", s=2, c=4)
            rows_f = ARENA[0:CH, 8 * P:20 * P].rearrange("p (s c e) -> p s c e", s=3, c=4)
            zero = ARENA[:, 20 * P:20 * P + 4 * ET]
            sent = ARENA[0:1, 20 * P + 4 * ET:20 * P + 4 * ET + RW]
            low_sent = ARENA[0:1, 20 * P + 4 * ET + RW:20 * P + 4 * ET + RW + D]
            with Stage(nc, "col") as st:
                padded, loaded, cast = st.sem("padded"), st.sem("loaded"), st.sem("cast")
                turned, moved, stored = st.sem("turned"), st.sem("moved"), st.sem("stored")
                zeroed = st.sem("zeroed")
                ps = st.stack.enter_context(nc.psum_tensor("col_ps", [P, 3, 512], F32))
                block = st.block()

                @block.gpsimd
                def _(eng):
                    eng.memset(rows_i, N).then_inc(padded, 1)
                    eng.memset(rows_f[:, 2], 0.0).then_inc(padded, 1)
                    eng.memset(zero, 0.0).then_inc(zeroed, 1)
                    eng.memset(sent, 0.0).then_inc(zeroed, 1)

                @block.sync
                def _(eng):
                    eng.wait_ge(padded, 2)
                    n = 0
                    for s, name, rows in ((0, "src", rows_i[:, 0]), (1, "dst", rows_i[:, 1]), (2, "edge_weight", rows_f[:, 2])):
                        flat = a[name]
                        eng.dma_start(rows[:, 0:3, :], flat[0:3 * CH * P].rearrange("(c p e) -> p c e", c=3, e=P)).then_inc(loaded, 16)
                        eng.dma_start(rows[0:whole, 3, :],
                                      flat[3 * CH * P:(3 * CH + whole) * P].rearrange("(p e) -> p e", e=P)).then_inc(loaded, 16)
                        eng.dma_start(rows[whole:whole + 1, 3, 0:part],
                                      flat[(3 * CH + whole) * P:E].rearrange("(o e) -> o e", o=1)).then_inc(loaded, 16)
                        n += 48
                    eng.wait_ge(zeroed, 2)
                    k = 0
                    for flag in (flag_dst, flag_src):
                        eng.dma_start(flag.rearrange("(p c) o -> p (c o)", p=P), zero[:, 0:ET]).then_inc(stored, 16)
                        k += 16
                    for half in range(2):
                        eng.dma_start(ERE.rearrange("(p c) h -> p (c h)", p=P)[:, half * 4 * ET:(half + 1) * 4 * ET],
                                      zero).then_inc(stored, 16)
                        k += 16
                    for h in (hist_start, hist_count):
                        eng.dma_start(h[:, HI * LO:NP], zero[0:2, 0:NP - HI * LO]).then_inc(stored, 16)
                        k += 16
                    eng.dma_start(PR[ROW_ZERO:ROW_ZERO + 1, :], zero[0:1, 0:D]).then_inc(stored, 16)
                    eng.wait_ge(cast, 2)
                    eng.dma_start(dst_row.rearrange("o (c p e) -> p (o c) e", c=4, e=P), rows_f[:, 1]).then_inc(stored, 16)
                    eng.wait_ge(zeroed, 4)
                    eng.dma_start(PR[ROW_LOW:ROW_LOW + 1, :], low_sent).then_inc(stored, 16)
                    eng.dma_start(PA[ROW_ZERO:ROW_ZERO + 1, :], sent[0:1, :]).then_inc(stored, 16)
                    eng.dma_start(CR[ET:ET + 1, :], sent[0:1, :]).then_inc(stored, 16)
                    eng.wait_ge(stored, k + 16 * 5)

                @block.vector
                def _(eng):
                    eng.wait_ge(zeroed, 2)
                    eng.memset(low_sent, LOW).then_inc(zeroed, 1)
                    eng.memset(sent[0:1, D + HEADS:RW], LOW).then_inc(zeroed, 1)
                    eng.wait_ge(loaded, 144)
                    for s in range(2):
                        eng.tensor_copy(rows_f[:, s], rows_i[:, s]).then_inc(cast, 1)
                    for s, dst in ((0, SRCF), (1, DSTF), (2, WE)):
                        eng.wait_ge(turned, s + 1)
                        eng.tensor_copy(dst[:, :], ps[:, s, 0:ET]).then_inc(moved, 1)
                    eng.wait_ge(moved, 1)
                    eng.tensor_copy(SRCI[:, :], SRCF[:, :]).then_inc(moved, 1)

                @block.tensor
                def _(eng):
                    eng.wait_ge(cast, 2)
                    eng.wait_ge(loaded, 144)
                    for s in range(3):
                        for c in range(4):
                            last = eng.transpose(ps[:, s, c * CH:(c + 1) * CH], rows_f[:, s, c, :], ident[0:CH, 0:CH])
                        last.then_inc(turned, 1)

        def split_key(c, key, hi, lo, tmp):
            c.link(c.eng.tensor_copy(tmp[:, 0], key[:, :]))
            c.inc(c.eng.tensor_scalar(tmp[:, 1], tmp[:, 0], LO.bit_length() - 1, None, ALU.arith_shift_right))
            c.link(c.eng.tensor_scalar(tmp[:, 2], tmp[:, 0], LO - 1, None, ALU.bitwise_and))
            c.inc(c.eng.tensor_copy(hi[:, :], tmp[:, 1]))
            c.link(c.eng.tensor_copy(lo[:, :], tmp[:, 2]))

        count = sb("count", [HI, LO])
        startv = sb("startv", [HI, LO])
        small = sb("small", [HI, LO + 2])

        def one_hot(eng, dst, key, t, n, width):
            return eng.tensor_tensor(dst, key[:, ds(t, n)].unsqueeze(2).broadcast_to([P, n, width]),
                                     iota_b[:, 0:width].unsqueeze(1).broadcast_to([P, n, width]), ALU.is_equal)

        def histogram(which, key, beside):
            steps = ET // HB
            with Stage(nc, f"hist{which}") as st:
                chain, hot, made, moved = (st.sem(n) for n in ("chain", "hot", "made", "moved"))
                passed, stored, rows_done = st.sem("passed"), st.sem("stored"), st.sem("rows")
                ps = st.stack.enter_context(nc.psum_tensor(f"hist{which}_ps", [HI, 2, 512], F32))
                rs = st.stack.enter_context(nc.psum_tensor(f"hist{which}_rs", [HI, 512], F32))
                side = beside(st)
                block = st.block()

                if "gpsimd" in side:
                    @block.gpsimd
                    def _(eng):
                        side["gpsimd"](eng)

                @block.vector
                def _(eng):
                    if "vector_first" in side:
                        side["vector_first"](eng)
                    c = Count(eng, chain)
                    split_key(c, key, key_hi, key_lo, key_tmp)
                    with eng.Fori(0, steps // 2) as i:
                        for b in range(2):
                            eng.wait_ge(made, i * 2 + (b + 1))
                            one_hot(eng, oh_hi[:, b], key_hi, i * (2 * HB) + b * HB, HB, HI).then_inc(hot, 1)
                            one_hot(eng, oh_lo[:, b], key_lo, i * (2 * HB) + b * HB, HB, LO).then_inc(hot, 1)
                    eng.wait_ge(moved, steps + 2)
                    c.link(eng.tensor_reduce(count[:, :], HIST[0:HI].rearrange("p t l -> p l t"), AX.X, ALU.add))
                    c.link(eng.tensor_tensor_scan(small[:, 0:LO], ones[0:HI, 0:LO], count[:, :], 0.0, ALU.mult, ALU.add))
                    c.link(eng.tensor_tensor(startv[:, :], small[:, 0:LO], count[:, :], ALU.subtract))
                    eng.sem_inc(rows_done, 1)
                    eng.wait_ge(rows_done, 2)
                    c.link(eng.tensor_copy(small[:, LO:LO + 1], rs[:, 0:1]))
                    c.link(eng.tensor_scalar(startv[:, :], startv[:, :], small[:, LO:LO + 1], None, ALU.add))
                    eng.sem_inc(rows_done, 1)
                    if "vector_last" in side:
                        side["vector_last"](eng)

                @block.tensor
                def _(eng):
                    eng.sem_inc(made, 2)
                    with eng.Fori(0, steps // 2) as i:
                        for b in range(2):
                            eng.wait_ge(moved, i * 2 + (b + 1))
                            eng.wait_ge(hot, i * 4 + (2 * b + 2))
                            for k in range(HB):
                                last = eng.matmul(ps[:, b, k * LO:(k + 1) * LO], oh_hi[:, b, k, :], oh_lo[:, b, k, :],
                                                  start=True, stop=True)
                            last.then_inc(made, 1)
                    if "tensor" in side:
                        side["tensor"](eng)
                    eng.wait_ge(rows_done, 1)
                    eng.matmul(rs[:, 0:1], before[0:HI, 0:HI], small[:, LO - 1:LO], start=True, stop=True).then_inc(rows_done, 1)

                @block.scalar
                def _(eng):
                    eng.sem_inc(moved, 2)
                    with eng.Fori(0, steps // 2) as i:
                        for b in range(2):
                            eng.wait_ge(made, i * 2 + (b + 3))
                            eng.sem_inc(passed, 1)
                            eng.activation(HIST[0:HI, ds(i * (2 * HB) + b * HB, HB), :],
                                           ps[:, b, 0:HB * LO].rearrange("p (k l) -> p k l", l=LO), ACT.Copy).then_inc(moved, 1)

                    if "scalar" in side:
                        side["scalar"](eng)

                @block.sync
                def _(eng):
                    if "sync" in side:
                        side["sync"](eng)
                    eng.wait_ge(rows_done, 3)
                    eng.dma_start(hist_start[which:which + 1, 0:HI * LO].rearrange("o (h l) -> (o h) l", l=LO), startv[:, :]).then_inc(stored, 16)
                    eng.dma_start(hist_count[which:which + 1, 0:HI * LO].rearrange("o (h l) -> (o h) l", l=LO), count[:, :]).then_inc(stored, 16)
                    eng.wait_ge(stored, 32)
            if which == 1:
                gathered[0].close(NT)

        node_f, flag_cols, mark_cols = carve(AGW_BASE[:, HB * (HI + LO) + (4 * LAYERS + 1) * D:NT * RW], ((6, NT), F32), ((ET,), F32), ((3, ET), BF16))
        START, CNT, HAS, LASTE, T1, T2_ = range(6)

        def load_numbers(eng, w, loaded):
            with nc.allow_non_contiguous_dma("node numbers across the partitions"):
                for k, h in ((START, hist_start), (CNT, hist_count)):
                    eng.dma_start(node_f[:, k, :], h[w:w + 1, :].rearrange("o (t p) -> p (o t)", p=P)).then_inc(loaded, 16)

        def node_numbers(c, w):
            f = node_f
            norm, first = ((norm_in, first_dst), (norm_out, first_src))[w]
            c.inc(c.eng.tensor_scalar(norm[:, :], f[:, CNT, :], 1.0, None, ALU.max))
            c.inc(c.eng.tensor_scalar(f[:, HAS, :], f[:, CNT, :], 1.0, None, ALU.min))
            c.link(c.eng.tensor_tensor(f[:, LASTE, :], f[:, START, :], f[:, CNT, :], ALU.add))
            c.link(c.eng.tensor_scalar(f[:, T1, :], f[:, START, :], -OOB, None, ALU.add))
            c.link(c.eng.tensor_tensor(f[:, T1, :], f[:, T1, :], f[:, HAS, :], ALU.mult))
            c.link(c.eng.tensor_scalar(f[:, T1, :], f[:, T1, :], OOB, None, ALU.add))
            c.link(c.eng.tensor_copy(first[:, :], f[:, T1, :]))
            for row, dst in (((ROW_ZERO, end_sum), (ROW_LOW, end_max)) if w == 0 else ((ROW_LOW, end_src),)):
                c.link(c.eng.tensor_scalar(f[:, T1, :], f[:, LASTE, :], -(row + 1.0), None, ALU.add))
                c.link(c.eng.tensor_tensor(f[:, T1, :], f[:, T1, :], f[:, HAS, :], ALU.mult))
                c.link(c.eng.tensor_scalar(f[:, T1, :], f[:, T1, :], float(row), None, ALU.add))
                c.link(c.eng.tensor_copy(dst[:, :], f[:, T1, :]))
            if w == 0:
                c.link(c.eng.tensor_scalar(f[:, T1, :], f[:, LASTE, :], -1.0, None, ALU.add))
                c.link(c.eng.tensor_scalar(f[:, T1, :], f[:, T1, :], 0.0, None, ALU.max))
                c.link(c.eng.tensor_copy(carry_row[:, :], f[:, T1, :]))
                c.link(c.eng.tensor_scalar(carry_row[:, :], carry_row[:, :], 7, None, ALU.arith_shift_right))
                c.link(c.eng.tensor_copy(f[:, T1, :], carry_row[:, :]))
                c.link(c.eng.tensor_scalar(f[:, T2_, :], f[:, T1, :], float(P), None, ALU.mult))
                c.link(c.eng.tensor_tensor(f[:, T2_, :], f[:, START, :], f[:, T2_, :], ALU.is_lt))
                c.link(c.eng.tensor_tensor(f[:, T2_, :], f[:, T2_, :], f[:, HAS, :], ALU.mult))
                c.link(c.eng.tensor_scalar(f[:, T1, :], f[:, T1, :], -(ET + 1.0), None, ALU.add))
                c.link(c.eng.tensor_tensor(f[:, T1, :], f[:, T1, :], f[:, T2_, :], ALU.mult))
                c.link(c.eng.tensor_scalar(f[:, T1, :], f[:, T1, :], float(ET), None, ALU.add))
                c.link(c.eng.tensor_copy(carry_row[:, :], f[:, T1, :]))

        def mark(eng, first, flag, marked):
            for t in range(NT):
                eng.indirect_dma_start(flag, bass.IndirectOffsetOnAxis(ap=first[:, t:t + 1], axis=0),
                                       ones[:, 0:1], None, bounds_check=EP - 1, oob_is_err=False).then_inc(marked.sem, 16)

        def dst_nodes_beside(st):
            loaded, node_chain, ready, flags_in, marks, rows_stored = (
                st.sem(f"node_{n}") for n in ("loaded", "chain", "ready", "flags_in", "marks", "stored"))
            marked = gathered[0]

            def on_sync(eng):
                load_numbers(eng, 0, loaded)
                marked.arrived(eng, NT)
                eng.dma_start(flag_cols, flag_dst.rearrange("(p c) o -> p (c o)", p=P)).then_inc(flags_in, 16)
                eng.wait_ge(marks, 3)
                for k, row in ((0, nst_dst), (1, low_dst)):
                    eng.dma_start(row[:, 0:EP].rearrange("o (p c) -> (o p) c", p=P), mark_cols[:, k, :]).then_inc(rows_stored, 16)
                for row in (nst_dst, low_dst, low_src):
                    eng.dma_start(row[:, EP:EP + P], mark_cols[0:1, 2, 0:P]).then_inc(rows_stored, 16)
                eng.wait_ge(rows_stored, 80)

            def vector_first(eng):
                eng.wait_ge(loaded, 32)
                node_numbers(Count(eng, node_chain), 0)
                eng.sem_inc(ready, 1)

            def vector_last(eng):
                eng.wait_ge(flags_in, 16)
                eng.tensor_scalar(mark_cols[:, 0, :], flag_cols, -1.0, 1.0, ALU.mult, ALU.add).then_inc(marks, 1)
                eng.tensor_scalar(mark_cols[:, 1, :], flag_cols, LOW, None, ALU.mult).then_inc(marks, 1)
                eng.memset(mark_cols[:, 2, :], 0.0).then_inc(marks, 1)

            def on_gpsimd(eng):
                eng.wait_ge(ready, 1)
                mark(eng, first_dst, flag_dst, marked)

            return dict(sync=on_sync, vector_first=vector_first, vector_last=vector_last, gpsimd=on_gpsimd)

        def src_nodes():
            with Stage(nc, "node") as st:
                loaded, chain, ready, rooted = (st.sem(n) for n in ("loaded", "chain", "ready", "rooted"))
                block = st.block()

                @block.sync
                def _(eng):
                    load_numbers(eng, 1, loaded)
                    eng.wait_ge(loaded, 32)

                @block.vector
                def _(eng):
                    c = Count(eng, chain)
                    for lo in range(LO):
                        c.inc(eng.tensor_tensor_scan(HIST[0:HI, :, lo], ones[0:HI, 0:1].broadcast_to([HI, ET]),
                                                     HIST[0:HI, :, lo], startv[:, lo:lo + 1], ALU.mult, ALU.add))
                    eng.wait_ge(loaded, 32)
                    node_numbers(c, 1)
                    eng.sem_inc(ready, 1)
                    eng.wait_ge(rooted, 2)
                    for norm in (norm_in, norm_out):
                        c.inc(eng.reciprocal(norm[:, :], norm[:, :]))

                @block.scalar
                def _(eng):
                    eng.wait_ge(ready, 1)
                    for norm in (norm_in, norm_out):
                        eng.activation(norm[:, :], norm[:, :], ACT.Sqrt).then_inc(rooted, 1)

        def both_beside(*parts):
            def beside(st):
                made = [part(st) for part in parts]

                def chained(engine):
                    def program(eng):
                        for m in made:
                            if engine in m:
                                m[engine](eng)
                    return program
                return {engine: chained(engine) for m in made for engine in m}
            return beside

        RANKS = -(-(ET // RB) // LAYERS)

        def rank_beside(layer):
            first = layer * RANKS
            steps = min(RANKS, ET // RB - first)

            def beside(st, name):
                names = ("hot", "flipped", "taken", "met", "passed", "ranked")
                hot, flipped, taken, met, passed, ranked = (st.sem(n) for n in names)
                pa = st.stack.enter_context(nc.psum_tensor(f"{name}_ra", [P, 512], F32))
                pb = st.stack.enter_context(nc.psum_tensor(f"{name}_rb", [P, 512], F32))
                turned_hot = pa[:, :].bitcast(BF16).rearrange("p (s e) -> p s e", s=2)

                def at(phase, fn):
                    def step(g, q, turn):
                        if q % 3 == phase and not (isinstance(g, int) and g // 3 >= steps):
                            fn(turn * (SETS // 3) + q // 3, q // 3 % 2)
                    return step

                def on_vector(eng):
                    eng.sem_inc(ranked, 2)

                    def one_hots(k, b):
                        eng.wait_ge(ranked, k + 1)
                        one_hot(eng, rank_hi[:, b], key_hi, (k + first) * RB, RB, HI).then_inc(hot, 1)
                        one_hot(eng, rank_lo[:, b], key_lo, (k + first) * RB, RB, LO).then_inc(hot, 1)

                    def places(k, b):
                        eng.wait_ge(met, k + 3)
                        for n in range(RB):
                            eng.scalar_tensor_tensor(rank_tmp[:, n, :], pb[:, n * P:(n + 1) * P], 2.0, upto[:, :],
                                                     ALU.is_equal, ALU.mult, accum_out=rank[:, 0, n:n + 1]).then_inc(passed, 1)
                        eng.tensor_tensor(sel[:, :, :], pa[:, 0:RB * LO].rearrange("p (k l) -> p k l", l=LO),
                                          rank_lo[:, b], ALU.mult).then_inc(passed, 1)
                        eng.wait_ge(passed, k * 6 + 5)
                        eng.tensor_reduce(rank[:, 1, :], sel[:, :, :], AX.X, ALU.add).then_inc(passed, 1)
                        eng.wait_ge(passed, k * 6 + 6)
                        eng.tensor_tensor(pos[:, ds((k + first) * RB, RB)], rank[:, 1, :], rank[:, 0, :], ALU.subtract).then_inc(ranked, 1)

                    return [(at(1, places), 0)], [(at(0, one_hots), 3)]

                def on_tensor(eng):
                    eng.sem_inc(met, 2)

                    def flip(k, b):
                        eng.wait_ge(hot, k * 2 + 2)
                        eng.wait_ge(ranked, k + 2)
                        for n in range(RB):
                            eng.transpose(turned_hot[0:HI, 0, n * P:(n + 1) * P], rank_hi[:, b, n, :], identb[:, :])
                            last = eng.transpose(turned_hot[0:LO, 1, n * P:(n + 1) * P], rank_lo[:, b, n, :], identb[:, :])
                        last.then_inc(flipped, 1)

                    def meet(k, b):
                        eng.wait_ge(taken, k + 1)
                        for n in range(RB):
                            cols = slice(n * P, (n + 1) * P)
                            eng.matmul(pb[:, cols], rank_t[0:HI, b, 0, cols], rank_t[0:HI, b, 0, cols], start=True, stop=False)
                            eng.matmul(pb[:, cols], rank_t[0:LO, b, 1, cols], rank_t[0:LO, b, 1, cols], start=False, stop=True)
                            last = eng.matmul(pa[:, n * LO:(n + 1) * LO], rank_tf[0:HI, b, cols],
                                              HIST[0:HI, ds((k + first) * RB + n, 1), :].rearrange("p o l -> p (o l)"), start=True, stop=True)
                        last.then_inc(met, 1)

                    return [(at(0, meet), 0)], [(at(0, flip), 2)]

                def on_scalar(eng):
                    def take(k, b):
                        eng.wait_ge(flipped, k + 1)
                        eng.wait_ge(met, k + 1)
                        eng.activation(rank_t[0:HI, b, 0, :], turned_hot[0:HI, 0, :], ACT.Copy)
                        eng.activation(rank_t[0:LO, b, 1, :], turned_hot[0:LO, 1, :], ACT.Copy)
                        eng.activation(rank_tf[0:HI, b, :], turned_hot[0:HI, 0, :], ACT.Copy).then_inc(taken, 1)

                    return [(at(0, take), 1)], []

                return on_vector, on_tensor, on_scalar, None, None
            return beside

        def order_beside(st, name):
            payload, placed, opened, summed, digits_chain = (st.sem(n) for n in ("payload", "placed", "opened", "summed", "digits"))
            sums = [st.stack.enter_context(nc.psum_tensor(f"{name}_{n}", [P, ET], F32)) for n in ("hi", "lo")]

            def digits_of(c, src, shift, hi, lo):
                c.link(c.eng.tensor_copy(digit_tmp[:, 0], src))
                c.inc(c.eng.tensor_scalar(digit_tmp[:, 1], digit_tmp[:, 0], shift, None, ALU.arith_shift_right))
                c.link(c.eng.tensor_scalar(digit_tmp[:, 2], digit_tmp[:, 0], (1 << shift) - 1, None, ALU.bitwise_and))
                c.inc(c.eng.tensor_copy(hi, digit_tmp[:, 1]))
                c.link(c.eng.tensor_copy(lo, digit_tmp[:, 2]))

            def on_vector(eng):
                c = Count(eng, digits_chain)
                digits_of(c, pos, 7, place_hi, place_lo)
                digits_of(c, DSTF[:, :], 6, pay_hi, pay_lo)
                c.link(eng.memset(no_places[:, :], 0.0))
                eng.sem_inc(opened, 1)
                eng.sem_inc(placed, 2)

                def one_hots(g, q, turn):
                    b = q % 2
                    eng.wait_ge(placed, g + 1)
                    for n in range(GT):
                        t = g * GT + n
                        eng.tensor_scalar(oh_place[:, b, n, :], iota_h[:, :], place_hi[:, ds(t, 1)], None, ALU.is_equal)
                        eng.tensor_scalar(oh_pay[:, b, n, 0, :], iota_b[:, :], place_lo[:, ds(t, 1)], pay_hi[:, ds(t, 1)], ALU.is_equal, ALU.mult)
                        last = eng.tensor_scalar(oh_pay[:, b, n, 1, :], iota_b[:, :], place_lo[:, ds(t, 1)], pay_lo[:, ds(t, 1)], ALU.is_equal, ALU.mult)
                    last.then_inc(payload, 1)

                return [], [(one_hots, 1)]

            def on_tensor(eng):
                eng.wait_ge(opened, 1)
                for d in range(2):
                    eng.matmul(sums[d][:, :], no_places[:, 0:P], no_places[:, P:P + ET], start=True, stop=False)

                def place(g, q, turn):
                    eng.wait_ge(payload, g + 1)
                    for n in range(GT):
                        for d in range(2):
                            last = eng.matmul(sums[d][:, :], oh_pay[:, q % 2, n, d, :], oh_place[:, q % 2, n, :], start=False, stop=False)
                    last.then_inc(placed, 1)

                return [], [(place, 0)]

            def on_scalar(eng):
                return [], []

            def vector_end(eng):
                c = Count(eng, digits_chain)
                c.n = 11
                eng.wait_ge(summed, 1)
                c.link(eng.tensor_scalar(place_hi, sums[0][:, :], 64.0, None, ALU.mult))
                c.link(eng.tensor_tensor(place_hi, sums[1][:, :], place_hi, ALU.add))
                c.link(eng.tensor_copy(BYSRC[:, :], place_hi))

            def tensor_end(eng):
                for d in range(2):
                    last = eng.matmul(sums[d][:, :], no_places[:, 0:P], no_places[:, P:P + ET], start=False, stop=True)
                last.then_inc(summed, 1)

            return on_vector, on_tensor, on_scalar, vector_end, tensor_end

        RST, NMR = sb("RST", [P, NT]), sb("NMR", [P, NT])
        BS, MV5 = sb("BS", [P, NODE_UNROLL, 6]), sb("MV5", [P, NODE_UNROLL, 2])
        root, factor, shift = carve(RST[:, 0:3 * NODE_UNROLL], *[((NODE_UNROLL,), F32)] * 3)

        def node_products(name, stage, w1, out1, w2=None, out2=None, gather=None, table=None, table2=None, scatter=None, marks=None,
                          norm=None):
            n2 = 0 if w2 is None else w2.shape[2]
            u = NODE_UNROLL
            with Stage(nc, name) as st:
                names = ("staged", "turned", "xt", "made", "moved", "done", "chain", "passed", "stored", "passed2")
                staged, turned, xt, made, moved, done, chain, passed, stored, passed2 = (st.sem(n) for n in names)
                got = gathered[0:NT // u]
                if norm is not None:
                    added, aggregated, rooted, factors, kept, apart = (
                        st.sem(n) for n in ("added", "aggregated", "rooted", "factors", "kept", "apart"))
                    adds = len(norm) + 1
                tps = st.stack.enter_context(nc.psum_tensor(f"{name}_t", [P, 3, 512], F32))
                mps = st.stack.enter_context(nc.psum_tensor(f"{name}_m", [P, u, 512], F32))
                tp = [tps[:, j % 3, 0:D] for j in range(u)]
                block = st.block()

                scatter_sem = gathered[-1]
                if gather is not None or scatter is not None or marks is not None:
                    @block.gpsimd
                    def _(eng):
                        if gather is not None:
                            rows, index = gather
                            for t in range(NT):
                                got[t % u].arrived(eng, t // u)
                                eng.indirect_dma_start(AGG[:, t, :], None, rows,
                                                       bass.IndirectOffsetOnAxis(ap=index[:, t:t + 1], axis=0)).then_inc(got[t % u].sem, 16)
                        if marks is not None:
                            mark(eng, *marks, scatter_sem)
                        if scatter is not None:
                            source, rows, index = scatter
                            for t in range(NT):
                                eng.wait_ge(done, u + t + 1)
                                eng.indirect_dma_start(rows, bass.IndirectOffsetOnAxis(ap=index[:, t:t + 1], axis=0),
                                                       source[:, t, :], None, bounds_check=EP - 1, oob_is_err=False).then_inc(scatter_sem.sem, 16)
                        if marks is not None or scatter is not None:
                            scatter_sem.arrived(eng, NT)

                @block.vector
                def _(eng):
                    eng.sem_inc(done, u)

                    def add_up(t, slot, turn):
                        if gather is not None:
                            got[slot].arrived(eng, turn + 1)
                        for n, step in enumerate(norm):
                            if n:
                                eng.wait_ge(added, t * adds + n)
                            step(eng, t).then_inc(added, 1)
                        if norm:
                            eng.wait_ge(added, t * adds + len(norm))
                            eng.sem_inc(apart, 1)
                        eng.bn_stats(BS[:, slot, :], tile_of(X, t)).then_inc(added, 1)

                    def aggregate(t, slot, _):
                        eng.wait_ge(added, t * adds + adds)
                        eng.sem_inc(apart, 1)
                        eng.bn_aggr(MV5[:, slot, :], BS[:, slot, :]).then_inc(aggregated, 1)
                        eng.wait_ge(aggregated, t * 2 + 1)
                        eng.tensor_scalar(root[:, slot:slot + 1], MV5[:, slot, 1:2], EPS, None, ALU.add).then_inc(aggregated, 1)

                    def apply(t, slot, _):
                        eng.wait_ge(rooted, t + 1)
                        eng.wait_ge(kept, t + 1)
                        eng.reciprocal(factor[:, slot:slot + 1], root[:, slot:slot + 1]).then_inc(factors, 1)
                        eng.wait_ge(factors, t * 2 + 1)
                        eng.tensor_scalar(shift[:, slot:slot + 1], MV5[:, slot, 0:1], factor[:, slot:slot + 1], -1.0,
                                          ALU.mult, ALU.mult).then_inc(factors, 1)
                        eng.wait_ge(factors, t * 2 + 2)
                        eng.wait_ge(turned, t + 1)
                        eng.tensor_scalar(R[:, slot, :], tile_of(X, t), factor[:, slot:slot + 1], shift[:, slot:slot + 1],
                                          ALU.mult, ALU.add).then_inc(staged, 1)

                    def ahead(t, slot, turn):
                        if gather is not None:
                            got[slot].arrived(eng, turn + 1)
                        eng.wait_ge(turned, t + 1)
                        stage(eng, t, slot, chain, staged)

                    def behind(t, slot, _):
                        eng.wait_ge(moved, t + 1)
                        eng.wait_ge(made, t + 1)
                        out2(eng, t, slot, mps[:, slot, :], done)

                    if norm is None:
                        pipelined(NT, u, eng, (ahead, 2), (behind, 0))
                    else:
                        pipelined(NT, u, eng, (add_up, 5), (apply, 2), (aggregate, 4), (behind, 0))

                @block.tensor
                def _(eng):
                    eng.sem_inc(turned, u)

                    def turn(t, slot, _):
                        eng.wait_ge(staged, t + 1)
                        eng.wait_ge(xt, t + (u - 1))
                        for k in range(2):
                            last = eng.transpose(tp[slot][:, k * P:(k + 1) * P], R[:, slot, k * P:(k + 1) * P], ident[:, :])
                        last.then_inc(turned, 1)

                    def product(t, slot, _):
                        eng.wait_ge(xt, t + (u + 1))
                        eng.wait_ge(done, t + 1)
                        for k in range(2):
                            last = eng.matmul(mps[:, slot, 0:D], XT[:, slot, k * P:(k + 1) * P], w1[:, k, :],
                                              start=k == 0, stop=k == 1)
                        if n2:
                            for k in range(2):
                                last = eng.matmul(mps[:, slot, D:D + n2], XT[:, slot, k * P:(k + 1) * P], w2[:, k, :],
                                                  start=k == 0, stop=k == 1)
                        last.then_inc(made, 1)

                    pipelined(NT, u, eng, (turn, 1), (product, 0))

                @block.scalar
                def _(eng):
                    eng.sem_inc(xt, u)

                    def ahead(t, slot, _):
                        eng.wait_ge(turned, t + (u + 1))
                        eng.wait_ge(made_free, t + 1)
                        eng.activation(XT[:, slot, :], tp[slot], ACT.Copy).then_inc(xt, 1)

                    def behind(t, slot, _):
                        eng.wait_ge(made, t + 1)
                        eng.wait_ge(done, t + 1)
                        eng.sem_inc(passed, 1)
                        out1(eng, t, slot, mps[:, slot, 0:D]).then_inc(moved, 1)

                    made_free = done

                    def square_root(t, slot, _):
                        eng.wait_ge(aggregated, t * 2 + 2)
                        eng.activation(root[:, slot:slot + 1], root[:, slot:slot + 1], ACT.Sqrt).then_inc(rooted, 1)

                    def keep(t, slot, _):
                        eng.wait_ge(staged, t + 1)
                        eng.activation(tile_of(X, t), tile_of(X, t), ACT.Identity,
                                       bias=shift[:, slot:slot + 1], scale=factor[:, slot:slot + 1]).then_inc(kept, 1)

                    if norm is None:
                        pipelined(NT, u, eng, (ahead, 1), (behind, 0))
                    else:
                        eng.sem_inc(kept, u)
                        pipelined(NT, u, eng, (square_root, 3), (ahead, 1), (keep, 1), (behind, 0))

                tables = [x for x in (table, table2) if x is not None]
                if tables:
                    @block.sync
                    def _(eng):
                        for k in range(NT // u):
                            eng.wait_ge(done, u + (k + 1) * u)
                            for src, dst in tables:
                                eng.dma_start(dst[k * u * P:(k + 1) * u * P, :].rearrange("(t p) d -> p t d", p=P),
                                              src[:, k * u:(k + 1) * u, :]).then_inc(stored, 16)
                        eng.wait_ge(stored, NT // u * 16 * len(tables))
            if gather is not None:
                for g in got:
                    g.close(NODE_UNROLL)
            if scatter is not None or marks is not None:
                scatter_sem.close(NT)


        def tile_of(view, t):
            return view[:, ds(t, 1), :].rearrange("p o d -> p (o d)") if not isinstance(t, int) else view[:, t, :]

        def stage_copy(src):
            def stage(eng, t, slot, chain, staged):
                eng.tensor_copy(R[:, slot, :], tile_of(src, t)).then_inc(staged, 1)
            return stage

        def stage_gcn(layer):
            def stage(eng, t, slot, chain, staged):
                eng.scalar_tensor_tensor(TMP2[:, slot, :], tile_of(AGG, t), norm_in[:, ds(t, 1)], CHB[:, layer, :],
                                         ALU.mult, ALU.add).then_inc(chain, 1)
                eng.wait_ge(chain, t + 1)
                eng.tensor_scalar(R[:, slot, :], TMP2[:, slot, :], 0.0, None, ALU.max).then_inc(staged, 1)
            return stage

        def gcn_table(layer, with_mlp):
            def out1(eng, t, slot, ps):
                return eng.activation(TMP[:, slot, :], ps, ACT.Copy, scale=norm_out[:, ds(t, 1)])

            def out2(eng, t, slot, ps, done):
                if with_mlp:
                    eng.tensor_tensor(tile_of(X, t), ps[:, D:2 * D], tile_of(X, t), ALU.add)
                eng.scalar_tensor_tensor(tile_of(AGG, t), GB[:, layer, :], norm_out[:, ds(t, 1)], TMP[:, slot, :],
                                         ALU.mult, ALU.add).then_inc(done, 1)
            return out1, out2

        def nothing_beside(st, name):
            def steps(eng):
                return [], []
            return steps, steps, steps, None, None

        def edge_pass(name, index, ops, mask, weighted, beside=nothing_beside):
            op0, op1 = ops
            with Stage(nc, name) as st:
                got = gathered
                ready = [st.sem(f"ready{q}") for q in range(SETS)]
                names = ("scaled", "turned", "scanned", "back", "pairs", "o_free", "stored", "go_pool", "go_act", "go_sp")
                scaled, turned, scanned, back, pairs, o_free, stored, go_pool, go_act, go_sp = (st.sem(n) for n in names)
                fm = st.stack.enter_context(nc.psum_tensor(f"{name}_fm", [P, 2, 2, GT * P], F32))
                em = st.stack.enter_context(nc.psum_tensor(f"{name}_em", [P, 2, 2, D], F32))
                on_vector, on_tensor, on_scalar, vector_end, tensor_end = beside(st, name)
                out_rows = PR[0:EP, :].rearrange("(t p) d -> p t d", p=P)
                uses = 3 if weighted else 2
                block = st.block()

                @block.sync
                def _(eng):
                    def prefetch(g, q):
                        eng.dma_start(idxbuf[:, q, :], index[:, ds(g * GT, GT)]).then_inc(ready[q], 16)
                        eng.dma_start(maskbuf[:, q, :], mask[0:1, ds(g * (GT * P), GT * P)].broadcast_to([P, GT * P])).then_inc(ready[q], 16)
                        if weighted:
                            eng.dma_start(wbuf[:, q, :], WE[:, ds(g * GT, GT)]).then_inc(ready[q], 16)

                    for q in range(SETS):
                        prefetch(q, q)

                    def store(g, q):
                        eng.wait_ge(pairs, g * 2 + 6)
                        eng.sem_inc(go_sp, 1)
                        eng.dma_start(out_rows[:, ds(g * GT, GT), :], O[:, q % 2, :, 0:D]).then_inc(stored, 16)
                        if not isinstance(g, int) or g + SETS < NG:
                            prefetch(g + SETS, q)
                        eng.wait_ge(stored, g * 16 + 16)
                        eng.sem_inc(o_free, 1)

                    with eng.Fori(0, (NG - SETS) // SETS) as i:
                        for q in range(SETS):
                            store(i * SETS + q, q)
                    for g in range((NG - SETS) // SETS * SETS, NG):
                        store(g, g % SETS)

                @block.gpsimd
                def _(eng):
                    def gather(g, q, turn):
                        eng.wait_ge(ready[q], turn * (16 * uses) + 16 * uses)
                        eng.sem_inc(go_pool, 1)
                        for k in range(GT):
                            eng.indirect_dma_start(G[:, q * GT + k, 0:D], None, T,
                                                   bass.IndirectOffsetOnAxis(ap=idxbuf[:, q, k:k + 1], axis=0)).then_inc(got[q].sem, 16)

                    pipelined(NG, SETS, eng, (gather, 0))

                @block.tensor
                def _(eng):
                    def forth(g, q, turn):
                        if weighted:
                            eng.wait_ge(scaled, g + 1)
                        else:
                            got[q].arrived(eng, turn * GT + GT)
                        eng.wait_ge(scanned, g + 1)
                        for k in range(GT):
                            for h in range(2):
                                last = eng.transpose(fm[:, q % 2, h, k * P:(k + 1) * P], G[:, q * GT + k, h * P:(h + 1) * P], ident[:, :])
                        last.then_inc(turned, 1)

                    def hither(g, q, turn):
                        eng.wait_ge(scanned, g + 3)
                        for pair in range(2):
                            eng.wait_ge(pairs, g * 2 + (pair + 3))
                            for k in range(2):
                                for h in range(2):
                                    last = eng.transpose(em[:, pair, k, h * P:(h + 1) * P],
                                                         S[:, q % 2, h, (2 * pair + k) * P:(2 * pair + k + 1) * P], ident[:, :])
                            last.then_inc(back, 1)

                    early, late = on_tensor(eng)
                    pipelined(NG, SETS, eng, *early, (forth, 1), (hither, 0), *late)
                    if tensor_end:
                        tensor_end(eng)

                @block.vector
                def _(eng):
                    eng.memset(S[:, 1, :, GT * P - 1:GT * P], 0.0).then_inc(scanned, 1)
                    eng.wait_ge(scanned, 1)
                    eng.sem_inc(scanned, 1)

                    def scan(g, q, turn):
                        eng.wait_ge(turned, g + 1)
                        eng.wait_ge(pairs, g * 2 + 2)
                        eng.wait_ge(scanned, g + 2)
                        for h in range(2):
                            last = eng.tensor_tensor_scan(S[:, q % 2, h, :], maskbuf[:, q, :], fm[:, q % 2, h, :],
                                                          S[:, 1 - q % 2, h, GT * P - 1:GT * P], op0, op1)
                        last.then_inc(scanned, 1)

                    early, late = on_vector(eng)
                    pipelined(NG, SETS, eng, *early, (scan, 0), *late)
                    if vector_end:
                        vector_end(eng)

                @block.scalar
                def _(eng):
                    eng.sem_inc(pairs, 4)
                    eng.sem_inc(o_free, 2)

                    def scale(g, q, turn):
                        got[q].arrived(eng, turn * GT + GT)
                        for k in range(GT):
                            last = eng.activation(G[:, q * GT + k, 0:D], G[:, q * GT + k, 0:D], ACT.Copy, scale=wbuf[:, q, k:k + 1])
                        last.then_inc(scaled, 1)

                    def evac(g, q, turn):
                        eng.wait_ge(o_free, g + 1)
                        for pair in range(2):
                            eng.wait_ge(back, g * 2 + (pair + 1))
                            eng.activation(O[:, q % 2, 2 * pair:2 * pair + 2, 0:D], em[:, pair], ACT.Copy).then_inc(pairs, 1)

                    early, late = on_scalar(eng)
                    scaling = [(scale, 2)] if weighted else []
                    pipelined(NG, SETS, eng, *early, *scaling, (evac, 0), *late)
            for q in range(SETS):
                got[q].close(GT * ((NG - q + SETS - 1) // SETS))



        def layer_norm(name, prepare, gather=None, out_rows=None):
            u = NODE_UNROLL
            with Stage(nc, name) as st:
                names = ("chain", "aggregated", "rooted", "scaled", "done", "stored", "apart")
                chain, aggregated, rooted, scaled, done, stored, apart = (st.sem(n) for n in names)
                got = gathered[0:NT // u]
                block = st.block()

                if gather is not None:
                    @block.gpsimd
                    def _(eng):
                        rows, index = gather
                        for t in range(NT):
                            got[t % u].arrived(eng, t // u)
                            eng.indirect_dma_start(AGG[:, t, :], None, rows,
                                                   bass.IndirectOffsetOnAxis(ap=index[:, t:t + 1], axis=0)).then_inc(got[t % u].sem, 16)

                @block.vector
                def _(eng):
                    c = Count(eng, chain)
                    with c.loop(NT // u, LINKS[prepare] + 3) as i:
                        if gather is not None:
                            for k in range(u):
                                got[k].arrived(eng, i + 1)
                        prepare(c, ds(i * u, u))
                        eng.sem_inc(apart, 1)
                        for j in range(u):
                            last = eng.bn_stats(BS[:, j, :], X[:, ds(i * u + j, 1), :].rearrange("p o d -> p (o d)"))
                        c.link(last)
                        eng.sem_inc(apart, 1)
                        for j in range(u):
                            last = eng.bn_aggr(MV5[:, j, :], BS[:, j, :])
                        c.link(last)
                        c.link(eng.tensor_copy(MV[:, ds(i * u, u), :], MV5[:, :, :]))
                    c.link(eng.tensor_scalar(RST[:, :], MV[:, :, 1], EPS, None, ALU.add))
                    eng.sem_inc(aggregated, 1)
                    eng.wait_ge(rooted, 1)
                    c.link(eng.reciprocal(RST[:, :], RST[:, :]))
                    c.link(eng.tensor_tensor(NMR[:, :], MV[:, :, 0], RST[:, :], ALU.mult))
                    c.link(eng.tensor_scalar(NMR[:, :], NMR[:, :], -1.0, None, ALU.mult))
                    eng.sem_inc(scaled, 1)

                @block.scalar
                def _(eng):
                    eng.wait_ge(aggregated, 1)
                    eng.activation(RST[:, :], RST[:, :], ACT.Sqrt).then_inc(rooted, 1)
                    eng.wait_ge(scaled, 1)
                    with eng.Fori(0, NT // u) as i:
                        for j in range(u):
                            t = i * u + j
                            last = eng.activation(tile_of(X, t), tile_of(X, t), ACT.Identity,
                                                  bias=NMR[:, ds(t, 1)], scale=RST[:, ds(t, 1)])
                        last.then_inc(done, 1)

                if out_rows is not None:
                    @block.sync
                    def _(eng):
                        eng.wait_ge(done, NT // u)
                        eng.dma_start(out_rows[0:(NT - 1) * P, :].rearrange("(t p) d -> p t d", p=P), X[:, 0:NT - 1, :]).then_inc(stored, 16)
                        eng.dma_start(out_rows[(NT - 1) * P:N, :], X[0:LAST, NT - 1, :]).then_inc(stored, 16)
                        eng.wait_ge(stored, 32)
            if gather is not None:
                for g in got:
                    g.close(NODE_UNROLL)


        def last(c, at):
            wide = [P, NODE_UNROLL, D]
            c.link(c.eng.tensor_tensor(Y[:, at, :], Y[:, at, :], rstd_b[:, :].unsqueeze(1).broadcast_to(wide), ALU.mult))
            c.link(c.eng.tensor_tensor(Y[:, at, :], Y[:, at, :], BET[:, LAYERS - 1, :].unsqueeze(1).broadcast_to(wide), ALU.add))
            c.link(c.eng.scalar_tensor_tensor(X[:, at, :], Y[:, at, :], 0.0, X[:, at, :], ALU.max, ALU.add))

        LINKS = {last: 3}

        mean_b, rstd_b = carve(SBASE, ((D,), F32), ((D,), F32))

        def batch_norm(name, layer, gather):
            u = NODE_UNROLL
            with Stage(nc, name) as st:
                names = ("chain", "made", "summed", "squared", "dev", "var_ready")
                chain, made, summed, squared, dev, var_ready = (st.sem(n) for n in names)
                got = gathered[0:NT // u]
                ps = st.stack.enter_context(nc.psum_tensor(f"{name}_ps", [P, 2, 512], F32))
                block = st.block()

                @block.gpsimd
                def _(eng):
                    rows, index = gather
                    for t in range(NT):
                        got[t % u].arrived(eng, t // u)
                        eng.indirect_dma_start(AGG[:, t, :], None, rows,
                                               bass.IndirectOffsetOnAxis(ap=index[:, t:t + 1], axis=0)).then_inc(got[t % u].sem, 16)

                def column_sums(eng, dst, src, ready):
                    for t in range(NT):
                        if t % u == 0:
                            eng.wait_ge(ready, t // u + 1)
                        n = P if t < NT - 1 else LAST
                        last = eng.matmul(dst, ones[0:n, :], src[0:n, t, :], start=t == 0, stop=t == NT - 1)
                    last.then_inc(summed, 1)

                @block.tensor
                def _(eng):
                    column_sums(eng, ps[:, 0, 0:D], Y, made)
                    column_sums(eng, ps[:, 1, 0:D], AGG, squared)

                @block.scalar
                def _(eng):
                    for k in range(NT // u):
                        at = slice(k * u, (k + 1) * u)
                        eng.wait_ge(dev, k + 1)
                        eng.activation(AGG[:, at, :], Y[:, at, :], ACT.Square).then_inc(squared, 1)
                    eng.wait_ge(var_ready, 1)
                    eng.activation(rstd_b[:, :], rstd_b[:, :], ACT.Sqrt).then_inc(var_ready, 1)

                @block.vector
                def _(eng):
                    c = Count(eng, chain)
                    wide = [P, u, D]
                    for k in range(NT // u):
                        at = slice(k * u, (k + 1) * u)
                        for g in got:
                            g.arrived(eng, k + 1)
                        c.link(eng.tensor_tensor(AGG[:, at, :], C[:, at, 0:D], AGG[:, at, :], ALU.add))
                        eng.tensor_scalar(Y[:, at, :], AGG[:, at, :], 0.0, None, ALU.max).then_inc(made, 1)
                    eng.wait_ge(summed, 1)
                    c.link(eng.tensor_scalar(mean_b[:, :], ps[:, 0, 0:D], 1.0 / N, None, ALU.mult))
                    for k in range(NT // u):
                        at = slice(k * u, (k + 1) * u)
                        eng.tensor_tensor(Y[:, at, :], Y[:, at, :], mean_b[:, :].unsqueeze(1).broadcast_to(wide),
                                          ALU.subtract).then_inc(dev, 1)
                    eng.wait_ge(summed, 2)
                    c.link(eng.tensor_scalar(rstd_b[:, :], ps[:, 1, 0:D], 1.0 / N, EPS, ALU.mult, ALU.add))
                    eng.sem_inc(var_ready, 1)
                    eng.wait_ge(var_ready, 2)
                    c.link(eng.reciprocal(rstd_b[:, :], rstd_b[:, :]))
                    c.link(eng.tensor_tensor(rstd_b[:, :], rstd_b[:, :], GAM[:, layer, :], ALU.mult))

            for g in got:
                g.close(NODE_UNROLL)


        def stage_normed(layer):
            def stage(eng, t, slot, chain, staged):
                eng.tensor_tensor(TMP2[:, slot, :], tile_of(Y, t), rstd_b[:, :], ALU.mult).then_inc(chain, 1)
                eng.wait_ge(chain, t * 2 + 1)
                eng.tensor_tensor(TMP2[:, slot, :], TMP2[:, slot, :], BET[:, layer, :], ALU.add).then_inc(chain, 1)
                eng.wait_ge(chain, t * 2 + 2)
                eng.tensor_scalar(R[:, slot, :], TMP2[:, slot, :], 0.0, None, ALU.max).then_inc(staged, 1)
            return stage

        def copy_to(dst):
            def out1(eng, t, slot, ps):
                return eng.activation(tile_of(dst, t), ps, ACT.Copy)
            return out1

        def flow_l0():
            out1, out2 = gcn_table(0, False)
            node_products("n0", stage_copy(X), GW[:, 0], out1, None, out2, table=(AGG, T), marks=(first_src, flag_src))
            for l in range(LAYERS):
                edge_pass(f"e{l}", SRCI, (ALU.mult, ALU.add), nst_dst, True, rank_beside(l))
                if l < LAYERS - 1:
                    out1, out2 = gcn_table(l + 1, True)
                    node_products(f"n{l + 1}", stage_gcn(l), GW[:, l + 1], out1, MW[:, l], out2,
                                  gather=(PR, end_sum), table=(AGG, T))
                else:
                    def out1(eng, t, slot, ps):
                        return eng.activation(TMP[:, slot, :], ps, ACT.Copy)

                    def out2(eng, t, slot, ps, done):
                        eng.tensor_tensor(tile_of(X, t), TMP[:, slot, :], tile_of(X, t), ALU.add).then_inc(done, 1)
                    node_products("n3", stage_gcn(l), MW[:, l], out1, None, out2, gather=(PR, end_sum))

        def flow_l1():
            def out2(eng, t, slot, ps, done):
                eng.tensor_tensor(tile_of(C[:, :, 0:D], t), ps[:, D:2 * D], B1[:, :], ALU.add).then_inc(done, 1)
            def add_bias(eng, t):
                return eng.tensor_tensor(tile_of(X, t), tile_of(X, t), MB[:, :], ALU.add)
            node_products("n4", None, DF1, copy_to(AGG), TH1, out2, table=(AGG, T), norm=(add_bias,))
            edge_pass("e3", SRCI, (ALU.add, ALU.max), low_dst, False, order_beside)

        CHK = ET // 4
        MASK3 = dram("attention_masks", [ET * HEADS, 3 * P], BF16)
        last_key = dram("last_key", [1, ET])
        elbuf, erbuf, dstbuf, mask3, run_max, seg_max, er_seg = carve(
            YBASE, ((2, GT * HEADS), F32), ((SETS, GT * HEADS), F32), ((SETS, GT * P), F32), ((SETS, 3, P), BF16),
            ((P,), F32), ((2, P), F32), ((P,), F32))
        same, zed, lrelu, score, prob = carve(SBASE, ((2, GT, P), F32), *[((2, P), F32)] * 4)
        GH = GT * HEADS

        def attention_masks():
            wide = YBASE[0:CHK, 0:4 * HEADS * 3 * P // 2].bitcast(BF16).rearrange("p (c h k e) -> p c h k e", c=4, h=HEADS, k=3)
            rows = ARENA[0:CHK, 0:6 * P].bitcast(BF16)\
                .rearrange("p (k c e) -> p k c e", k=3, c=4)
            with Stage(nc, "am") as st:
                loaded, spread, stored = (st.sem(n) for n in ("loaded", "spread", "stored"))
                flags_in, flags_spread = (st.sem(n) for n in ("flags_in", "flags_spread"))
                flags, low = carve(ARENA[:, 6 * P:6 * P + 2 * ET], ((ET,), F32), ((ET,), BF16))
                block = st.block()

                @block.sync
                def _(eng):
                    eng.dma_start(flags, flag_src.rearrange("(p c) o -> p (c o)", p=P)).then_inc(flags_in, 16)
                    for k, (row, shift) in enumerate(((nst_dst, 0), (low_dst, 0), (low_dst, 1))):
                        eng.dma_start(rows[:, k], row[:, shift:shift + EP].rearrange("o (c p e) -> p (o c) e", c=4, e=P)).then_inc(loaded, 16)
                    eng.wait_ge(spread, 4)
                    for c in range(4):
                        eng.dma_start(MASK3[c * CHK * HEADS:(c + 1) * CHK * HEADS, :].rearrange("(p h) k -> p (h k)", h=HEADS),
                                      wide[:, c].rearrange("p h k e -> p (h k e)")).then_inc(stored, 16)
                    eng.wait_ge(flags_spread, 1)
                    eng.dma_start(low_src[:, 0:EP].rearrange("o (p c) -> (o p) c", p=P), low).then_inc(stored, 16)
                    eng.wait_ge(stored, 80)

                @block.vector
                def _(eng):
                    eng.wait_ge(loaded, 48)
                    for c in range(4):
                        for k in range(3):
                            last_ = eng.tensor_copy(wide[:, c, :, k, :], rows[:, k, c, :].unsqueeze(1).broadcast_to([CHK, HEADS, P]))
                        last_.then_inc(spread, 1)
                    eng.wait_ge(flags_in, 16)
                    eng.tensor_scalar(low, flags, LOW, None, ALU.mult).then_inc(flags_spread, 1)

        tile_key, tile_key_i, tile_er, z4 = (v[0:CHK] for v in carve(
            YBASE[:, YBASE.shape[1] - 224:YBASE.shape[1]], ((2, 4), F32), ((2, 4), I32), ((2, 4, HEADS), F32), ((4, 4, HEADS), F32)))

        def attention_er():
            with Stage(nc, "er") as st:
                loaded, cast, stored = (st.sem(n) for n in ("loaded", "cast", "stored"))
                got = gathered[0]
                block = st.block()

                @block.sync
                def _(eng):
                    with nc.allow_non_contiguous_dma("one element a tile"):
                        for s, e in ((0, 0), (1, P - 1)):
                            eng.dma_start(tile_key[:, s, :], dst_row.rearrange("o (c p e) -> p (o c) e", c=4, e=P)[:, :, e]).then_inc(loaded, 16)
                        eng.wait_ge(cast, 1)
                        eng.dma_start(last_key.rearrange("o (c p) -> p (o c)", c=4), tile_key[:, 1, :]).then_inc(stored, 16)
                    got.arrived(eng, 8)
                    eng.dma_start(ERE.rearrange("(c p e) h -> p c e h", c=4, e=P)[:, :, 0, :], tile_er[:, 0]).then_inc(stored, 16)
                    eng.wait_ge(stored, 32)

                @block.vector
                def _(eng):
                    eng.wait_ge(loaded, 32)
                    eng.tensor_copy(tile_key_i[:, :, :], tile_key[:, :, :]).then_inc(cast, 1)

                @block.gpsimd
                def _(eng):
                    eng.wait_ge(cast, 1)
                    for s in range(2):
                        for c in range(4):
                            eng.indirect_dma_start(tile_er[:, s, c, :], None, ERT,
                                                   bass.IndirectOffsetOnAxis(ap=tile_key_i[:, s, c:c + 1], axis=0)).then_inc(got.sem, 16)
            got.close(8)


        def attention_pass():
            SL = slice(0, GH)
            with Stage(nc, "att") as st:
                got = gathered
                ready = [st.sem(f"ready{q}") for q in range(SETS)]
                names = ("turned", "scored", "chain", "expd", "spread", "masked", "made", "moved", "o_free", "stored", "go_pool", "go_sp", "packed", "go_pe")
                turned, scored, chain, expd, spread, masked, made, moved, o_free, stored, go_pool, go_sp, packed, go_pe = (st.sem(n) for n in names)
                ta = st.stack.enter_context(nc.psum_tensor("att_a", [P, 2, 512], F32))
                tb = st.stack.enter_context(nc.psum_tensor("att_b", [P, 2, 512], F32))
                po = st.stack.enter_context(nc.psum_tensor("att_o", [P, GT, 512], F32))
                out_rows = PA[0:EP, :].rearrange("(t p) d -> p t d", p=P)
                er_rows = ERE.rearrange("(t p) h -> p t h", p=P)
                block = st.block()

                @block.sync
                def _(eng):
                    def prefetch(g, q):
                        eng.dma_start(idxbuf[:, q, :], SRCI[:, ds(g * GT, GT)]).then_inc(ready[q], 16)
                        eng.dma_start(dstbuf[:, q, :], dst_row[0:1, ds(g * (GT * P), GT * P)].broadcast_to([P, GT * P])).then_inc(ready[q], 16)
                        eng.dma_start(erbuf[:, q, :].rearrange("p (t h) -> p t h", h=HEADS), er_rows[:, ds(g * GT, GT), :]).then_inc(ready[q], 16)
                        eng.dma_start(mask3[SL, q].rearrange("p k e -> p (k e)"), MASK3[ds(g * GH, GH), :]).then_inc(ready[q], 16)

                    for q in range(SETS):
                        prefetch(q, q)

                    def store(g, q):
                        eng.wait_ge(moved, g * 4 + 12)
                        eng.sem_inc(go_sp, 1)
                        eng.dma_start(out_rows[:, ds(g * GT, GT), :], O[:, q % 2, :, :]).then_inc(stored, 16)
                        if not isinstance(g, int) or g + SETS < NG:
                            prefetch(g + SETS, q)
                        eng.wait_ge(stored, g * 16 + 16)
                        eng.sem_inc(o_free, 1)

                    with eng.Fori(0, (NG - SETS) // SETS) as i:
                        for q in range(SETS):
                            store(i * SETS + q, q)
                    for g in range((NG - SETS) // SETS * SETS, NG):
                        store(g, g % SETS)

                @block.gpsimd
                def _(eng):
                    def gather(g, q, turn):
                        eng.wait_ge(ready[q], turn * 64 + 64)
                        eng.sem_inc(go_pool, 1)
                        for k in range(GT):
                            eng.indirect_dma_start(G[:, q * GT + k, :], None, T2,
                                                   bass.IndirectOffsetOnAxis(ap=idxbuf[:, q, k:k + 1], axis=0)).then_inc(got[q].sem, 16)

                    pipelined(NG, SETS, eng, (gather, 0))

                @block.tensor
                def _(eng):
                    eng.sem_inc(made, 8)
                    eng.sem_inc(turned, 2)

                    def turn_el(g, q, turn):
                        eng.wait_ge(packed, g + 1)
                        eng.wait_ge(scored, g + 1)
                        eng.transpose(ta[SL, q % 2, 0:P], elbuf[:, q % 2, :], ident[:, :])
                        eng.transpose(ta[SL, q % 2, P:2 * P], erbuf[:, q, :], ident[:, :]).then_inc(turned, 1)

                    def turn_p(g, q, turn):
                        eng.wait_ge(expd, g + 1)
                        eng.wait_ge(masked, g + 1)
                        eng.wait_ge(moved, g * 4 + 4)
                        eng.sem_inc(go_pe, 1)
                        eng.transpose(tb[:, q % 2, 0:GH], prob[SL, q % 2, :], ident[SL, SL])
                        eng.transpose(tb[:, q % 2, GH:2 * GH], seg_max[SL, q % 2, :], ident[SL, SL]).then_inc(spread, 1)

                    def product(g, q, turn):
                        eng.wait_ge(masked, g + 3)
                        for k in range(GT):
                            eng.wait_ge(moved, g * 4 + (k + 5))
                            eng.matmul(po[:, k, 0:TW], same[:, q % 2, k, :], G[:, q * GT + k, :], start=True, stop=True).then_inc(made, 1)

                    pipelined(NG, SETS, eng, (turn_el, 2), (turn_p, 1), (product, 0))

                @block.vector
                def _(eng):
                    eng.sem_inc(scored, 2)
                    eng.sem_inc(masked, 2)

                    rev = slice(None, None, -1)

                    def scan_forth(g, q, turn):
                        eng.wait_ge(turned, g + 3)
                        eng.tensor_tensor_scan(run_max[SL, :], mask3[SL, q, 1, :], ta[SL, q % 2, 0:P], LOW, ALU.add, ALU.max).then_inc(chain, 1)
                        eng.tensor_tensor_scan(er_seg[SL, :], mask3[SL, q, 0, :], ta[SL, q % 2, P:2 * P], 0.0, ALU.mult, ALU.add).then_inc(chain, 1)

                    def scan_back(g, q, turn):
                        eng.wait_ge(chain, g * 6 + 2)
                        eng.tensor_tensor(zed[SL, 0, :], ta[SL, q % 2, 0:P], er_seg[SL, :], ALU.add).then_inc(chain, 1)
                        eng.wait_ge(spread, g + 1)
                        eng.tensor_tensor_scan(seg_max[SL, q % 2, rev], mask3[SL, q, 2, rev], run_max[SL, rev], LOW, ALU.add, ALU.max).then_inc(chain, 1)

                    def greatest(g, q, turn):
                        eng.wait_ge(chain, g * 6 + 4)
                        eng.tensor_tensor(zed[SL, 1, :], seg_max[SL, q % 2, :], er_seg[SL, :], ALU.add).then_inc(chain, 1)

                    def leaky(g, q, turn):
                        eng.wait_ge(chain, g * 6 + 5)
                        eng.scalar_tensor_tensor(lrelu[SL, :, :], zed[SL, :, :], 0.2, zed[SL, :, :], ALU.mult, ALU.max).then_inc(chain, 1)

                    def subtract(g, q, turn):
                        eng.wait_ge(chain, g * 6 + 6)
                        eng.tensor_tensor(score[SL, q % 2, :], lrelu[SL, 0, :], lrelu[SL, 1, :], ALU.subtract).then_inc(scored, 1)

                    def met(g, q, k):
                        return eng.scalar_tensor_tensor(same[:, q % 2, k, :], dstbuf[:, q, k * P:(k + 1) * P],
                                                        DSTF[:, ds(g * GT + k, 1)], upto[:, :], ALU.is_equal, ALU.mult)

                    def met_01(g, q, turn):
                        eng.wait_ge(made, g * 4 + 4)
                        met(g, q, 0)
                        met(g, q, 1)

                    def met_2(g, q, turn):
                        met(g, q, 2)

                    def met_3(g, q, turn):
                        met(g, q, 3)

                    def weigh(g, q, turn):
                        eng.wait_ge(spread, g + 3)
                        p = tb[:, q % 2, 0:GH].rearrange("p (t h) -> p t h", h=HEADS)
                        rows = G[:, q * GT:(q + 1) * GT, :]
                        eng.tensor_tensor(rows[:, :, 0:D].rearrange("p t (h c) -> p t h c", h=HEADS),
                                          rows[:, :, 0:D].rearrange("p t (h c) -> p t h c", h=HEADS),
                                          p.unsqueeze(3).broadcast_to([P, GT, HEADS, D // HEADS]), ALU.mult)
                        eng.tensor_copy(rows[:, :, D:TW], p).then_inc(masked, 1)

                    pipelined(NG, SETS, eng, (met_01, 0), (scan_forth, 1), (scan_back, 1), (met_2, 0), (greatest, 1),
                              (met_3, 0), (leaky, 1), (weigh, 0), (subtract, 1))

                @block.scalar
                def _(eng):
                    eng.sem_inc(moved, 8)
                    eng.sem_inc(o_free, 2)
                    eng.sem_inc(spread, 2)

                    def pack(g, q, turn):
                        got[q].arrived(eng, turn * GT + GT)
                        eng.wait_ge(turned, g + 1)
                        eng.activation(elbuf[:, q % 2, :].rearrange("p (t h) -> p t h", h=HEADS),
                                       G[:, q * GT:(q + 1) * GT, D:TW], ACT.Copy).then_inc(packed, 1)

                    def exp_step(g, q, turn):
                        eng.wait_ge(scored, g + 3)
                        eng.activation(prob[SL, q % 2, :], score[SL, q % 2, :], ACT.Exp).then_inc(expd, 1)

                    def move(g, q, turn):
                        eng.wait_ge(o_free, g + 1)
                        for k in range(GT):
                            eng.wait_ge(made, g * 4 + (k + 9))
                            if k == 0:
                                eng.activation(O[:, q % 2, :, TW:RW], tb[:, q % 2, GH:2 * GH].rearrange("p (t h) -> p t h", h=HEADS), ACT.Copy)
                            eng.activation(O[:, q % 2, k, 0:TW], po[:, k, 0:TW], ACT.Copy).then_inc(moved, 1)

                    pipelined(NG, SETS, eng, (pack, 2), (exp_step, 1), (move, 0))
            for q in range(SETS):
                got[q].close(GT * ((NG - q + SETS - 1) // SETS))


        def attention_carry():
            rows, key_all, same_t, prod_t, s8, res = carve(
                YBASE, ((4, RW), F32), ((ET,), F32), ((10, CHK), F32), ((2, 4, HEADS), F32), ((3, ET + 2), F32), ((4, RW), F32))
            H8 = slice(0, HEADS)
            CS = slice(0, CHK)
            rev = slice(None, None, -1)
            pairs = [(a_, c_) for c_ in range(4) for a_ in range(c_ + 1)]
            with Stage(nc, "car") as st:
                names = ("loaded", "chain", "turned", "back", "expd", "weighted", "made", "moved", "stored", "maxed", "scored")
                loaded, chain, turned, back, expd, weighted, made, moved, stored, maxed, scored = (st.sem(n) for n in names)
                t8 = st.stack.enter_context(nc.psum_tensor("car_8", [P, 512], F32))
                tk = st.stack.enter_context(nc.psum_tensor("car_k", [P, 512], F32))
                po = st.stack.enter_context(nc.psum_tensor("car_o", [P, 4, 512], F32))
                block = st.block()

                @block.sync
                def _(eng):
                    eng.dma_start(rows[CS], PA[0:EP, :].rearrange("(c p e) d -> p c e d", c=4, e=P)[:, :, P - 1, :]).then_inc(loaded, 16)
                    eng.dma_start(key_all[CS, :], last_key.broadcast_to([CHK, ET])).then_inc(loaded, 16)
                    eng.wait_ge(moved, 5)
                    eng.dma_start(CR[0:ET, :].rearrange("(c p) d -> p c d", c=4), res[CS]).then_inc(stored, 16)
                    eng.wait_ge(stored, 16)

                @block.tensor
                def _(eng):
                    eng.wait_ge(loaded, 32)
                    for c in range(4):
                        last_ = eng.transpose(t8[H8, c * CHK:(c + 1) * CHK], rows[CS, c, TW:RW], ident[CS, CS])
                    last_.then_inc(turned, 1)
                    eng.wait_ge(maxed, 1)
                    for c in range(4):
                        last_ = eng.transpose(tk[CS, c * HEADS:(c + 1) * HEADS], s8[H8, 2, c * CHK:(c + 1) * CHK], ident[H8, H8])
                    last_.then_inc(back, 1)
                    eng.wait_ge(weighted, 1)
                    for n, (a_, c_) in enumerate(pairs):
                        last_ = eng.matmul(po[CS, c_, 0:TW], same_t[CS, n, :], rows[CS, a_, 0:TW], start=a_ == 0, stop=a_ == c_)
                    last_.then_inc(made, 1)

                @block.scalar
                def _(eng):
                    eng.wait_ge(scored, 1)
                    eng.activation(prod_t[CS, 0], z4[:, 2], ACT.Exp).then_inc(expd, 1)
                    eng.wait_ge(made, 1)
                    for c in range(4):
                        eng.activation(res[CS, c, 0:TW], po[CS, c, 0:TW], ACT.Copy).then_inc(moved, 1)

                @block.vector
                def _(eng):
                    c = Count(eng, chain)
                    eng.wait_ge(loaded, 32)
                    c.link(eng.tensor_tensor(s8[H8, 0, 1:ET], key_all[H8, 1:ET], key_all[H8, 0:ET - 1], ALU.not_equal))
                    c.link(eng.tensor_scalar(s8[H8, 0, 1:ET], s8[H8, 0, 1:ET], LOW, None, ALU.mult))
                    c.inc(eng.memset(s8[H8, 0, 0:1], LOW))
                    c.inc(eng.memset(s8[H8, 0, ET:ET + 2], LOW))
                    for n, (a_, c_) in enumerate(pairs):
                        there = key_all[CS, c_ * CHK:(c_ + 1) * CHK]
                        c.inc(eng.scalar_tensor_tensor(same_t[CS, n, :], there, tile_key[:, 1, a_:a_ + 1],
                                                       upto[CS, CS] if a_ == c_ else ones[CS, CS], ALU.is_equal, ALU.mult))
                    c.wait()
                    eng.wait_ge(turned, 1)
                    c.link(eng.tensor_tensor_scan(s8[H8, 1, 0:ET], s8[H8, 0, 0:ET], t8[H8, 0:ET], LOW, ALU.add, ALU.max))
                    c.link(eng.tensor_tensor_scan(s8[H8, 2, 0:ET][:, rev],
                                                  s8[H8, 0, 1:ET + 1][:, rev], s8[H8, 1, 0:ET][:, rev], LOW, ALU.add, ALU.max))
                    eng.sem_inc(maxed, 1)
                    eng.wait_ge(back, 1)
                    mk = tk[CS, 0:4 * HEADS].rearrange("p (c h) -> p c h", h=HEADS)
                    eng.tensor_copy(res[CS, :, TW:RW], mk).then_inc(moved, 1)
                    er = tile_er[:, 1]
                    c.inc(eng.tensor_tensor(z4[:, 0], rows[CS, :, TW:RW], er, ALU.add))
                    c.link(eng.tensor_tensor(z4[:, 1], mk, er, ALU.add))
                    c.link(eng.scalar_tensor_tensor(z4[:, 2:4], z4[:, 0:2], 0.2, z4[:, 0:2], ALU.mult, ALU.max))
                    c.link(eng.tensor_tensor(z4[:, 2], z4[:, 2], z4[:, 3], ALU.subtract))
                    eng.sem_inc(scored, 1)
                    eng.wait_ge(expd, 1)
                    w = prod_t[CS, 0]
                    c.inc(eng.tensor_tensor(rows[CS, :, 0:D].rearrange("p c (h d) -> p c h d", h=HEADS),
                                            rows[CS, :, 0:D].rearrange("p c (h d) -> p c h d", h=HEADS),
                                            w.unsqueeze(3).broadcast_to([CHK, 4, HEADS, D // HEADS]), ALU.mult))
                    c.inc(eng.tensor_tensor(rows[CS, :, D:TW], rows[CS, :, D:TW], w, ALU.mult))
                    c.wait()
                    eng.sem_inc(weighted, 1)

        def attention_combine():
            u = NODE_UNROLL
            with Stage(nc, "comb") as st:
                chain, expd, scored = (st.sem(n) for n in ("chain", "expd", "scored"))
                m4, z_, l_, e_, den = carve(WORK, ((4, NT, HEADS), F32), ((4, NT, HEADS), F32), ((4, NT, HEADS), F32),
                                            ((4, NT, HEADS), F32), ((2, NT, HEADS), F32))
                block = st.block()

                @block.gpsimd
                def _(eng):
                    for t in range(NT):
                        got = gathered[t // u]
                        eng.indirect_dma_start(YW[:, t, :], None, PA, bass.IndirectOffsetOnAxis(ap=end_sum[:, t:t + 1], axis=0)).then_inc(got.sem, 16)
                        eng.indirect_dma_start(AGW[:, t, :], None, CR, bass.IndirectOffsetOnAxis(ap=carry_row[:, t:t + 1], axis=0)).then_inc(got.sem, 16)

                @block.scalar
                def _(eng):
                    for k in range(NT // u):
                        T = slice(k * u, k * u + u)
                        eng.wait_ge(scored, k + 1)
                        eng.activation(e_[:, 0:3, T], z_[:, 0:3, T], ACT.Exp).then_inc(expd, 1)

                @block.vector
                def _(eng):
                    c = Count(eng, chain)

                    def scores(k):
                        T = slice(k * u, k * u + u)
                        er = C[:, T, TW:RW]
                        gathered[k].arrived(eng, 2 * u)
                        c.inc(eng.tensor_copy(m4[:, 0, T], YW[:, T, TW:RW]))
                        c.inc(eng.tensor_copy(m4[:, 1, T], AGW[:, T, TW:RW]))
                        c.link(eng.tensor_copy(m4[:, 2, T], C[:, T, D:TW]))
                        c.link(eng.tensor_tensor(m4[:, 3, T], m4[:, 0, T], m4[:, 1, T], ALU.max))
                        c.link(eng.tensor_tensor(m4[:, 3, T], m4[:, 3, T], m4[:, 2, T], ALU.max))
                        for n in range(4):
                            c.inc(eng.tensor_tensor(z_[:, n, T], m4[:, n, T], er, ALU.add))
                        c.wait()
                        c.link(eng.scalar_tensor_tensor(l_[:, :, T], z_[:, :, T], 0.2, z_[:, :, T], ALU.mult, ALU.max))
                        for n in range(3):
                            c.inc(eng.tensor_tensor(z_[:, n, T], l_[:, n, T], l_[:, 3, T], ALU.subtract))
                        c.wait()
                        eng.sem_inc(scored, 1)

                    def weigh(k):
                        T = slice(k * u, k * u + u)
                        eng.wait_ge(expd, k + 1)
                        c.inc(eng.tensor_tensor(l_[:, 0, T], e_[:, 0, T], YW[:, T, D:TW], ALU.mult))
                        c.link(eng.tensor_tensor(l_[:, 1, T], e_[:, 1, T], AGW[:, T, D:TW], ALU.mult))
                        c.link(eng.tensor_tensor(den[:, 0, T], l_[:, 0, T], l_[:, 1, T], ALU.add))
                        c.link(eng.tensor_tensor(den[:, 0, T], den[:, 0, T], e_[:, 2, T], ALU.add))
                        c.link(eng.tensor_scalar(den[:, 0, T], den[:, 0, T], 1e-16, None, ALU.add))
                        c.link(eng.reciprocal(den[:, 1, T], den[:, 0, T]))
                        for n in range(3):
                            c.inc(eng.tensor_tensor(e_[:, n, T], e_[:, n, T], den[:, 1, T], ALU.mult))
                        c.wait()
                        parts = (YW, AGW, C)
                        for n, part in enumerate(parts):
                            v = part[:, T, 0:D].rearrange("p t (h d) -> p t h d", h=HEADS)
                            c.inc(eng.tensor_tensor(v, v, e_[:, n, T].unsqueeze(3).broadcast_to([P, u, HEADS, D // HEADS]), ALU.mult))
                        for part in parts:
                            c.wait()
                            c.inc(eng.tensor_tensor(X[:, T, :], X[:, T, :], part[:, T, 0:D], ALU.add))

                    for k in range(NT // u):
                        scores(k)
                        weigh(k)
            for k in range(NT // u):
                gathered[k].close(2 * u)

        def flow_l2():
            def out2(eng, t, slot, ps, done):
                eng.tensor_copy(tile_of(C[:, :, D:RW], t), ps[:, D:D + 2 * HEADS]).then_inc(done, 1)

            def own_term(eng, t):
                return eng.tensor_tensor(tile_of(AGG, t), tile_of(C[:, :, 0:D], t), tile_of(AGG, t), ALU.add)

            def positive(eng, t):
                return eng.scalar_tensor_tensor(tile_of(X, t), tile_of(AGG, t), 0.0, tile_of(X, t), ALU.max, ALU.add)
            node_products("n5", None, W2, copy_to(C[:, :, 0:D]), WA, out2, table=(C[:, :, 0:TW], T2), table2=(C[:, :, TW:RW], ERT),
                          scatter=(C[:, :, TW:RW], ERE, first_dst), gather=(PR, end_max), norm=(own_term, positive))
            attention_er()
            attention_pass()
            attention_carry()
            attention_combine()

        def flow_l3():
            for l in range(LAYERS):
                def out2(eng, t, slot, ps, done):
                    eng.tensor_copy(tile_of(C[:, :, 0:D], t), ps[:, D:2 * D]).then_inc(done, 1)
                node_products(f"n{6 + l}", None if l == 0 else stage_normed(l - 1), TH3[:, l], copy_to(AGG),
                              DF3[:, l], out2, table=(AGG, T), norm=() if l == 0 else None)
                edge_pass(f"e{5 + l}", BYSRC, (ALU.add, ALU.max), low_src, False)
                batch_norm(f"bn{l}", l, gather=(PR, end_src))
            layer_norm("ln3", last, out_rows=out)

        constants()
        edge_columns()
        load_weights, turn_weights = weights_beside()
        histogram(0, DSTF, load_weights)
        histogram(1, SRCF, both_beside(turn_weights, dst_nodes_beside))
        src_nodes()
        flow_l0()
        flow_l1()
        attention_masks()
        flow_l2()
        flow_l3()


INPUTS = ["x", "src", "dst", "edge_weight",
          "L0_gnn_fc_w", "L0_gnn_fc_b", "L0_gnn_ch_w", "L0_gnn_ch_b", "L0_gnn_mlp_w", "L0_gnn_mlp_b",
          "L1_gnn_theta_w", "L1_gnn_theta_b", "L1_gnn_phi_w", "L1_gnn_phi_b",
          "L2_gnn_W", "L2_gnn_a_left", "L2_gnn_a_right",
          "L3_gnn_thetas", "L3_gnn_phis", "L3_gnn_gammas", "L3_gnn_betas"]


def kernel(**inputs):
    import numpy as np
    import concourse.bacc as bacc
    from concourse.bass_utils import run_bass_kernel_spmd

    nc = bacc.Bacc("TRN2", target_bir_lowering=False, num_devices=1)
    arrays, a = {}, {}
    for name in INPUTS:
        v = np.ascontiguousarray(inputs[name])
        arrays[f"in_{name}"] = v
        a[name] = nc.dram_tensor(f"in_{name}", v.shape, mybir.dt.from_np(v.dtype), kind="ExternalInput").ap()
    out = nc.dram_tensor("out_0", (N, D), F32, kind="ExternalOutput").ap()
    build(nc, a, out)
    r = run_bass_kernel_spmd(nc, [arrays], core_ids=[0])
    return r.results[0]["out_0"]
```
